# Optimizing a Trainium2 kernel written in Bass

```python
import numpy as np
import jax
import jax.numpy as jnp

def _softmax(x, axis=-1):
    return jax.nn.softmax(x, axis=axis)

def _gelu(x):
    return jax.nn.gelu(x, approximate=True)

def _silu(x):
    return jax.nn.silu(x)

def _sigmoid(x):
    return jax.nn.sigmoid(x)

def _layernorm(x, axis=-1, eps=1e-05):
    m = jnp.mean(x, axis=axis, keepdims=True)
    v = jnp.var(x, axis=axis, keepdims=True)
    return (x - m) / jnp.sqrt(v + eps)

def _scatter_add(tgt, idx, src, axis=0):
    return tgt.at[idx].add(src)

def _segment_sum(src, seg, n):
    return jax.ops.segment_sum(src, seg, n)
kernel_name = 'mk_early_fusion_d1_tok_img768_r4_4321bd'

def setup_inputs(seed: int=0):
    np.random.seed(seed)
    _w = jnp.asarray

    def _rec_inputs():
        import jax
        import jax.numpy as jnp
        _rk = jax.random.key(seed)
        x = -0.00100294 + 1.00044 * jax.random.normal(jax.random.fold_in(_rk, 1), (4, 3, 64, 64), jnp.float32)
        txt = 1.6064e-06 + 0.02 * jax.random.normal(jax.random.fold_in(_rk, 2), (4, 128, 192), jnp.float32)
        return (x, txt)
    x, txt = _rec_inputs()

    def _L0_tok_setup():
        import jax, jax.numpy as jnp
        import numpy as np
        IMAGE_SIZE = 64
        PATCH = 4
        EMBED = 192
        KDIM = 96
        VDIM = 96
        QDIM = 96
        IN_CH = 3
        BATCH = 8
        key = jax.random.key(seed)
        ks = jax.random.split(key, 10)
        s = 0.02
        x = jax.random.normal(ks[0], (BATCH, IN_CH, IMAGE_SIZE, IMAGE_SIZE), dtype=jnp.float32)
        conv_w = jax.random.normal(ks[1], (EMBED, IN_CH, PATCH, PATCH), dtype=jnp.float32) * s
        conv_b = jnp.zeros((EMBED,), dtype=jnp.float32)
        k_w = jax.random.normal(ks[2], (KDIM, EMBED), dtype=jnp.float32) * s
        k_b = jnp.zeros((KDIM,), dtype=jnp.float32)
        v_w = jax.random.normal(ks[3], (VDIM, EMBED), dtype=jnp.float32) * s
        v_b = jnp.zeros((VDIM,), dtype=jnp.float32)
        q_w = jax.random.normal(ks[4], (QDIM, EMBED), dtype=jnp.float32) * s
        q_b = jnp.zeros((QDIM,), dtype=jnp.float32)
        proj_w = jax.random.normal(ks[5], (EMBED, VDIM), dtype=jnp.float32) * s
        proj_b = jnp.zeros((EMBED,), dtype=jnp.float32)
        return {'x': x, 'conv_w': conv_w, 'conv_b': conv_b, 'k_w': k_w, 'k_b': k_b, 'v_w': v_w, 'v_b': v_b, 'q_w': q_w, 'q_b': q_b, 'proj_w': proj_w, 'proj_b': proj_b}
    _L0_tok_all = _L0_tok_setup()
    _L0_tok_in = {k: v for k, v in _L0_tok_all.items() if k in ('conv_w', 'conv_b', 'k_w', 'k_b', 'v_w', 'v_b', 'q_w', 'q_b', 'proj_w', 'proj_b')}
    del _L0_tok_all

    def _L0_attn_setup():
        import jax, jax.numpy as jnp
        import numpy as np
        import math
        H = 12

        def _ln(x, w, b, eps=1e-05):
            mu = x.mean(-1, keepdims=True)
            var = ((x - mu) ** 2).mean(-1, keepdims=True)
            return (x - mu) / jnp.sqrt(var + eps) * w + b

        def _reference_tuple_inner(x, Wqkv, bqkv, Wb1, Wb2, temperature, Wproj, bproj, ln_w, ln_b, mn_w, mn_b):
            B, L, D = x.shape
            d = D // H
            x_norm = _ln(x, ln_w, ln_b)
            qkv = x_norm @ Wqkv + bqkv
            q, k, v = jnp.split(qkv, 3, axis=-1)
            params = (jax.nn.silu(x @ Wb1) @ Wb2).reshape(B, L, H, 5)
            sem_amp = jax.nn.sigmoid(params[..., 0])
            sem_phase = jnp.tanh(params[..., 1]) * math.pi
            ctx_amp = jax.nn.sigmoid(params[..., 2])
            ctx_phase = jnp.tanh(params[..., 3]) * math.pi
            temp = jnp.clip(temperature, 0.1, 2.0)
            interference = jnp.tanh(sem_amp * ctx_amp * jnp.cos(sem_phase - ctx_phase)) * temp
            gate = jax.nn.sigmoid(interference)
            q_f = (jax.nn.elu(q) + 1.0).reshape(B, L, H, d)
            k_f = (jax.nn.elu(k) + 1.0).reshape(B, L, H, d)
            v_f = v.reshape(B, L, H, d)
            kv_gated = jnp.einsum('blhd,blhe->blhde', k_f, v_f) * (1.0 + gate)[..., None, None]
            kv_states = jnp.cumsum(kv_gated, axis=1)
            z_states = jnp.cumsum(k_f, axis=1)
            out_num = jnp.einsum('blhd,blhde->blhe', q_f, kv_states)
            den = jnp.sum(q_f * z_states, axis=-1, keepdims=True) + 1e-06
            out = _ln(out_num / den, mn_w, mn_b)
            attn_out = out.reshape(B, L, D)
            return (attn_out @ Wproj + bproj, gate)
        key = jax.random.key(seed)
        B, L, D, R = (2, 256, 192, 128)
        d_head = D // H
        ks = jax.random.split(key, 6)
        s = 0.02
        return {'x': jax.random.normal(ks[0], (B, L, D), jnp.float32), 'Wqkv': jax.random.normal(ks[1], (D, 3 * D), jnp.float32) * s, 'bqkv': jnp.zeros((3 * D,), jnp.float32), 'Wb1': jax.random.normal(ks[2], (D, R), jnp.float32) * s, 'Wb2': jax.random.normal(ks[3], (R, H * 5), jnp.float32) * s, 'temperature': jnp.ones((1,), jnp.float32) * 0.5, 'Wproj': jax.random.normal(ks[4], (D, D), jnp.float32) * s, 'bproj': jnp.zeros((D,), jnp.float32), 'ln_w': jnp.ones((D,), jnp.float32), 'ln_b': jnp.zeros((D,), jnp.float32), 'mn_w': jnp.ones((d_head,), jnp.float32), 'mn_b': jnp.zeros((d_head,), jnp.float32)}
    _L0_attn_all = _L0_attn_setup()
    _L0_attn_in = {k: v for k, v in _L0_attn_all.items() if k in ('Wqkv', 'bqkv', 'Wb1', 'Wb2', 'temperature', 'Wproj', 'bproj', 'ln_w', 'ln_b', 'mn_w', 'mn_b')}
    del _L0_attn_all

    def _L0_ffn_setup():
        import jax, jax.numpy as jnp
        import numpy as np
        DECAY = 0.9
        EPS = 0.01
        TOP_K = 2
        key = jax.random.key(seed)
        k1, k2, k3, k4 = jax.random.split(key, 4)
        B, S, H, I, E = (4, 512, 192, 512, 8)
        return {'hidden_states': jax.random.normal(k1, (B, S, H), jnp.float32), 'router_w': jax.random.normal(k2, (E, H), jnp.float32) * 0.02, 'w1': jax.random.normal(k3, (E, I, H), jnp.float32) * 0.02, 'w2': jax.random.normal(k4, (E, H, I), jnp.float32) * 0.02}
    _L0_ffn_all = _L0_ffn_setup()
    _L0_ffn_in = {k: v for k, v in _L0_ffn_all.items() if k in ('router_w', 'w1', 'w2')}
    del _L0_ffn_all
    return {'x': x, 'txt': txt, 'L0_tok_conv_w': _L0_tok_in['conv_w'], 'L0_tok_conv_b': _L0_tok_in['conv_b'], 'L0_tok_k_w': _L0_tok_in['k_w'], 'L0_tok_k_b': _L0_tok_in['k_b'], 'L0_tok_v_w': _L0_tok_in['v_w'], 'L0_tok_v_b': _L0_tok_in['v_b'], 'L0_tok_q_w': _L0_tok_in['q_w'], 'L0_tok_q_b': _L0_tok_in['q_b'], 'L0_tok_proj_w': _L0_tok_in['proj_w'], 'L0_tok_proj_b': _L0_tok_in['proj_b'], 'L0_attn_Wqkv': _L0_attn_in['Wqkv'], 'L0_attn_bqkv': _L0_attn_in['bqkv'], 'L0_attn_Wb1': _L0_attn_in['Wb1'], 'L0_attn_Wb2': _L0_attn_in['Wb2'], 'L0_attn_temperature': _L0_attn_in['temperature'], 'L0_attn_Wproj': _L0_attn_in['Wproj'], 'L0_attn_bproj': _L0_attn_in['bproj'], 'L0_attn_ln_w': _L0_attn_in['ln_w'], 'L0_attn_ln_b': _L0_attn_in['ln_b'], 'L0_attn_mn_w': _L0_attn_in['mn_w'], 'L0_attn_mn_b': _L0_attn_in['mn_b'], 'L0_ffn_router_w': _L0_ffn_in['router_w'], 'L0_ffn_w1': _L0_ffn_in['w1'], 'L0_ffn_w2': _L0_ffn_in['w2']}

def reference(x, txt, L0_tok_conv_w, L0_tok_conv_b, L0_tok_k_w, L0_tok_k_b, L0_tok_v_w, L0_tok_v_b, L0_tok_q_w, L0_tok_q_b, L0_tok_proj_w, L0_tok_proj_b, L0_attn_Wqkv, L0_attn_bqkv, L0_attn_Wb1, L0_attn_Wb2, L0_attn_temperature, L0_attn_Wproj, L0_attn_bproj, L0_attn_ln_w, L0_attn_ln_b, L0_attn_mn_w, L0_attn_mn_b, L0_ffn_router_w, L0_ffn_w1, L0_ffn_w2):
    import jax
    import jax.numpy as jnp

    def _L0_tok_ref(x, conv_w, conv_b, k_w, k_b, v_w, v_b, q_w, q_b, proj_w, proj_b):
        import jax, jax.numpy as jnp
        import numpy as np
        IMAGE_SIZE = 64
        PATCH = 4
        EMBED = 192
        KDIM = 96
        VDIM = 96
        QDIM = 96
        IN_CH = 3
        BATCH = 8
        h = jax.lax.conv_general_dilated(x, conv_w, window_strides=(PATCH, PATCH), padding='VALID', dimension_numbers=('NCHW', 'OIHW', 'NCHW'))
        h = h + conv_b[None, :, None, None]
        b, e, gh, gw = h.shape
        tokens = h.reshape(b, e, gh * gw).transpose(0, 2, 1)
        k = tokens @ k_w.T + k_b
        v = tokens @ v_w.T + v_b
        q = tokens @ q_w.T + q_b
        scores = jnp.einsum('bnd,bmd->bnm', q, k) / jnp.sqrt(jnp.float32(KDIM))
        attn = jax.nn.softmax(scores, axis=2)
        out = jnp.einsum('bnm,bmd->bnd', attn, v)
        out = out @ proj_w.T + proj_b
        return out

    def _L0_attn_ref(x, Wqkv, bqkv, Wb1, Wb2, temperature, Wproj, bproj, ln_w, ln_b, mn_w, mn_b):
        import jax, jax.numpy as jnp
        import numpy as np
        import math
        H = 12

        def _ln(x, w, b, eps=1e-05):
            mu = x.mean(-1, keepdims=True)
            var = ((x - mu) ** 2).mean(-1, keepdims=True)
            return (x - mu) / jnp.sqrt(var + eps) * w + b

        def _reference_tuple_inner(x, Wqkv, bqkv, Wb1, Wb2, temperature, Wproj, bproj, ln_w, ln_b, mn_w, mn_b):
            B, L, D = x.shape
            d = D // H
            x_norm = _ln(x, ln_w, ln_b)
            qkv = x_norm @ Wqkv + bqkv
            q, k, v = jnp.split(qkv, 3, axis=-1)
            params = (jax.nn.silu(x @ Wb1) @ Wb2).reshape(B, L, H, 5)
            sem_amp = jax.nn.sigmoid(params[..., 0])
            sem_phase = jnp.tanh(params[..., 1]) * math.pi
            ctx_amp = jax.nn.sigmoid(params[..., 2])
            ctx_phase = jnp.tanh(params[..., 3]) * math.pi
            temp = jnp.clip(temperature, 0.1, 2.0)
            interference = jnp.tanh(sem_amp * ctx_amp * jnp.cos(sem_phase - ctx_phase)) * temp
            gate = jax.nn.sigmoid(interference)
            q_f = (jax.nn.elu(q) + 1.0).reshape(B, L, H, d)
            k_f = (jax.nn.elu(k) + 1.0).reshape(B, L, H, d)
            v_f = v.reshape(B, L, H, d)
            kv_gated = jnp.einsum('blhd,blhe->blhde', k_f, v_f) * (1.0 + gate)[..., None, None]
            kv_states = jnp.cumsum(kv_gated, axis=1)
            z_states = jnp.cumsum(k_f, axis=1)
            out_num = jnp.einsum('blhd,blhde->blhe', q_f, kv_states)
            den = jnp.sum(q_f * z_states, axis=-1, keepdims=True) + 1e-06
            out = _ln(out_num / den, mn_w, mn_b)
            attn_out = out.reshape(B, L, D)
            return (attn_out @ Wproj + bproj, gate)
        return _reference_tuple_inner(x, Wqkv, bqkv, Wb1, Wb2, temperature, Wproj, bproj, ln_w, ln_b, mn_w, mn_b)[0]

    def _L0_ffn_ref(hidden_states, router_w, w1, w2):
        import jax, jax.numpy as jnp
        import numpy as np
        DECAY = 0.9
        EPS = 0.01
        TOP_K = 2
        B, S, H = hidden_states.shape
        E = router_w.shape[0]
        flat = hidden_states.reshape(B * S, H)
        logits = flat @ router_w.T
        probs = jax.nn.softmax(logits, axis=-1)
        topk_probs, topk_idx = jax.lax.top_k(probs, TOP_K)
        importance = jax.lax.stop_gradient(probs).sum(axis=0)
        running = jnp.ones((E,), dtype=flat.dtype)
        blended = running + (1.0 - DECAY) * (importance - running)
        running = blended + EPS
        balance = running[topk_idx]
        balanced = topk_probs / balance
        balanced = balanced / balanced.sum(axis=-1, keepdims=True)
        h = jnp.einsum('th,eih->tei', flat, w1)
        h = jax.nn.silu(h)
        outs = jnp.einsum('tei,ehi->teh', h, w2)
        sel = jnp.take_along_axis(outs, topk_idx[:, :, None], axis=1)
        combined = (sel * balanced[..., None]).sum(axis=1)
        return combined.reshape(B, S, H)
    h = _L0_tok_ref(x, L0_tok_conv_w, L0_tok_conv_b, L0_tok_k_w, L0_tok_k_b, L0_tok_v_w, L0_tok_v_b, L0_tok_q_w, L0_tok_q_b, L0_tok_proj_w, L0_tok_proj_b)
    h = jnp.concatenate([h, txt], axis=1)
    h = h + _L0_attn_ref(_layernorm(h, axis=-1), L0_attn_Wqkv, L0_attn_bqkv, L0_attn_Wb1, L0_attn_Wb2, L0_attn_temperature, L0_attn_Wproj, L0_attn_bproj, L0_attn_ln_w, L0_attn_ln_b, L0_attn_mn_w, L0_attn_mn_b)
    h = h + _L0_ffn_ref(_layernorm(h, axis=-1), L0_ffn_router_w, L0_ffn_w1, L0_ffn_w2)
    return h

_drawn_inputs = setup_inputs


def setup_inputs(seed=0):
    import zlib

    import numpy as np

    out = dict(_drawn_inputs(seed))
    spreads = {'L0_tok_conv_b': (0.0, 0.1),
     'L0_tok_k_b': (0.0, 0.8),
     'L0_tok_v_b': (0.0, 0.1),
     'L0_tok_q_b': (0.0, 0.8),
     'L0_tok_proj_b': (0.0, 0.1),
     'L0_attn_bqkv': (0.0, 0.1),
     'L0_attn_bproj': (0.0, 0.1),
     'L0_attn_ln_w': (1.0, 0.2),
     'L0_attn_ln_b': (0.0, 0.1),
     'L0_attn_mn_w': (1.0, 0.2),
     'L0_attn_mn_b': (0.0, 0.1)}
    factors = {'x': 8.0,
     'L0_tok_conv_w': 8.0,
     'L0_tok_k_w': 8.0,
     'L0_tok_q_w': 8.0,
     'L0_attn_Wb1': 8.0,
     'L0_attn_Wb2': 8.0}
    for name, (base, spread) in spreads.items():
        noise = np.random.default_rng([zlib.crc32(name.encode()), seed]).standard_normal(out[name].shape)
        drawn = base * np.exp(spread * noise) if base else spread * noise
        out[name] = jnp.asarray(drawn.astype(out[name].dtype))
    for name, factor in factors.items():
        out[name] = (out[name] * factor).astype(out[name].dtype)
    return out
```

```python
from contextlib import ExitStack

import concourse.bass as bass
from concourse import mybir

ALU = mybir.AluOpType
ACT = mybir.ActivationFunctionType
F32 = mybir.dt.float32
F16 = mybir.dt.float16
I32 = mybir.dt.int32
U32 = mybir.dt.uint32
AX_X = mybir.AxisListType.X

P = 128
B = 4
NI = 256
D = 192
DC = D // 2
KD = 96
NP1 = 3 * 4 * 4 + 1
CT = 3
T = B * CT
IT = NI // P
H = 12
DH = D // H
SLOT = 32
HG = P // SLOT
G = H // HG
VE = DH + 1
R = 128
E = 8
FI = 512
MC = FI // P
NS = T * 2 + E - 1
NSP = NS + 1
LEAD = 7
assert (NS - LEAD) % 4 == 0
NTOK = T * P
WS = 256.0
STG = 2048
EPS = 1e-5
PI = 3.141592653589793
RSQRT_MAGIC = float(0x5F3759DF)
NO_TOKEN = 100000.0

def build(nc, A, x2_dram, y_dram, out):
    with ExitStack() as ctx:
        def sb(name, shape, dt=F32):
            return ctx.enter_context(nc.sbuf_tensor(name, shape, dt))

        def sem(name):
            return ctx.enter_context(nc.semaphore(name))

        bank = [ctx.enter_context(nc.psum_tensor(f"bank{i}", [P, 512], F32)) for i in range(8)]

        ident = sb("ident", [P, P])
        ident16 = sb("ident16", [P, P], F16)
        causal = sb("causal", [P, P])
        before = sb("before", [P, P])
        ones = sb("ones", [P, P])
        headmask = sb("headmask", [P, G, HG, VE])
        qkT = sb("qkT", [P, 2, 2 * G * P])
        qT, kT = (qkT[:, i, :].rearrange("p (b n) -> p b n", b=2) for i in range(2))
        xp1 = qkT[:].rearrange("p a n -> p (a n)")[0:NP1, 0:B * NI]
        early = sb("early", [P, 2 * STG])
        stage = early[:].rearrange("p (b n) -> p b n", b=2)
        atm = sb("atm", [P, HG, G, P])
        cwb = sb("cwb", [DC, 2, NP1])
        wtok = sb("wtok", [DC, 2, 3 * KD])
        btok = sb("btok", [1, 3 * KD])
        unit = sb("unit", [1, NP1])
        pjt = sb("pjt", [KD, D])
        pjb = sb("pjb", [1, D])
        axt = sb("axt", [KD, 3, NP1])
        mt = sb("mt", [NP1, NP1])
        wv = sb("wv", [NP1, D])
        gsb = atm[:].rearrange("p i g l -> p (i g l)")[0:NP1, 0:B * NI]
        prob = early[:, 0:2 * IT * NI].rearrange("p (b n m) -> p b n m", b=2, n=IT)
        probT = early[:, 2 * IT * NI:4 * IT * NI].rearrange("p (b n m) -> p b n m", b=2, n=IT)
        vs = early[:, 4 * IT * NI:4 * IT * NI + B * IT * D].rearrange("p (t d) -> p t d", d=D)
        nmax = sb("nmax", [P, B * IT])
        nbias = sb("nbias", [P, B * IT])
        rsum = sb("rsum", [P, B * IT])
        rinv = sb("rinv", [P, B * IT])
        h = sb("h", [P, T, D])
        wq = sb("wq", [DC + 1, 2, 3 * D + R])
        lnw = sb("lnw", [DC, 2])
        lnb = sb("lnb", [DC, 2])
        bq = sb("bq", [DC + 1, 3 * D])
        wb2 = sb("wb2", [R, 4 * H])
        wp = sb("wp", [DC + 1, 2, D])
        mnw = sb("mnw", [DC, 1])
        mnb = sb("mnb", [DC, 1])
        bp = sb("bp", [DC + 1, D])
        temp = sb("temp", [P, 1])
        htemp = sb("htemp", [P, 1])
        stat = sb("stat", [P, T, 6])
        mv = sb("mv", [P, T, 2])
        nwt = sb("nwt", [P, 6, CT * H])
        r1 = sb("r1", [P, T])
        r12 = sb("r12", [P, T])
        nmr = sb("nmr", [P, T])
        sh = sb("sh", [P, T])
        xn = sb("xn", [P, 2, D])
        xT = sb("xT", [DC + 1, 2, 2, P])
        eb = sb("eb", [P, 2, 2 * D])
        th = sb("th", [P, 2, R])
        g1 = sb("g1", [P, 2, R])
        g1T = sb("g1T", [P, 2, P])
        pr = sb("pr", [P, T, 4 * H])
        qk = sb("qk", [P, T, 2 * H, SLOT])
        ga = sb("ga", [P, T, 2 * H])
        gb = sb("gb", [P, T, 2 * H])
        gc = sb("gc", [P, T, H])
        gd = sb("gd", [P, T, H])
        gate1 = sb("gate1", [P, T, H])
        vg = sb("vg", [P, T, H, VE])
        state = sb("state", [P, 2, G, HG, VE])
        rden = sb("rden", [P, 2, H])
        o = sb("o", [P, 2, CT * H, DH])
        osq = sb("osq", [P, CT * H, DH])
        osum = sb("osum", [P, CT * H])
        oT = sb("oT", [DC + 1, 2, 2, P])
        x2 = sb("x2", [P, 2, CT, D])
        xr = sb("xr", [P, 2 * CT, 2 * D], F16)
        x2T = sb("x2T", [DC, 2, 2, P])
        wr = sb("wr", [DC, 2, E])
        lg = sb("lg", [P, T, E])
        w1h = sb("w1h", [P, E * FI], F16)
        w1l = sb("w1l", [P, E * FI], F16)
        w1bh = sb("w1bh", [P, E * FI], F16)
        w1bl = sb("w1bl", [D - P, E * FI], F16)
        w2h = sb("w2h", [P, E * MC * D], F16)
        w2l = sb("w2l", [P, E * MC * D], F16)
        iota_e = sb("iota_e", [P, E])
        iota_p = sb("iota_p", [P, P])
        iota_p16 = sb("iota_p16", [P, P], F16)
        row1 = sb("row1", [P, 1])
        choice1 = sb("choice1", [P, 2 * T])
        keep = sb("keep", [P, E, T])
        ls = sb("ls", [P, T, E])
        ex = sb("ex", [P, T, E])
        pb = sb("pb", [P, T, E])
        tmp = sb("tmp", [P, T, E])
        sel = sb("sel", [P, 2, T, E])
        selsum = sb("selsum", [P, T, E])
        small = sb("small", [P, 10, T])
        tot = sb("tot", [P, E, T])
        inc = sb("inc", [P, E, T])
        cnt = sb("cnt", [P, 4, E])
        cnti = sb("cnti", [P, E], I32)
        slot = sb("slot", [P, 2, T])
        sloti = sb("sloti", [P, 3, 2 * T], I32)
        slotf = sb("slotf", [P, 2, 2 * T])
        late = qk[:].rearrange("p t h e -> p (t h e)")
        at = [0]

        def carve(words):
            at[0] += words
            return late[:, at[0] - words:at[0]]

        cola = carve(T * P).bitcast(F16).rearrange("p (n c) -> p n c", c=P)
        cole = carve(2 * T * NSP).rearrange("p (n c) -> p n c", c=NSP)
        colb = carve(2 * T * NSP).bitcast(F16).rearrange("p (n v c) -> p n v c", v=2, c=NSP)
        src = sb("src", [P, 4, NSP])
        dst_row = sb("dst_row", [P, NSP], U32)
        tok_row = sb("tok_row", [P, NSP], U32)
        passed = sb("passed", [1, NSP, E])
        expf = sb("expf", [1, NSP])
        expert = sb("expert", [1, NSP], I32)
        imp = sb("imp", [P, E])
        gate = sb("gate", [P, 2, T])
        xg = carve(4 * D).bitcast(F16).rearrange("p (k c) -> p k c", k=4)
        xe = carve(3 * P).bitcast(F16).rearrange("p (k c) -> p k c", k=2)
        act32 = carve(2 * FI).rearrange("p (k c) -> p k c", k=2)
        acth = carve(FI).bitcast(F16).rearrange("p (k c) -> p k c", k=2)
        actl = carve(FI).bitcast(F16).rearrange("p (k c) -> p k c", k=2)
        ye = carve(4 * D).rearrange("p (k c) -> p k c", k=4)

        s_tok_loaded = sem("tok_loaded")
        s_img_loaded = sem("img_loaded")
        s_txt_loaded = sem("txt_loaded")
        s_attn_loaded = sem("attn_loaded")
        s_const_ready = sem("const_ready")
        s_pool_step = sem("pool_step")
        s_axt_mm = sem("axt_mm")
        s_axt_ready = sem("axt_ready")
        s_setup_mm = sem("setup_mm")
        s_mt_ready = sem("mt_ready")
        s_wv_ready = sem("wv_ready")
        s_lnb_mm = sem("lnb_mm")
        s_mnb_mm = sem("mnb_mm")
        s_wq_ready = sem("wq_ready")
        s_wp_ready = sem("wp_ready")
        s_step = sem("step")
        s_ones_ready = sem("ones_ready")
        s_g_mm = sem("g_mm")
        s_g_ready = sem("g_ready")
        s_vp_mm = sem("vp_mm")
        s_vp_ready = sem("vp_ready")
        s_score_mm = sem("score_mm")
        s_nbias_ready = sem("nbias_ready")
        s_prob_ready = sem("prob_ready")
        s_rinv_ready = sem("rinv_ready")
        s_pT_mm = sem("pT_mm")
        s_pT_ready = sem("pT_ready")
        s_himg_mm = sem("himg_mm")
        s_himg_ready = sem("himg_ready")
        s_ln1_ready = sem("ln1_ready")
        s_xn_ready = sem("xn_ready")
        s_xT_mm = sem("xT_mm")
        s_xT_ready = sem("xT_ready")
        s_qk_mm = sem("qk_mm")
        s_vb_mm = sem("vb_mm")
        s_exp_ready = sem("exp_ready")
        s_feat_ready = sem("feat_ready")
        s_tanh_ready = sem("tanh_ready")
        s_v_ready = sem("v_ready")
        s_g1_ready = sem("g1_ready")
        s_gT_mm = sem("gT_mm")
        s_gT_ready = sem("gT_ready")
        s_pr_mm = sem("pr_mm")
        s_pr_ready = sem("pr_ready")
        s_ga_ready = sem("ga_ready")
        s_dph_ready = sem("dph_ready")
        s_sin_ready = sem("sin_ready")
        s_cos_ready = sem("cos_ready")
        s_int_ready = sem("int_ready")
        s_gate_tanh = sem("gate_tanh")
        s_vg_ready = sem("vg_ready")
        s_t0_full = sem("t0_full")
        s_t0_free = sem("t0_free")
        s_t1_full = sem("t1_full")
        s_t1_free = sem("t1_free")
        s_at_mm = sem("at_mm")
        s_mask_done = sem("mask_done")
        s_state_mm = sem("state_mm")
        s_state_ready = sem("state_ready")
        s_num_mm = sem("num_mm")
        s_o_ready = sem("o_ready")
        s_osq_ready = sem("osq_ready")
        s_ohat_ready = sem("ohat_ready")
        s_x2_ready = sem("x2_ready")
        s_xhi_ready = sem("xhi_ready")
        s_xlo_ready = sem("xlo_ready")
        s_x2_stored = [sem(f"x2_stored{i}") for i in range(2)]
        s_w_loaded = [sem(f"w_loaded{i}") for i in range(2)]
        s_w_scaled = sem("w_scaled")
        s_w_high = sem("w_high")
        s_w_low = sem("w_low")
        s_iota_ready = sem("iota_ready")
        s_ls_ready = sem("ls_ready")
        s_ex_ready = sem("ex_ready")
        s_pb_ready = sem("pb_ready")
        s_sel_ready = sem("sel_ready")
        s_rank_mm = sem("rank_mm")
        s_imp_mm = sem("imp_mm")
        s_onehot_ready = sem("onehot_ready")
        s_src_mm = sem("src_mm")
        s_rows_ready = sem("rows_ready")
        s_expert_ready = sem("expert_ready")
        s_xg_clear = sem("xg_clear")
        s_gathered = [sem(f"gathered{i}") for i in range(4)]
        s_scattered = [sem(f"scattered{i}") for i in range(4)]
        s_xe_mm = sem("xe_mm")
        s_xe_ready = sem("xe_ready")
        s_up_mm = sem("up_mm")
        s_act_ready = sem("act_ready")
        s_high_ready = sem("high_ready")
        s_low_ready = sem("low_ready")
        s_down_mm = sem("down_mm")
        s_y_ready = sem("y_ready")
        s_y_loaded = [sem(f"y_loaded{i}") for i in range(4)]
        s_sum_ready = sem("sum_ready")
        s_out_done = sem("out_done")

        misc = [("tr", 0)]
        for t in range(T + 7):
            misc += [("tr", t + 1)] * (t + 1 < T) + [("o", t - 4)] * (0 <= t - 4 < T) + [("x", t - 7)] * (0 <= t - 7 < T)
        use = {k: n for n, k in enumerate(misc)}

        jobs = [("w1a", c) for c in range(0, E * FI, STG)] + [("w1b", c) for c in range(0, E * FI, STG)] + \
               [("w2", c) for c in range(0, E * MC * D, STG)]
        loads = [sum(2 if k == "w1b" else 1 for k, _ in jobs[n % 2:n + 1:2]) for n in range(len(jobs))]
        halves = {"w1a": (w1h, w1l), "w1b": (w1bh, w1bl), "w2": (w2h, w2l)}
        yt = [v[:, 0:T * D].rearrange("p (t d) -> p t d", t=T) for v in (vg[:].rearrange("p t h e -> p (t h e)"), late)]

        block = ctx.enter_context(nc.Block())

        @block.sync
        def _(sp):
            for dst, src in ((cwb, A["cwb"]), (wtok, A["wtok"]), (btok, A["btok"]), (unit, A["unit"]), (pjt, A["pjt"]), (pjb, A["pjb"])):
                sp.dma_start(dst[:], src).then_inc(s_tok_loaded, 16)
            sp.dma_start(xp1, A["xp1"]).then_inc(s_img_loaded, 16)
            for b in range(B):
                sp.dma_start(h[:, CT * b + IT, :], A["txt"][b]).then_inc(s_txt_loaded, 16)
            for dst, src_ in ((wq[0:DC, :, :], A["wq"]), (lnw[:], A["lnw"]), (lnb[:], A["lnb"]), (bq[DC:DC + 1, :], A["bqkv"]),
                             (wb2[:], A["wb2"]), (wp[0:DC, :, :], A["wp"]), (mnw[:], A["mnw"]), (mnb[:], A["mnb"]),
                             (bp[DC:DC + 1, :], A["bproj"]), (temp[:], A["temp"]), (wr[:], A["wr"])):
                sp.dma_start(dst, src_).then_inc(s_attn_loaded, 16)
            sp.wait_ge(s_himg_mm, B)
            for n, (kind, c0) in enumerate(jobs):
                if n >= 2:
                    sp.wait_ge(s_w_low, n - 1)
                if kind == "w1b":
                    for r in range(2):
                        sp.dma_start(stage[r * 64:(r + 1) * 64, n % 2, :], A["w1b"][:, c0:c0 + STG]).then_inc(s_w_loaded[n % 2], 16)
                else:
                    sp.dma_start(stage[:, n % 2, :], A[kind][:, c0:c0 + STG]).then_inc(s_w_loaded[n % 2], 16)
            for t in range(T):
                sp.wait_ge(s_xhi_ready, 2 * (t + 1))
                sp.wait_ge(s_xlo_ready, 2 * (t + 1))
                sp.dma_start(x2_dram[t * P:(t + 1) * P, :], xr[:, t % (2 * CT), :]).then_inc(s_x2_stored[t // CT % 2], 16)
            for k in range(4):
                sp.wait_ge(s_scattered[k], 16 * len(range(k, NS, 4)))
            for b in range(B):
                for k in range(2):
                    r0 = k * NTOK + b * CT * P
                    sp.dma_start(yt[k][:, b * CT:(b + 1) * CT, :], y_dram[r0:r0 + CT * P, :].rearrange("(c p) d -> p c d", p=P)).then_inc(s_y_loaded[b], 16)
            for b in range(B):
                sp.wait_ge(s_sum_ready, (b + 1) * CT)
                sp.dma_start(out[b].rearrange("(c p) d -> p c d", p=P), h[:, b * CT:(b + 1) * CT, :]).then_inc(s_out_done, 16)
            sp.wait_ge(s_out_done, 16 * B)

        @block.gpsimd
        def _(pool):
            step = [0]

            def link(ins):
                step[0] += 1
                ins.then_inc(s_pool_step, 1)
                pool.wait_ge(s_pool_step, step[0])

            pool.memset(ident[:], 0.0).then_inc(s_pool_step, 1)
            pool.memset(ident16[:], 0.0).then_inc(s_pool_step, 1)
            pool.memset(causal[:], 1.0).then_inc(s_pool_step, 1)
            pool.memset(before[:], 1.0).then_inc(s_pool_step, 1)
            pool.memset(headmask[:], 1.0).then_inc(s_pool_step, 1)
            step[0] = 5
            pool.wait_ge(s_pool_step, 5)
            for m in (ident, ident16):
                pool.affine_select(out=m[:], in_=m[:], compare_op=ALU.not_equal, fill=1.0, base=0,
                                   pattern=[[-1, P]], channel_multiplier=1).then_inc(s_const_ready, 1)
            pool.affine_select(out=causal[:], in_=causal[:], compare_op=ALU.is_ge, fill=0.0, base=0,
                               pattern=[[1, P]], channel_multiplier=-1).then_inc(s_const_ready, 1)
            pool.affine_select(out=before[:], in_=before[:], compare_op=ALU.is_ge, fill=0.0, base=-1,
                               pattern=[[1, P]], channel_multiplier=-1).then_inc(s_const_ready, 1)
            link(pool.affine_select(out=headmask[:], in_=headmask[:], compare_op=ALU.is_ge, fill=0.0, base=0,
                                    pattern=[[0, G], [-SLOT, HG], [0, VE]], channel_multiplier=1))
            pool.affine_select(out=headmask[:], in_=headmask[:], compare_op=ALU.is_ge, fill=0.0, base=SLOT - 1,
                               pattern=[[0, G], [SLOT, HG], [0, VE]], channel_multiplier=-1).then_inc(s_const_ready, 1)

            for dst, pattern, base, mul in ((iota_e, [[1, E]], -E, 0), (iota_p, [[1, P]], 0, 0), (iota_p16, [[1, P]], 0, 0),
                                            (row1, [[0, 1]], 1, 1), (choice1, [[1, 2 * T]], 1, 0)):
                pool.iota(dst[:], pattern, base=base, channel_multiplier=mul, allow_small_or_imprecise_dtypes=True).then_inc(s_iota_ready, 1)
            for n in range(len(jobs) + 1):
                if n < len(jobs):
                    pool.wait_ge(s_w_loaded[n % 2], 16 * loads[n])
                    pool.tensor_scalar(stage[:, n % 2, :], stage[:, n % 2, :], WS, None, ALU.mult).then_inc(s_w_scaled, 1)
                if n:
                    kind, c0 = jobs[n - 1]
                    high, low = halves[kind]
                    rows = D - P if kind == "w1b" else P
                    pool.wait_ge(s_w_high, n)
                    pool.tensor_tensor(low[0:rows, c0:c0 + STG], stage[0:rows, (n - 1) % 2, :], high[0:rows, c0:c0 + STG], ALU.subtract).then_inc(s_w_low, 1)

            def gather(i):
                if i >= 4:
                    pool.wait_ge(s_xe_mm, i - 3)
                pool.indirect_dma_start(xg[:, i % 4, :], None, x2_dram, bass.IndirectOffsetOnAxis(ap=tok_row[:, i:i + 1], axis=0),
                                        bounds_check=NTOK - 1, oob_is_err=False).then_inc(s_gathered[i % 4], 16)

            def scatter(i):
                pool.wait_ge(s_y_ready, i + 1)
                pool.indirect_dma_start(y_dram, bass.IndirectOffsetOnAxis(ap=dst_row[:, i:i + 1], axis=0), ye[:, i % 4, :], None,
                                        bounds_check=2 * NTOK - 1, oob_is_err=False).then_inc(s_scattered[i % 4], 16)

            pool.wait_ge(s_rank_mm, 1)
            pool.memset(xg, 0.0).then_inc(s_xg_clear, 1)
            pool.wait_ge(s_xg_clear, 1)
            for k in range(2):
                pool.wait_ge(s_x2_stored[k], 16 * T // 2)
            pool.wait_ge(s_rows_ready, 2)
            for i in range(4):
                gather(i)
            for i in range(NS):
                if i + 4 < NSP:
                    gather(i + 4)
                scatter(i)

        @block.tensor
        def _(pe):
            pe.wait_ge(s_tok_loaded, 96)
            for i in range(3):
                w = slice(i * KD, (i + 1) * KD)
                o_ = bank[0][0:KD, i * NP1:(i + 1) * NP1]
                pe.matmul(o_, wtok[:, 0, w], cwb[:, 0, :], start=True, stop=False)
                pe.matmul(o_, wtok[:, 1, w], cwb[:, 1, :], start=False, stop=False)
                mm = pe.matmul(o_, btok[:, w], unit[:], start=False, stop=True)
            mm.then_inc(s_axt_mm, 1)
            pe.wait_ge(s_axt_ready, 1)
            pe.matmul(bank[1][0:NP1, 0:NP1], axt[:, 1, :], axt[:, 0, :], start=True, stop=True).then_inc(s_setup_mm, 1)
            pe.matmul(bank[2][0:NP1, 0:D], axt[:, 2, :], pjt[:], start=True, stop=False)
            pe.matmul(bank[2][0:NP1, 0:D], unit[:], pjb[:], start=False, stop=True).then_inc(s_setup_mm, 1)
            pe.wait_ge(s_img_loaded, 16)
            pe.wait_ge(s_mt_ready, 1)
            for i in range(2):
                if i:
                    pe.wait_ge(s_g_ready, i)
                pe.matmul(bank[7][0:NP1, :], mt[:], xp1[:, i * 512:(i + 1) * 512], start=True, stop=True).then_inc(s_g_mm, 1)

            def scores(b):
                pe.wait_ge(s_g_ready, b // 2 + 1)
                if b >= 2:
                    pe.wait_ge(s_prob_ready, IT * (b - 1))
                else:
                    pe.wait_ge(s_axt_ready, 1)
                    pe.wait_ge(s_mt_ready, 1)
                for n in range(IT):
                    q0 = b * NI + n * P
                    mm = pe.matmul(bank[b % 2][:, n * NI:(n + 1) * NI], xp1[:, q0:q0 + P], gsb[:, b * NI:(b + 1) * NI], start=True, stop=True)
                mm.then_inc(s_score_mm, 1)

            def values(i):
                pe.wait_ge(s_wv_ready, 1)
                if i >= 2:
                    pe.wait_ge(s_vp_ready, i - 1)
                for n in range(IT):
                    m0 = (i * IT + n) * P
                    mm = pe.matmul(bank[5 + i % 2][:, n * D:(n + 1) * D], xp1[:, m0:m0 + P], wv[:], start=True, stop=True)
                mm.then_inc(s_vp_mm, 1)

            def prob_t(b):
                pe.wait_ge(s_prob_ready, IT * (b + 1))
                if b == 0:
                    pe.wait_ge(s_const_ready, 5)
                    pe.wait_ge(s_wv_ready, 1)
                if b >= 2:
                    pe.wait_ge(s_pT_ready, b - 1)
                for n in range(IT):
                    for j in range(IT):
                        mm = pe.transpose(bank[2 + b % 2][:, j * NI + n * P:j * NI + (n + 1) * P], prob[:, b % 2, n, j * P:(j + 1) * P], ident[:])
                mm.then_inc(s_pT_mm, 1)

            def himg(b):
                pe.wait_ge(s_pT_ready, b + 1)
                if b == 0:
                    pe.wait_ge(s_vp_ready, B)
                if b >= 2:
                    pe.wait_ge(s_himg_ready, IT * (b - 1))
                for n in range(IT):
                    for j in range(IT):
                        mm = pe.matmul(bank[5 + b % 2][:, n * D:(n + 1) * D], probT[:, b % 2, j, n * P:(n + 1) * P], vs[:, b * IT + j, :],
                                       start=(j == 0), stop=(j == IT - 1))
                mm.then_inc(s_himg_mm, 1)

            scores(0)
            scores(1)
            for i in range(B):
                values(i)
            pe.wait_ge(s_attn_loaded, 16 * 11)
            pe.wait_ge(s_g_ready, 2)
            for lo, hi, bk in ((0, 512, 4), (512, 3 * D, 7)):
                for c in range(2):
                    mm = pe.matmul(bank[bk][DC:DC + 1, 0:hi - lo], lnb[:, c:c + 1], wq[0:DC, c, lo:hi], start=(c == 0), stop=(c == 1))
            mm.then_inc(s_lnb_mm, 1)
            for c in range(2):
                mm = pe.matmul(bank[3][DC:DC + 1, 0:D], mnb[:, 0:1], wp[0:DC, c, :], start=(c == 0), stop=(c == 1))
            mm.then_inc(s_mnb_mm, 1)
            prob_t(0)
            himg(0)
            for b in range(1, B):
                if b + 1 < B:
                    scores(b + 1)
                if b == 1:
                    pe.wait_ge(s_wp_ready, 1)
                prob_t(b)
                himg(b)

            def x_t(t):
                pe.wait_ge(s_xn_ready, t + 1)
                if t >= 2:
                    pe.wait_ge(s_xT_ready, t - 1)
                else:
                    pe.wait_ge(s_prob_ready, B * IT)
                for c in range(2):
                    mm = pe.transpose(bank[t % 2][0:DC, c * P:(c + 1) * P], xn[:, t % 2, c * DC:(c + 1) * DC], ident[:])
                mm.then_inc(s_xT_mm, 1)

            def qkv(t):
                pe.wait_ge(s_xT_ready, t + 1)
                if t == 0:
                    pe.wait_ge(s_wq_ready, 3)
                    pe.wait_ge(s_ones_ready, 3)
                    pe.wait_ge(s_pT_ready, B)
                    pe.wait_ge(s_himg_ready, B * IT)
                if t >= 2:
                    pe.wait_ge(s_feat_ready, t - 1)
                for c in range(2):
                    mm = pe.matmul(bank[2 + t % 2][:, 0:2 * D], xT[0:DC + c, t % 2, c, :], wq[0:DC + c, c, 0:2 * D], start=(c == 0), stop=(c == 1))
                mm.then_inc(s_qk_mm, 1)
                if t >= 2:
                    pe.wait_ge(s_v_ready, t - 1)
                    pe.wait_ge(s_g1_ready, t - 1)
                for c in range(2):
                    mm = pe.matmul(bank[4 + t % 2][:, 0:D + R], xT[0:DC + c, t % 2, c, :], wq[0:DC + c, c, 2 * D:3 * D + R], start=(c == 0), stop=(c == 1))
                mm.then_inc(s_vb_mm, 1)

            def hidden_t(t):
                pe.wait_ge(s_g1_ready, t + 1)
                if t >= 1:
                    pe.wait_ge(s_gT_ready, t)
                pe.transpose(bank[6][:, 0:P], g1[:, t % 2, :], ident[:]).then_inc(s_gT_mm, 1)

            def params(t):
                pe.wait_ge(s_gT_ready, t + 1)
                if t >= 1:
                    pe.wait_ge(s_pr_ready, t)
                pe.matmul(bank[7][:, 0:4 * H], g1T[:, t % 2, :], wb2[:], start=True, stop=True).then_inc(s_pr_mm, 1)

            x_t(0)
            x_t(1)
            for t in range(T + 2):
                if t < T:
                    qkv(t)
                if t + 2 < T:
                    x_t(t + 2)
                if 1 <= t <= T:
                    hidden_t(t - 1)
                if t >= 2:
                    params(t - 2)

            def take(u):
                if u == 0:
                    pe.wait_ge(s_xT_ready, T)
                else:
                    pe.wait_ge(s_t0_free, u)
                    pe.wait_ge(s_t1_free, u)

            def heads_t(t):
                u = use["tr", t]
                take(u)
                pe.wait_ge(s_feat_ready, t + 1)
                for half, full in ((0, s_t0_full), (1, s_t1_full)):
                    for g in range(G):
                        h0 = half * H + g * HG
                        mm = pe.transpose(bank[half][:, g * P:(g + 1) * P], qk[:, t, h0:h0 + HG, :].rearrange("p h e -> p (h e)"), ident[:])
                    mm.then_inc(full, 1)

            def qk_products(t):
                pe.wait_ge(s_t0_free, use["tr", t] + 1)
                pe.wait_ge(s_t1_free, use["tr", t] + 1)
                if t:
                    pe.wait_ge(s_mask_done, HG * t)
                else:
                    pe.wait_ge(s_feat_ready, T)
                    pe.wait_ge(s_v_ready, T)
                for g in range(G):
                    for i in range(HG):
                        r = slice(SLOT * i, SLOT * i + DH)
                        mm = pe.matmul(bank[2 + i][:, g * P:(g + 1) * P], kT[r, t % 2, g * P:(g + 1) * P], qT[r, t % 2, g * P:(g + 1) * P],
                                       start=True, stop=True, tile_position=(SLOT * i, 0))
                mm.then_inc(s_at_mm, 1)

            def state_step(t):
                b, c = divmod(t, CT)
                pe.wait_ge(s_vg_ready, b + 1)
                if t == 0:
                    pe.wait_ge(s_pr_ready, T)
                else:
                    pe.wait_ge(s_state_ready, b * 2 + c)
                for g in range(G):
                    mm = pe.matmul(bank[7][:, g * HG * VE:(g + 1) * HG * VE],
                                   qk[:, t, H + g * HG:H + (g + 1) * HG, :].rearrange("p h e -> p (h e)"),
                                   vg[:, t, g * HG:(g + 1) * HG, :].rearrange("p h e -> p (h e)"),
                                   start=(c == 0 and g == 0), stop=(c == 1 and g == G - 1), skip_group_check=True)
                mm.then_inc(s_state_mm, 1)

            def numerators(t):
                b, c = divmod(t, CT)
                if t == 0:
                    pe.wait_ge(s_gT_ready, T)
                else:
                    pe.wait_ge(s_o_ready, t)
                if c:
                    pe.wait_ge(s_state_ready, 2 * b + c)
                    for g in range(G):
                        pe.matmul(bank[6][:, g * HG * VE:(g + 1) * HG * VE], qT[:, t % 2, g * P:(g + 1) * P],
                                  state[:, (t - 1) % 2, g, :, :].rearrange("p h e -> p (h e)"), start=(g == 0), stop=False, skip_group_check=True)
                pe.wait_ge(s_mask_done, HG * (t + 1))
                for hh in range(H):
                    g, i = divmod(hh, HG)
                    mm = pe.matmul(bank[6][:, hh * VE:(hh + 1) * VE], atm[:, i, g, :], vg[:, t, hh, :],
                                   start=(c == 0 and hh == 0), stop=(hh == H - 1), skip_group_check=True)
                mm.then_inc(s_num_mm, 1)

            def project(t):
                b, c = divmod(t, CT)
                u = use["o", t]
                take(u)
                pe.wait_ge(s_ohat_ready, b + 1)
                for j in range(2):
                    mm = pe.transpose(bank[0][0:DC, j * P:(j + 1) * P],
                                      o[:, b % 2, c * H:(c + 1) * H, :].rearrange("p h e -> p (h e)")[:, j * DC:(j + 1) * DC], ident[:])
                mm.then_inc(s_t0_full, 1)
                pe.wait_ge(s_t0_free, u + 1)
                if t == 0:
                    pe.wait_ge(s_wp_ready, 3)
                for j in range(2):
                    mm = pe.matmul(bank[1][:, 0:D], oT[0:DC + j, u % 2, j, :], wp[0:DC + j, j, :], start=(j == 0), stop=(j == 1))
                mm.then_inc(s_t1_full, 1)

            def route(t):
                b, c = divmod(t, CT)
                u = use["x", t]
                take(u)
                pe.wait_ge(s_x2_ready, t + 1)
                for j in range(2):
                    mm = pe.transpose(bank[0][0:DC, j * P:(j + 1) * P], x2[:, b % 2, c, j * DC:(j + 1) * DC], ident[:])
                mm.then_inc(s_t0_full, 1)
                pe.wait_ge(s_t0_free, u + 1)
                for j in range(2):
                    mm = pe.matmul(bank[1][:, 0:E], x2T[:, t % 2, j, :], wr[:, j, :], start=(j == 0), stop=(j == 1))
                mm.then_inc(s_t1_full, 1)

            heads_t(0)
            for t in range(T + 7):
                if t < T:
                    qk_products(t)
                if t + 1 < T:
                    heads_t(t + 1)
                if t < T and t % CT < 2:
                    state_step(t)
                if 0 <= t - 4 < T:
                    project(t - 4)
                if 0 <= t - 7 < T:
                    route(t - 7)
                if t < T:
                    numerators(t)

            pe.wait_ge(s_sel_ready, 1)
            pe.wait_ge(s_ones_ready, 1)
            pe.wait_ge(s_t0_free, len(misc))
            mv_ = selsum[:].rearrange("p t e -> p (t e)")
            pe.matmul(bank[0][:, 0:T * E], before[:], mv_, start=True, stop=True)
            pe.matmul(bank[0][:, T * E:2 * T * E], ones[:], mv_, start=True, stop=True).then_inc(s_rank_mm, 1)
            pe.wait_ge(s_pb_ready, 1)
            pe.wait_ge(s_t1_free, len(misc))
            pe.matmul(bank[5][:, 0:T * E], ones[:], pb[:].rearrange("p t e -> p (t e)"), start=True, stop=True).then_inc(s_imp_mm, 1)
            pe.wait_ge(s_onehot_ready, 2)
            for n in range(2 * T):
                mm = pe.matmul(bank[2][:, 0:2 * NSP], cola[:, n, :], colb[:, n, :, :].rearrange("p v j -> p (v j)"), start=(n == 0), stop=(n == 2 * T - 1))
            mm.then_inc(s_src_mm, 1)

            def rows_t(i, k, rnd, first=False):
                pe.wait_ge(s_gathered[k], 16 * (rnd + 1))
                if not first:
                    pe.wait_ge(s_xe_ready, i - 1)
                ps = bank[k % 2][:, 0:3 * P // 2].bitcast(F16)
                for j in range(3):
                    mm = pe.transpose(ps[:, j * P:(j + 1) * P], xg[:, k, j * P:(j + 1) * P], ident16[:])
                mm.then_inc(s_xe_mm, 1)

            def up(i, k, first=False):
                e = pe.value_load(expert[0:1, bass.ds(i, 1)], min_val=0, max_val=E - 1)
                pe.wait_ge(s_xe_ready, i + 1)
                if not first:
                    pe.wait_ge(s_high_ready, i - 1)
                k %= 2
                for m in range(MC):
                    o_ = bank[2 + k][:, m * P:(m + 1) * P]
                    w = bass.ds(e * FI + m * P, P)
                    pe.matmul(o_, w1h[:, w], xe[:, k, 0:P], start=True, stop=False)
                    pe.matmul(o_, w1h[:, w], xe[:, k, P:2 * P], start=False, stop=False)
                    pe.matmul(o_, w1l[:, w], xe[:, k, 0:P], start=False, stop=False)
                    pe.matmul(o_, w1bh[:, w], xe[:, k, 2 * P:3 * P], start=False, stop=False)
                    mm = pe.matmul(o_, w1bl[:, w], xe[0:D - P, k, 2 * P:3 * P], start=False, stop=True)
                mm.then_inc(s_up_mm, 1)

            def down(i, k, first=False):
                e = pe.value_load(expert[0:1, bass.ds(i, 1)], min_val=0, max_val=E - 1)
                pe.wait_ge(s_low_ready, i + 1)
                if not first:
                    pe.wait_ge(s_y_ready, i - 1)
                k %= 2
                o_ = bank[4 + k][:, 0:D]
                for m in range(MC):
                    c = slice(m * P, (m + 1) * P)
                    w = bass.ds(e * (MC * D) + m * D, D)
                    pe.matmul(o_, acth[:, k, c], w2h[:, w], start=(m == 0), stop=False)
                    pe.matmul(o_, acth[:, k, c], w2l[:, w], start=False, stop=False)
                    mm = pe.matmul(o_, actl[:, k, c], w2h[:, w], start=False, stop=(m == MC - 1))
                mm.then_inc(s_down_mm, 1)

            pe.wait_ge(s_w_low, len(jobs))
            pe.wait_ge(s_expert_ready, 1)
            rows_t(0, 0, 0, first=True)
            rows_t(1, 1, 0, first=True)
            up(0, 0, first=True)
            for i in range(1, LEAD):
                rows_t(i + 1, (i + 1) % 4, (i + 1) // 4)
                up(i, i % 4, first=(i < 2))
                down(i - 1, (i - 1) % 4, first=(i < 3))
            with pe.Fori(0, (NS - LEAD) // 4) as j:
                for k in range(LEAD, LEAD + 4):
                    i = 4 * j + k
                    rows_t(i + 1, (k + 1) % 4, j + (k + 1) // 4)
                    up(i, k % 4)
                    down(i - 1, (k - 1) % 4)
            down(NS - 1, (NS - 1) % 4)

        @block.scalar
        def _(act):
            act.wait_ge(s_setup_mm, 2)
            act.activation(wv[:], bank[2][0:NP1, 0:D], ACT.Copy).then_inc(s_wv_ready, 1)
            for i in range(2):
                act.wait_ge(s_g_mm, i + 1)
                act.activation(gsb[:, i * 512:(i + 1) * 512], bank[7][0:NP1, :], ACT.Copy).then_inc(s_g_ready, 1)
            for i in range(B):
                act.wait_ge(s_vp_mm, i + 1)
                act.activation(vs[:, i * IT:(i + 1) * IT, :].rearrange("p a d -> p (a d)"), bank[5 + i % 2][:, 0:IT * D], ACT.Copy).then_inc(s_vp_ready, 1)

            def softmax(b):
                act.wait_ge(s_nbias_ready, b + 1)
                if b >= 2:
                    act.wait_ge(s_pT_mm, b - 1)
                for n in range(IT):
                    i = b * IT + n
                    act.activation(prob[:, b % 2, n, :], bank[b % 2][:, n * NI:(n + 1) * NI], ACT.Exp, bias=nbias[:, i:i + 1],
                                   scale=KD ** -0.5, accum_out=rsum[:, i:i + 1]).then_inc(s_prob_ready, 1)

            def himg(b):
                act.wait_ge(s_himg_mm, b + 1)
                act.wait_ge(s_rinv_ready, b + 1)
                for n in range(IT):
                    i = b * IT + n
                    act.activation(h[:, b * CT + n, :], bank[5 + b % 2][:, n * D:(n + 1) * D], ACT.Copy, scale=rinv[:, i:i + 1]).then_inc(s_himg_ready, 1)

            softmax(0)
            softmax(1)
            for b in range(B):
                himg(b)
                if b + 2 < B:
                    softmax(b + 2)

            def x_t(t):
                act.wait_ge(s_xT_mm, t + 1)
                if t >= 2:
                    act.wait_ge(s_vb_mm, t - 1)
                act.activation(xT[0:DC, t % 2, :, :].rearrange("p c n -> p (c n)"), bank[t % 2][0:DC, 0:2 * P], ACT.Copy).then_inc(s_xT_ready, 1)

            x_t(0)
            x_t(1)
            for t in range(T + 2):
                if t < T:
                    act.wait_ge(s_qk_mm, t + 1)
                    if t >= 2:
                        act.wait_ge(s_feat_ready, t - 1)
                    act.activation(eb[:, t % 2, :], bank[2 + t % 2][:, 0:2 * D], ACT.Exp).then_inc(s_exp_ready, 1)
                    act.wait_ge(s_vb_mm, t + 1)
                    if t >= 2:
                        act.wait_ge(s_g1_ready, t - 1)
                    act.activation(th[:, t % 2, :], bank[4 + t % 2][:, D:D + R], ACT.Tanh, scale=sh[:, t:t + 1]).then_inc(s_tanh_ready, 1)
                    act.activation(vg[:, t, :, 0:DH], bank[4 + t % 2][:, 0:D].rearrange("p (h e) -> p h e", e=DH), ACT.Copy).then_inc(s_v_ready, 1)
                if t + 2 < T:
                    x_t(t + 2)
                if 1 <= t <= T:
                    act.wait_ge(s_gT_mm, t)
                    if t >= 3:
                        act.wait_ge(s_pr_mm, t - 2)
                    act.activation(g1T[:, (t - 1) % 2, :], bank[6][:, 0:P], ACT.Copy).then_inc(s_gT_ready, 1)
                if t >= 2:
                    act.wait_ge(s_pr_mm, t - 1)
                    act.activation(pr[:, t - 2, :], bank[7][:, 0:4 * H], ACT.Copy, scale=sh[:, t - 2:t - 1]).then_inc(s_pr_ready, 1)
            act.wait_ge(s_pr_ready, T)
            act.activation(ga[:], pr[:, :, 0:2 * H], ACT.Tanh, scale=0.5).then_inc(s_ga_ready, 1)
            act.activation(gb[:], pr[:, :, 2 * H:4 * H], ACT.Tanh).then_inc(s_ga_ready, 1)
            act.wait_ge(s_dph_ready, 1)
            act.activation(gd[:], gc[:], ACT.Sin, scale=PI / 4).then_inc(s_sin_ready, 1)
            act.wait_ge(s_cos_ready, 1)
            act.activation(gd[:], gc[:], ACT.Tanh, scale=0.25).then_inc(s_gate_tanh, 1)
            act.wait_ge(s_gate_tanh, 1)
            act.activation(gate1[:], gd[:], ACT.Tanh, scale=htemp[:, 0:1]).then_inc(s_gate_tanh, 1)

            def heads_t(t):
                u = use["tr", t]
                if t >= 2:
                    act.wait_ge(s_at_mm, t - 1)
                    act.wait_ge(s_num_mm, t - 1)
                act.wait_ge(s_t0_full, u + 1)
                act.activation(qT[:, t % 2, :], bank[0][:, 0:G * P], ACT.Copy).then_inc(s_t0_free, 1)
                act.wait_ge(s_t1_full, u + 1)
                act.activation(kT[:, t % 2, :], bank[1][:, 0:G * P], ACT.Copy).then_inc(s_t1_free, 1)

            heads_t(0)
            for t in range(T + 7):
                if t + 1 < T:
                    heads_t(t + 1)
                if 0 <= t - 4 < T:
                    u = use["o", t - 4]
                    act.wait_ge(s_t0_full, u + 1)
                    act.activation(oT[0:DC, u % 2, :, :].rearrange("p c n -> p (c n)"), bank[0][0:DC, 0:2 * P], ACT.Copy).then_inc(s_t0_free, 1)
                if 0 <= t - 7 < T:
                    u = use["x", t - 7]
                    act.wait_ge(s_t0_full, u + 1)
                    act.activation(x2T[:, (t - 7) % 2, :, :].rearrange("p c n -> p (c n)"), bank[0][0:DC, 0:2 * P], ACT.Copy).then_inc(s_t0_free, 1)
                    act.wait_ge(s_t1_full, u + 1)
                    act.activation(lg[:, t - 7, :], bank[1][:, 0:E], ACT.Copy).then_inc(s_t1_free, 1)
                if t % CT == 0 and 0 <= t // CT - 2 < B:
                    b = t // CT - 2
                    for c in range(CT):
                        act.wait_ge(s_x2_ready, b * CT + c + 1)
                        if b >= 2:
                            act.wait_ge(s_x2_stored[b % 2], 16 * CT)
                        xrow = xr[:, b % 2 * CT + c, :]
                        act.activation(xrow[:, 0:P], x2[:, b % 2, c, 0:P], ACT.Copy).then_inc(s_xhi_ready, 1)
                        act.activation(xrow[:, 2 * P:P + D], x2[:, b % 2, c, P:D], ACT.Copy).then_inc(s_xhi_ready, 1)
                if t < len(jobs):
                    kind, c0 = jobs[t]
                    act.wait_ge(s_w_scaled, t + 1)
                    act.activation(halves[kind][0][:, c0:c0 + STG], stage[:, t % 2, :], ACT.Copy).then_inc(s_w_high, 1)
            act.wait_ge(s_ls_ready, 1)
            act.activation(ex[:], ls[:], ACT.Exp).then_inc(s_ex_ready, 1)

            def silu(i, k, first=False):
                act.wait_ge(s_up_mm, i + 1)
                if not first:
                    act.wait_ge(s_low_ready, i - 1)
                    act.wait_ge(s_down_mm, i - 1)
                act.activation(act32[:, k, :], bank[2 + k][:, :], ACT.Silu, scale=1.0 / WS).then_inc(s_act_ready, 1)
                act.activation(acth[:, k, :], bank[2 + k][:, :], ACT.Silu, scale=1.0 / WS).then_inc(s_high_ready, 1)

            silu(0, 0, first=True)
            silu(1, 1, first=True)
            for i in range(2, LEAD):
                silu(i, i % 2)
            with act.Fori(0, (NS - LEAD) // 4) as j:
                for k in range(LEAD, LEAD + 4):
                    silu(4 * j + k, k % 2)

        @block.vector
        def _(dve):
            step = [0]

            def link(ins):
                step[0] += 1
                ins.then_inc(s_step, 1)
                dve.wait_ge(s_step, step[0])

            def rsqrt(y, a, w):
                sq = nwt[:, 5, 0:w]
                yi = y.bitcast(I32)
                link(dve.tensor_scalar(yi, a.bitcast(I32), 1, None, ALU.logical_shift_right))
                link(dve.tensor_scalar(yi, yi, -1.0, RSQRT_MAGIC, ALU.mult, ALU.add))
                for _ in range(3):
                    link(dve.tensor_tensor(sq, y, y, ALU.mult))
                    link(dve.scalar_tensor_tensor(out=sq, in0=sq, scalar=-0.5, in1=a, op0=ALU.mult, op1=ALU.mult))
                    link(dve.scalar_tensor_tensor(out=y, in0=sq, scalar=1.5, in1=y, op0=ALU.add, op1=ALU.mult))

            dve.memset(ones[:], 1.0).then_inc(s_ones_ready, 1)
            dve.memset(xT[DC:DC + 1, :, :, :], 1.0).then_inc(s_ones_ready, 1)
            dve.memset(oT[DC:DC + 1, :, :, :], 1.0).then_inc(s_ones_ready, 1)
            dve.memset(wq[DC:DC + 1, 1, 3 * D:3 * D + R], 0.0).then_inc(s_wq_ready, 1)
            link(dve.memset(qk[:, :, :, DH:SLOT], 0.0))
            link(dve.memset(vg[:, :, :, DH:VE], 1.0))
            dve.wait_ge(s_axt_mm, 1)
            dve.tensor_copy(axt[:].rearrange("p a n -> p (a n)"), bank[0][0:KD, 0:3 * NP1]).then_inc(s_axt_ready, 1)
            dve.wait_ge(s_setup_mm, 1)
            dve.tensor_copy(mt[:], bank[1][0:NP1, 0:NP1]).then_inc(s_mt_ready, 1)

            def negmax(b):
                dve.wait_ge(s_score_mm, b + 1)
                i = b * IT
                link(dve.tensor_reduce(nmax[:, i:i + IT], bank[b % 2][:, :].rearrange("p (n m) -> p n m", n=IT), AX_X, ALU.max, negate=True))
                dve.tensor_scalar(nbias[:, i:i + IT], nmax[:, i:i + IT], KD ** -0.5, None, ALU.mult).then_inc(s_nbias_ready, 1)

            negmax(0)
            negmax(1)
            dve.wait_ge(s_attn_loaded, 16 * 11)
            dve.wait_ge(s_lnb_mm, 1)
            dve.wait_ge(s_mnb_mm, 1)
            link(dve.tensor_tensor(wq[DC:DC + 1, 1, 0:512], bank[4][DC:DC + 1, 0:512], bq[DC:DC + 1, 0:512], ALU.add))
            link(dve.tensor_tensor(wq[DC:DC + 1, 1, 512:3 * D], bank[7][DC:DC + 1, 0:3 * D - 512], bq[DC:DC + 1, 512:3 * D], ALU.add))
            dve.tensor_tensor(wp[DC:DC + 1, 1, :], bank[3][DC:DC + 1, 0:D], bp[DC:DC + 1, :], ALU.add).then_inc(s_wp_ready, 1)
            for c in range(2):
                dve.tensor_scalar(wq[0:DC, c, 0:3 * D], wq[0:DC, c, 0:3 * D], lnw[:, c:c + 1], None, ALU.mult).then_inc(s_wq_ready, 1)
                dve.tensor_scalar(wp[0:DC, c, :], wp[0:DC, c, :], mnw[:, 0:1], None, ALU.mult).then_inc(s_wp_ready, 1)
            link(dve.tensor_scalar(htemp[:], temp[:], 0.1, 2.0, ALU.max, ALU.min))
            link(dve.tensor_scalar(htemp[:], htemp[:], 0.5, None, ALU.mult))

            def moments(t, src):
                link(dve.bn_stats(stat[:, t, :], src))
                link(dve.bn_aggr(mv[:, t, :], stat[:, t, :]))

            dve.wait_ge(s_txt_loaded, 16 * B)
            for b in range(B):
                moments(b * CT + IT, h[:, b * CT + IT, :])
            for b in range(B):
                dve.wait_ge(s_prob_ready, IT * (b + 1))
                dve.reciprocal(rinv[:, b * IT:(b + 1) * IT], rsum[:, b * IT:(b + 1) * IT]).then_inc(s_rinv_ready, 1)
                dve.wait_ge(s_pT_mm, b + 1)
                if b >= 2:
                    dve.wait_ge(s_himg_mm, b - 1)
                dve.tensor_copy(probT[:, b % 2, :, :].rearrange("p a n -> p (a n)"), bank[2 + b % 2][:, :]).then_inc(s_pT_ready, 1)
                if b + 2 < B:
                    negmax(b + 2)
                if b >= 1:
                    for n in range(IT):
                        dve.wait_ge(s_himg_ready, (b - 1) * IT + n + 1)
                        moments((b - 1) * CT + n, h[:, (b - 1) * CT + n, :])
            for n in range(IT):
                dve.wait_ge(s_himg_ready, (B - 1) * IT + n + 1)
                moments((B - 1) * CT + n, h[:, (B - 1) * CT + n, :])

            mean, var = mv[:, :, 0], mv[:, :, 1]
            va, r2 = nwt[:, 0, 0:T], nwt[:, 1, 0:T]
            link(dve.tensor_scalar(va, var, EPS, None, ALU.add))
            rsqrt(r1[:], va, T)
            link(dve.tensor_tensor(va, var, r1[:], ALU.mult))
            link(dve.tensor_tensor(va, va, r1[:], ALU.mult))
            link(dve.tensor_scalar(va, va, EPS, None, ALU.add))
            rsqrt(r2, va, T)
            link(dve.scalar_tensor_tensor(out=sh[:], in0=va, scalar=0.5, in1=r2, op0=ALU.mult, op1=ALU.mult))
            link(dve.tensor_tensor(r12[:], r1[:], r2, ALU.mult))
            link(dve.scalar_tensor_tensor(out=nmr[:], in0=mean, scalar=-1.0, in1=r12[:], op0=ALU.mult, op1=ALU.mult))

            def normalize(t):
                if t >= 2:
                    dve.wait_ge(s_xT_mm, t - 1)
                dve.tensor_scalar(xn[:, t % 2, :], h[:, t, :], r12[:, t:t + 1], nmr[:, t:t + 1], ALU.mult, ALU.add).then_inc(s_xn_ready, 1)

            normalize(0)
            normalize(1)
            for t in range(T):
                dve.wait_ge(s_exp_ready, t + 1)
                link(dve.tensor_scalar(eb[:, t % 2, :], eb[:, t % 2, :], 1.0, None, ALU.min))
                dve.scalar_tensor_tensor(out=qk[:, t, :, 0:DH], in0=bank[2 + t % 2][:, 0:2 * D].rearrange("p (h e) -> p h e", e=DH), scalar=0.0,
                                         in1=eb[:, t % 2, :].rearrange("p (h e) -> p h e", e=DH), op0=ALU.max, op1=ALU.add).then_inc(s_feat_ready, 1)
                dve.wait_ge(s_tanh_ready, t + 1)
                dve.wait_ge(s_v_ready, t + 1)
                if t >= 2:
                    dve.wait_ge(s_gT_mm, t - 1)
                dve.scalar_tensor_tensor(out=g1[:, t % 2, :], in0=th[:, t % 2, :], scalar=1.0, in1=bank[4 + t % 2][:, D:D + R],
                                         op0=ALU.add, op1=ALU.mult).then_inc(s_g1_ready, 1)
                if t + 2 < T:
                    normalize(t + 2)
            dve.wait_ge(s_ga_ready, 2)
            dve.tensor_tensor(gc[:], gb[:, :, 0:H], gb[:, :, H:2 * H], ALU.subtract).then_inc(s_dph_ready, 1)
            link(dve.tensor_scalar(ga[:], ga[:], 1.0, None, ALU.add))
            link(dve.tensor_tensor(ga[:, :, 0:H], ga[:, :, 0:H], ga[:, :, H:2 * H], ALU.mult))
            dve.wait_ge(s_sin_ready, 1)
            link(dve.tensor_tensor(gc[:], gd[:], gd[:], ALU.mult))
            link(dve.tensor_scalar(gc[:], gc[:], -2.0, 1.0, ALU.mult, ALU.add))
            link(dve.tensor_tensor(gc[:], gc[:], gc[:], ALU.mult))
            link(dve.tensor_scalar(gc[:], gc[:], 2.0, -1.0, ALU.mult, ALU.add))
            dve.tensor_tensor(gc[:], gc[:], ga[:, :, 0:H], ALU.mult).then_inc(s_cos_ready, 1)
            dve.wait_ge(s_gate_tanh, 2)
            link(dve.tensor_scalar(gate1[:], gate1[:], 0.5, 1.5, ALU.mult, ALU.add))

            def gated_values(b):
                for t in range(b * CT, (b + 1) * CT):
                    ins = dve.tensor_tensor(vg[:, t, :, 0:DH], vg[:, t, :, 0:DH],
                                            gate1[:, t, :].unsqueeze(2).broadcast_to([P, H, DH]), ALU.mult)
                    if t == (b + 1) * CT - 1:
                        ins.then_inc(s_vg_ready, 1)

            gated_values(0)
            for t in range(T + 7):
                b, c = divmod(t, CT)
                if t < T:
                    dve.wait_ge(s_at_mm, t + 1)
                    if t:
                        dve.wait_ge(s_num_mm, t)
                    for i in range(HG):
                        dve.tensor_tensor(atm[:, i, :, :], bank[2 + i][:, 0:G * P].rearrange("p (g l) -> p g l", g=G),
                                          causal[:].unsqueeze(1).broadcast_to([P, G, P]), ALU.mult).then_inc(s_mask_done, 1)
                    if c < 2:
                        dve.wait_ge(s_state_mm, 2 * b + c + 1)
                        dve.tensor_tensor(state[:, t % 2, :, :, :].rearrange("p g h e -> p (g h e)"), bank[7][:, 0:H * VE],
                                          headmask[:].rearrange("p g h e -> p (g h e)"), ALU.mult).then_inc(s_state_ready, 1)
                if c == 0 and 1 <= b <= B:
                    ob = o[:, (b - 1) % 2, :, :]
                    va, r = nwt[:, 0, :], nwt[:, 1, :]
                    dve.wait_ge(s_o_ready, t)
                    link(dve.tensor_reduce(osum[:], ob, AX_X, ALU.add))
                    link(dve.tensor_scalar(osum[:], osum[:], 1.0 / DH, None, ALU.mult))
                    link(dve.tensor_tensor(ob, ob, osum[:].unsqueeze(2).broadcast_to([P, CT * H, DH]), ALU.subtract))
                    link(dve.tensor_tensor(osq[:], ob, ob, ALU.mult))
                    link(dve.tensor_reduce(va, osq[:], AX_X, ALU.add))
                    link(dve.tensor_scalar(va, va, 1.0 / DH, EPS, ALU.mult, ALU.add))
                    rsqrt(r, va, CT * H)
                    dve.tensor_tensor(ob, ob, r.unsqueeze(2).broadcast_to([P, CT * H, DH]), ALU.mult).then_inc(s_ohat_ready, 1)
                if c == 1 and b + 1 < B:
                    gated_values(b + 1)
                if 0 <= t - 4 < T:
                    tt = t - 4
                    u = use["o", tt]
                    dve.wait_ge(s_t1_full, u + 1)
                    dve.tensor_tensor(h[:, tt, :], bank[1][:, 0:D], h[:, tt, :], ALU.add).then_inc(s_t1_free, 1)
                    dve.wait_ge(s_t1_free, u + 1)
                    moments(tt, h[:, tt, :])
                    if tt % CT == CT - 1:
                        t0 = tt - CT + 1
                        va, r = nwt[:, 2, 0:CT], nwt[:, 3, 0:CT]
                        nm = nwt[:, 4, 0:CT]
                        link(dve.tensor_scalar(va, mv[:, t0:tt + 1, 1], EPS, None, ALU.add))
                        rsqrt(r, va, CT)
                        link(dve.scalar_tensor_tensor(out=nm, in0=mv[:, t0:tt + 1, 0], scalar=-1.0, in1=r, op0=ALU.mult, op1=ALU.mult))
                        if tt // CT >= 2:
                            dve.wait_ge(s_t0_full, use["x", tt - 2 * CT] + 1)
                        for cc in range(CT):
                            dve.tensor_scalar(x2[:, (tt // CT) % 2, cc, :], h[:, t0 + cc, :], r[:, cc:cc + 1], nm[:, cc:cc + 1],
                                              ALU.mult, ALU.add).then_inc(s_x2_ready, 1)
                        for cc in range(CT):
                            dve.wait_ge(s_xhi_ready, 2 * (t0 + cc + 1))
                            xrow, xf = xr[:, (tt // CT) % 2 * CT + cc, :], x2[:, (tt // CT) % 2, cc, :]
                            dve.tensor_tensor(xrow[:, P:2 * P], xf[:, 0:P], xrow[:, 0:P], ALU.subtract).then_inc(s_xlo_ready, 1)
                            dve.tensor_tensor(xrow[:, P + D:2 * D], xf[:, P:D], xrow[:, 2 * P:P + D], ALU.subtract).then_inc(s_xlo_ready, 1)
                if t < T:
                    dve.wait_ge(s_num_mm, t + 1)
                    num = bank[6][:, 0:H * VE].rearrange("p (h e) -> p h e", e=VE)
                    link(dve.tensor_scalar(rden[:, 0, :], num[:, :, DH], 1e-6, None, ALU.add))
                    link(dve.reciprocal(rden[:, 1, :], rden[:, 0, :]))
                    dve.tensor_tensor(o[:, b % 2, c * H:(c + 1) * H, :], num[:, :, 0:DH], rden[:, 1, :].unsqueeze(2).broadcast_to([P, H, DH]),
                                      ALU.mult).then_inc(s_o_ready, 1)

            def bt(v, n=E):
                return v.unsqueeze(2).broadcast_to([P, T, n])

            def be(v):
                return v.unsqueeze(1).broadcast_to([P, T, E])

            dve.wait_ge(s_iota_ready, 5)
            link(dve.memset(keep[:], 1.0))
            link(dve.memset(keep[:, :, 0:1], 0.0))
            dve.wait_ge(s_t1_free, len(misc))
            mx, e1, e2, b1, b2, rs, z = (small[:, n, :] for n in range(7))
            link(dve.tensor_reduce(mx, lg[:], AX_X, ALU.max))
            dve.tensor_tensor(ls[:], lg[:], bt(mx), ALU.subtract).then_inc(s_ls_ready, 1)
            dve.wait_ge(s_ls_ready, 1)

            def first_of(eq, dst):
                link(dve.tensor_tensor(eq, eq, be(iota_e[:]), ALU.mult))
                link(dve.tensor_reduce(mx, eq, AX_X, ALU.min))
                link(dve.tensor_tensor(dst, be(iota_e[:]), bt(mx), ALU.is_equal))

            link(dve.tensor_scalar(tmp[:], ls[:], 0.0, None, ALU.is_equal))
            first_of(tmp[:], sel[:, 0, :, :])
            link(dve.scalar_tensor_tensor(out=pb[:], in0=sel[:, 0, :, :], scalar=-1e30, in1=ls[:], op0=ALU.mult, op1=ALU.add))
            link(dve.tensor_reduce(mx, pb[:], AX_X, ALU.max))
            link(dve.tensor_tensor(tmp[:], pb[:], bt(mx), ALU.is_equal))
            first_of(tmp[:], sel[:, 1, :, :])
            dve.tensor_tensor(selsum[:], sel[:, 0, :, :], sel[:, 1, :, :], ALU.add).then_inc(s_sel_ready, 1)
            dve.wait_ge(s_ex_ready, 1)
            link(dve.tensor_reduce(z, ex[:], AX_X, ALU.add))
            link(dve.reciprocal(rs, z))
            dve.tensor_tensor(pb[:], ex[:], bt(rs), ALU.mult).then_inc(s_pb_ready, 1)
            dve.wait_ge(s_rank_mm, 1)
            link(dve.tensor_copy(tot[:], bank[0][:, T * E:2 * T * E].rearrange("p (t e) -> p e t", e=E)))
            flat = lambda v: v[:].rearrange("p e t -> p (e t)")
            link(dve.tensor_tensor_scan(flat(inc), flat(keep), flat(tot), 0.0, ALU.mult, ALU.add))
            link(dve.tensor_scalar(cnti[:], inc[:, :, T - 1], float(P - 1), None, ALU.add))
            link(dve.tensor_scalar(cnti[:], cnti[:], 7, None, ALU.logical_shift_right))
            link(dve.tensor_copy(cnt[:, 0, :], cnti[:]))
            link(dve.tensor_tensor_scan(cnt[:, 1, :], ones[:, 0:E], cnt[:, 0, :], 0.0, ALU.mult, ALU.add))
            link(dve.tensor_tensor(cnt[:, 2, :], cnt[:, 1, :], cnt[:, 0, :], ALU.subtract))
            link(dve.tensor_tensor(inc[:], inc[:], tot[:], ALU.subtract))
            link(dve.tensor_tensor(tmp[:], bank[0][:, 0:T * E].rearrange("p (t e) -> p t e", e=E), inc[:].rearrange("p e t -> p t e"), ALU.add))
            link(dve.tensor_scalar(cnt[:, 3, :], cnt[:, 2, :], float(P), None, ALU.mult))
            link(dve.tensor_tensor(tmp[:], tmp[:], be(cnt[:, 3, :]), ALU.add))
            for k in range(2):
                link(dve.tensor_tensor(ls[:], sel[:, k, :, :], tmp[:], ALU.mult))
                link(dve.tensor_reduce(slot[:, k, :], ls[:], AX_X, ALU.add))
            link(dve.tensor_copy(sloti[:, 0, :], slot[:].rearrange("p k t -> p (k t)")))
            link(dve.tensor_scalar(sloti[:, 1, :], sloti[:, 0, :], 7, None, ALU.logical_shift_right))
            link(dve.tensor_scalar(sloti[:, 2, :], sloti[:, 0, :], P - 1, None, ALU.bitwise_and))
            link(dve.tensor_copy(slotf[:], sloti[:, 1:3, :]))
            for n in range(2 * T):
                ins = dve.tensor_scalar(cola[:, n, :], iota_p16[:], slotf[:, 1, n:n + 1], None, ALU.is_equal)
            ins.then_inc(s_onehot_ready, 1)
            link(dve.tensor_tensor(cole, iota_p[:, 0:NSP].unsqueeze(1).broadcast_to([P, 2 * T, NSP]),
                                   slotf[:, 0, :].unsqueeze(2).broadcast_to([P, 2 * T, NSP]), ALU.is_equal))
            link(dve.tensor_scalar(colb[:, :, 0, :], cole, row1[:, 0:1], None, ALU.mult))
            dve.tensor_tensor(colb[:, :, 1, :], cole, choice1[:].unsqueeze(2).broadcast_to([P, 2 * T, NSP]), ALU.mult).then_inc(s_onehot_ready, 1)
            link(dve.tensor_tensor(passed[:], cnt[0:1, 1, :].unsqueeze(1).broadcast_to([1, NSP, E]),
                                   iota_p[0:1, 0:NSP].unsqueeze(2).broadcast_to([1, NSP, E]), ALU.is_le))
            link(dve.tensor_reduce(expf[:], passed[:], AX_X, ALU.add))
            dve.tensor_scalar(expert[:], expf[:], float(E - 1), None, ALU.min).then_inc(s_expert_ready, 1)
            dve.wait_ge(s_src_mm, 1)
            link(dve.tensor_copy(src[:, 0:2, :].rearrange("p v j -> p (v j)"), bank[2][:, 0:2 * NSP]))
            link(dve.scalar_tensor_tensor(out=src[:, 2, :], in0=src[:, 1, :], scalar=float(P), in1=src[:, 0, :], op0=ALU.mult, op1=ALU.add))
            link(dve.tensor_scalar(src[:, 3, :], src[:, 0, :], 0.0, NO_TOKEN, ALU.is_equal, ALU.mult))
            link(dve.tensor_tensor(src[:, 2, :], src[:, 2, :], src[:, 3, :], ALU.add))
            dve.tensor_scalar(dst_row[:], src[:, 2, :], -float(P + 1), None, ALU.add).then_inc(s_rows_ready, 1)
            link(dve.tensor_scalar(src[:, 3, :], src[:, 2, :], float(NTOK + P + 1), -float(NTOK), ALU.is_ge, ALU.mult))
            link(dve.tensor_tensor(src[:, 3, :], src[:, 3, :], src[:, 2, :], ALU.add))
            dve.tensor_scalar(tok_row[:], src[:, 3, :], -float(P + 1), None, ALU.add).then_inc(s_rows_ready, 1)

            def rows_t(i, k, first=False):
                dve.wait_ge(s_xe_mm, i + 1)
                if not first:
                    dve.wait_ge(s_up_mm, i - 1)
                dve.tensor_copy(xe[:, k, :], bank[k][:, 0:3 * P // 2].bitcast(F16)).then_inc(s_xe_ready, 1)

            def low(i, k, first=False):
                dve.wait_ge(s_high_ready, i + 1)
                if not first:
                    dve.wait_ge(s_down_mm, i - 1)
                dve.tensor_tensor(actl[:, k, :], act32[:, k, :], acth[:, k, :], ALU.subtract).then_inc(s_low_ready, 1)

            def result(i, k, rnd=None):
                dve.wait_ge(s_down_mm, i + 1)
                if rnd is not None:
                    dve.wait_ge(s_scattered[k], 16 * rnd)
                dve.tensor_scalar(ye[:, k, :], bank[4 + k % 2][:, 0:D], 1.0 / WS, None, ALU.mult).then_inc(s_y_ready, 1)

            dve.wait_ge(s_imp_mm, 1)
            link(dve.tensor_reduce(imp[:], bank[5][:, 0:T * E].rearrange("p (t e) -> p e t", e=E), AX_X, ALU.add))
            link(dve.tensor_scalar(imp[:], imp[:], 0.1, 0.91, ALU.mult, ALU.add))
            for k, ek, bk in ((0, e1, b1), (1, e2, b2)):
                link(dve.tensor_tensor(ls[:], sel[:, k, :, :], ex[:], ALU.mult))
                link(dve.tensor_reduce(ek, ls[:], AX_X, ALU.add))
                link(dve.tensor_tensor(ls[:], sel[:, k, :, :], be(imp[:]), ALU.mult))
                link(dve.tensor_reduce(bk, ls[:], AX_X, ALU.add))
            link(dve.tensor_tensor(e1, e1, b2, ALU.mult))
            link(dve.tensor_tensor(e2, e2, b1, ALU.mult))
            link(dve.tensor_tensor(z, e1, e2, ALU.add))
            link(dve.reciprocal(rs, z))
            link(dve.tensor_tensor(gate[:, 0, :], e1, rs, ALU.mult))
            link(dve.tensor_tensor(gate[:, 1, :], e2, rs, ALU.mult))
            rows_t(0, 0, first=True)
            rows_t(1, 1, first=True)
            low(0, 0, first=True)
            for i in range(1, LEAD):
                rows_t(i + 1, (i + 1) % 2)
                low(i, i % 2, first=(i < 2))
                result(i - 1, (i - 1) % 4, rnd=(i - 1) // 4 or None)
            with dve.Fori(0, (NS - LEAD) // 4) as j:
                for k in range(LEAD, LEAD + 4):
                    i = 4 * j + k
                    rows_t(i + 1, (k + 1) % 2)
                    low(i, k % 2)
                    result(i - 1, (k - 1) % 4, rnd=j + (k - 1) // 4)
            result(NS - 1, (NS - 1) % 4, rnd=(NS - 1) // 4)

            for b in range(B):
                dve.wait_ge(s_y_loaded[b], 32)
                for t in range(b * CT, (b + 1) * CT):
                    link(dve.scalar_tensor_tensor(out=h[:, t, :], in0=yt[0][:, t, :], scalar=gate[:, 0, t:t + 1], in1=h[:, t, :], op0=ALU.mult, op1=ALU.add))
                    dve.scalar_tensor_tensor(out=h[:, t, :], in0=yt[1][:, t, :], scalar=gate[:, 1, t:t + 1], in1=h[:, t, :],
                                             op0=ALU.mult, op1=ALU.add).then_inc(s_sum_ready, 1)


def kernel(**inputs):
    import numpy as np
    import concourse.bacc as _bacc
    from concourse.bass_utils import run_bass_kernel_spmd as _run

    a = {k: np.asarray(v) for k, v in inputs.items()}
    f32 = np.float32
    two = lambda w: np.ascontiguousarray(w.reshape(2, DC, -1).transpose(1, 0, 2))
    unit = np.zeros((1, NP1), f32)
    unit[0, NP1 - 1] = 1.0
    x = a["x"].reshape(B, 3, 16, 4, 16, 4).transpose(1, 3, 5, 0, 2, 4).reshape(48, B * NI)
    wb2 = a["L0_attn_Wb2"].reshape(R, H, 5)
    lay = {
        "xp1": np.concatenate([x, np.ones((1, B * NI), f32)], 0),
        "cwb": two(np.concatenate([a["L0_tok_conv_w"].reshape(D, 48), a["L0_tok_conv_b"][:, None]], 1)),
        "wtok": two(np.concatenate([a["L0_tok_q_w"], a["L0_tok_k_w"], a["L0_tok_v_w"]], 0).T),
        "btok": np.concatenate([a["L0_tok_q_b"], a["L0_tok_k_b"], a["L0_tok_v_b"]])[None],
        "unit": unit,
        "pjt": a["L0_tok_proj_w"].T,
        "pjb": a["L0_tok_proj_b"][None],
        "txt": a["txt"],
        "wq": two(np.concatenate([a["L0_attn_Wqkv"], a["L0_attn_Wb1"]], 1)),
        "lnw": a["L0_attn_ln_w"].reshape(2, DC).T,
        "lnb": a["L0_attn_ln_b"].reshape(2, DC).T,
        "bqkv": a["L0_attn_bqkv"][None],
        "wb2": np.concatenate([wb2[:, :, i] for i in (0, 2, 1, 3)], 1),
        "wp": two(a["L0_attn_Wproj"]),
        "mnw": np.tile(a["L0_attn_mn_w"], DC // DH)[:, None],
        "mnb": np.tile(a["L0_attn_mn_b"], DC // DH)[:, None],
        "bproj": a["L0_attn_bproj"][None],
        "temp": np.broadcast_to(a["L0_attn_temperature"][None], (P, 1)),
        "wr": two(a["L0_ffn_router_w"].T),
        "w1a": a["L0_ffn_w1"].transpose(2, 0, 1).reshape(D, E * FI)[0:P],
        "w1b": a["L0_ffn_w1"].transpose(2, 0, 1).reshape(D, E * FI)[P:D],
        "w2": a["L0_ffn_w2"].transpose(2, 0, 1).reshape(MC, P, E, D).transpose(1, 2, 0, 3).reshape(P, E * MC * D),
    }
    nc = _bacc.Bacc("TRN2", target_bir_lowering=False, num_devices=1)
    arrays = {f"in_{k}": np.ascontiguousarray(v) for k, v in lay.items()}
    aps = {k: nc.dram_tensor(f"in_{k}", arrays[f"in_{k}"].shape, F32, kind="ExternalInput").ap() for k in lay}
    x2_dram = nc.dram_tensor("x2_rows", (NTOK, 2 * D), F16, kind="Internal").ap()
    y_dram = nc.dram_tensor("y_rows", (2 * NTOK, D), F32, kind="Internal").ap()
    out = nc.dram_tensor("out_0", (B, CT * P, D), F32, kind="ExternalOutput").ap()
    build(nc, aps, x2_dram, y_dram, out)
    r = _run(nc, [arrays], core_ids=[0])
    return r.results[0]["out_0"]
```

```python
from contextlib import ExitStack
from math import log, prod

import concourse.bass as bass
from concourse import mybir

ALU = mybir.AluOpType
ACT = mybir.ActivationFunctionType
F32 = mybir.dt.float32
F16 = mybir.dt.float16
I32 = mybir.dt.int32
U32 = mybir.dt.uint32
AX_X = mybir.AxisListType.X

P = 128
B = 4
NI = 256
D = 192
DC = D // 2
KD = 96
NP1 = 3 * 4 * 4 + 1
CT = 3
T = B * CT
IT = NI // P
H = 12
DH = D // H
SLOT = 4 * DH
HG = P // SLOT
G = H // HG
GB = G // 2
VS = 64.0
FS = 16.0
VE = DH + 1
R = 128
E = 8
FI = 512
MC = FI // P
NS = T * 2 + E - 1
NSP = NS + 1
LEAD = 7
STEP = 8
LAG = 2
assert (NS - LEAD) % STEP == 0
WIN = STEP + LAG
WINDOWS = [0] + list(range(LEAD - LAG, NS - LAG, STEP))
assert WIN * 3 < 32 and LEAD <= WIN
NTOK = T * P
WS = 256.0
W1H, W1L = 0, FI
W1BH, W1BL = 2 * FI, 3 * FI
W2H = 4 * FI
W2L = W2H + MC * D
XW = W2L + MC * D
STG = 2048
EPS = 1e-5
PI = 3.141592653589793
RSQRT_MAGIC = float(0x5F3759DF)
NO_TOKEN = 100000.0

def build(nc, A, x2_dram, y_dram, out):
    with ExitStack() as ctx:
        def sb(name, shape, dt=F32):
            return ctx.enter_context(nc.sbuf_tensor(name, shape, dt))

        def sem(name):
            return ctx.enter_context(nc.semaphore(name))

        bank = [ctx.enter_context(nc.psum_tensor(f"bank{i}", [P, 512], F32)) for i in range(8)]

        def parts_of(name, *shapes):
            sizes = [prod(s[1:]) for s in shapes]
            whole = places.setdefault(name, sb(name, [P, max_words[name]]) if name not in places else None)
            views, at_ = [], 0
            for shape, n in zip(shapes, sizes):
                view = whole[0:shape[0], at_:at_ + n]
                names = "abc"[:len(shape) - 1]
                if len(names) > 1:
                    view = view.rearrange("p (" + " ".join(names) + ") -> p " + " ".join(names), **dict(zip(names, shape[1:])))
                views.append(view)
                at_ += n
            assert at_ <= max_words[name]
            return views

        places = {}
        max_words = {"first_place": 2 * CT * D, "second_place": 2 * CT * D, "fourth_place": 2 * D, "third_place": 2 * (D + 2 * D + 3 * R + D)}
        wtok, btok, pjt = parts_of("first_place", (DC, 2, 3 * KD), (1, 3 * KD), (KD, D))
        (o,) = parts_of("first_place", (P, 2, CT * H * DH))
        o = o.rearrange("p b (h e) -> p b h e", e=DH)
        (bias_half,) = parts_of("first_place", (1, 3 * D))
        bias_half = bias_half.bitcast(F16).rearrange("p (v n) -> p v n", v=2)
        bq, pr = parts_of("second_place", (1, 3 * D), (P, T, 4 * H))
        (x2,) = parts_of("second_place", (P, 2, CT * D))
        x2 = x2.rearrange("p b (c d) -> p b c d", d=D)
        xn, eb, th, g1, g1T, xs = parts_of("third_place", (P, 2, D), (P, 2, 2 * D), (P, 2, R), (P, 2, R), (P, 2, P), (P, 2 * D))
        xs = xs.bitcast(F16).rearrange("p (b n) -> p b n", b=2)
        osq, x2T, keep, ls, ex, pb, tmp, selsum, tot, inc = parts_of(
            "third_place", (P, CT * H, DH), (DC, CT, 2 * P), (P, E, T), (P, T, E), (P, T, E), (P, T, E), (P, T, E), (P, T, E), (P, E, T), (P, E, T))
        x2T = x2T.rearrange("p b (c n) -> p b c n", n=P)
        wv, pjb = parts_of("fourth_place", (NP1, D), (1, D))
        (passed,) = parts_of("fourth_place", (1, NSP, E))
        ident = sb("ident", [P, P])
        ident16 = sb("ident16", [P, P], F16)
        causal = sb("causal", [P, P])
        before = sb("before", [P, P])
        ones = sb("ones", [P, P])
        ones16 = sb("ones16", [1, P], F16)
        headmask = sb("headmask", [P, G, HG, VE])
        ln_fs = sb("ln_fs", [P, 1])
        qkT = sb("qkT", [P, 2, G * P])
        qT, kT = (qkT[:, i, :].bitcast(F16).rearrange("p (b n) -> p b n", b=2) for i in range(2))
        xp1 = qkT[:].rearrange("p a n -> p (a n)")[0:NP1, 0:B * NI]
        early = sb("early", [P, 2 * STG])
        stage = early[:].rearrange("p (b n) -> p b n", b=2)
        atm = sb("atm", [P, HG, G, P])
        cwb = sb("cwb", [DC, 2, NP1])
        unit = sb("unit", [1, NP1])
        axt = sb("axt", [KD, 3, NP1])
        mt = sb("mt", [NP1, NP1])
        at_half = sb("at_half", [P, 2, HG, G, P], F16)
        wq = at_half[:].rearrange("p v i g l -> p (v i g l)").bitcast(F32)[:, 0:2 * (3 * D + R)].rearrange("p (c n) -> p c n", c=2)
        gsb = atm[:].rearrange("p i g l -> p (i g l)")[0:NP1, 0:B * NI]
        prob = early[:, 0:2 * IT * NI].rearrange("p (b n m) -> p b n m", b=2, n=IT)
        probT = early[:, 2 * IT * NI:4 * IT * NI].rearrange("p (b n m) -> p b n m", b=2, n=IT)
        vs = early[:, 4 * IT * NI:4 * IT * NI + B * IT * D].rearrange("p (t d) -> p t d", d=D)
        nmax = sb("nmax", [P, B * IT])
        nbias = sb("nbias", [P, B * IT])
        rsum = sb("rsum", [P, B * IT])
        rinv = sb("rinv", [P, B * IT])
        h = sb("h", [P, T, D])
        w_half = sb("w_half", [P, 2, 2, 3 * D + R], F16)
        lnw = sb("lnw", [P, 2])
        lnb = sb("lnb", [P, 2])
        wb2 = sb("wb2", [R, 4 * H])
        wp = sb("wp", [DC + 1, 2, D])
        mnw = sb("mnw", [DC, 1])
        mnb = sb("mnb", [DC, 1])
        bp = sb("bp", [DC + 1, D])
        temp = sb("temp", [P, 1])
        htemp = sb("htemp", [P, 1])
        stat = sb("stat", [P, T, 6])
        mv = sb("mv", [P, T, 2])
        nwt = sb("nwt", [P, 6, CT * H])
        r1 = sb("r1", [P, T])
        r12 = sb("r12", [P, T])
        nmr = sb("nmr", [P, T])
        sh = sb("sh", [P, T])
        xT = sb("xT", [P, 2, 3, P], F16)
        qk = sb("qk", [P, T, 2 * H, 4, DH], F16)
        ga = sb("ga", [P, T, 2 * H])
        gb = sb("gb", [P, T, 2 * H])
        gc = sb("gc", [P, T, H])
        gd = sb("gd", [P, T, H])
        gate1 = sb("gate1", [P, T, H])
        v32 = sb("v32", [P, T * H, DH])
        vg = sb("vg", [P, T * H, 2, VE], F16)
        state = sb("state", [P, G * HG * VE])
        st_half = sb("st_half", [P, 2, 2, G * HG * VE], F16)
        rden = sb("rden", [P, 2, H])
        osum = sb("osum", [P, CT * H])
        oT = sb("oT", [DC + 1, CT, 2, P])
        xr = sb("xr", [P, 2 * CT, 2 * D], F16)
        wr = sb("wr", [DC, 2, E])
        lg = sb("lg", [P, T, E])
        wx = sb("wx", [P, E * XW], F16)
        by_expert = wx[:].rearrange("p (e c) -> p e c", c=XW)
        iota_e = sb("iota_e", [P, E])
        iota_p = sb("iota_p", [P, P])
        iota_p16 = sb("iota_p16", [P, P], F16)
        row1 = sb("row1", [P, 1])
        choice1 = sb("choice1", [P, 2 * T])
        sel = sb("sel", [P, 2, T, E])
        small = sb("small", [P, 10, T])
        cnt = sb("cnt", [P, 4, E])
        cnti = sb("cnti", [P, E], I32)
        slot = sb("slot", [P, 2, T])
        sloti = sb("sloti", [P, 3, 2 * T], I32)
        slotf = sb("slotf", [P, 2, 2 * T])
        late = qk[:].rearrange("p t h s e -> p (t h s e)").bitcast(F32)
        at = [0]

        def carve(words):
            at[0] += words
            return late[:, at[0] - words:at[0]]

        cola = carve(T * P).bitcast(F16).rearrange("p (n c) -> p n c", c=P)
        cole = carve(2 * T * NSP).rearrange("p (n c) -> p n c", c=NSP)
        colb = carve(2 * T * NSP).bitcast(F16).rearrange("p (n v c) -> p n v c", v=2, c=NSP)
        src = sb("src", [P, 4, NSP])
        dst_row = sb("dst_row", [P, NSP], U32)
        tok_row = sb("tok_row", [P, NSP], U32)
        expf = sb("expf", [1, NSP])
        pow8 = sb("pow8", [1, WIN])
        packf = sb("packf", [1, len(WINDOWS), WIN])
        packs = sb("packs", [1, len(WINDOWS), 2])
        packi = sb("packi", [1, len(WINDOWS), 2], I32)
        expert = sb("expert", [1, len(WINDOWS)], I32)
        imp = sb("imp", [P, E])
        gate = sb("gate", [P, 2, T])
        xg = carve(4 * D).bitcast(F16).rearrange("p (k c) -> p k c", k=4)
        xe = carve(3 * P).bitcast(F16).rearrange("p (k c) -> p k c", k=2)
        act32 = carve(2 * FI).rearrange("p (k c) -> p k c", k=2)
        acth = carve(FI).bitcast(F16).rearrange("p (k c) -> p k c", k=2)
        actl = carve(FI).bitcast(F16).rearrange("p (k c) -> p k c", k=2)
        actT = carve(2 * FI).bitcast(F16).rearrange("p (k v n) -> p k v n", k=2, v=2)
        ye = carve(4 * D).rearrange("p (k c) -> p k c", k=4)

        s_tok_loaded = sem("tok_loaded")
        s_img_loaded = sem("img_loaded")
        s_txt_loaded = sem("txt_loaded")
        s_attn_loaded = sem("attn_loaded")
        s_const_ready = sem("const_ready")
        s_pool_step = sem("pool_step")
        s_axt_mm = sem("axt_mm")
        s_axt_ready = sem("axt_ready")
        s_setup_mm = sem("setup_mm")
        s_mt_ready = sem("mt_ready")
        s_wv_ready = sem("wv_ready")
        s_lnb_mm = sem("lnb_mm")
        s_mnb_mm = sem("mnb_mm")
        s_wq_ready = sem("wq_ready")
        s_wp_ready = sem("wp_ready")
        s_step = sem("step")
        s_ones_ready = sem("ones_ready")
        s_g_mm = sem("g_mm")
        s_g_ready = sem("g_ready")
        s_vp_mm = sem("vp_mm")
        s_vp_ready = sem("vp_ready")
        s_score_mm = sem("score_mm")
        s_nbias_ready = sem("nbias_ready")
        s_prob_ready = sem("prob_ready")
        s_rinv_ready = sem("rinv_ready")
        s_pT_mm = sem("pT_mm")
        s_pT_ready = sem("pT_ready")
        s_himg_mm = sem("himg_mm")
        s_himg_ready = sem("himg_ready")
        s_ln1_ready = sem("ln1_ready")
        s_wqhigh_ready = sem("wqhigh_ready")
        s_wqlow_ready = sem("wqlow_ready")
        s_xn_ready = sem("xn_ready")
        s_xhigh_ready = sem("xhigh_ready")
        s_xlow_ready = sem("xlow_ready")
        s_xT_mm = sem("xT_mm")
        s_xT_ready = sem("xT_ready")
        s_qk_mm = sem("qk_mm")
        s_vb_mm = sem("vb_mm")
        s_exp_ready = sem("exp_ready")
        s_f32_ready = sem("f32_ready")
        s_fhigh_ready = sem("fhigh_ready")
        s_feat_ready = sem("feat_ready")
        s_tanh_ready = sem("tanh_ready")
        s_v_ready = sem("v_ready")
        s_g1_ready = sem("g1_ready")
        s_gT_mm = sem("gT_mm")
        s_gT_ready = sem("gT_ready")
        s_pr_mm = sem("pr_mm")
        s_pr_ready = sem("pr_ready")
        s_ga_ready = sem("ga_ready")
        s_dph_ready = sem("dph_ready")
        s_sin_ready = sem("sin_ready")
        s_cos_ready = sem("cos_ready")
        s_int_ready = sem("int_ready")
        s_gate_tanh = sem("gate_tanh")
        s_gated = sem("gated")
        s_vhigh_ready = sem("vhigh_ready")
        s_vg_ready = sem("vg_ready")
        s_t0_full = sem("t0_full")
        s_t0_free = sem("t0_free")
        s_t1_full = sem("t1_full")
        s_t1_free = sem("t1_free")
        s_at_mm = sem("at_mm")
        s_mask_done = sem("mask_done")
        s_athigh_ready = sem("athigh_ready")
        s_atlow_ready = sem("atlow_ready")
        s_state_mm = sem("state_mm")
        s_state32 = sem("state32")
        s_sthigh_ready = sem("sthigh_ready")
        s_state_ready = sem("state_ready")
        s_num_mm = sem("num_mm")
        s_o_ready = sem("o_ready")
        s_osq_ready = sem("osq_ready")
        s_ohat_ready = sem("ohat_ready")
        s_x2_ready = sem("x2_ready")
        s_last_oT_mm = sem("last_oT_mm")
        s_last_oT = sem("last_oT")
        s_last_proj = sem("last_proj")
        s_last_xT_mm = sem("last_xT_mm")
        s_last_xT = sem("last_xT")
        s_last_route = sem("last_route")
        s_last_logits = sem("last_logits")
        s_xhi_ready = sem("xhi_ready")
        s_xlo_ready = sem("xlo_ready")
        s_x2_stored = [sem(f"x2_stored{i}") for i in range(2)]
        s_w_loaded = [sem(f"w_loaded{i}") for i in range(2)]
        s_w_scaled = sem("w_scaled")
        s_w_high = sem("w_high")
        s_w_low = sem("w_low")
        s_iota_ready = sem("iota_ready")
        s_ls_ready = sem("ls_ready")
        s_ex_ready = sem("ex_ready")
        s_pb_ready = sem("pb_ready")
        s_sel_ready = sem("sel_ready")
        s_rank_mm = sem("rank_mm")
        s_imp_mm = sem("imp_mm")
        s_onehot_ready = sem("onehot_ready")
        s_src_mm = sem("src_mm")
        s_rows_ready = sem("rows_ready")
        s_expert_ready = sem("expert_ready")
        s_xg_clear = sem("xg_clear")
        s_gathered = [sem(f"gathered{i}") for i in range(4)]
        s_scattered = [sem(f"scattered{i}") for i in range(4)]
        s_xe_mm = sem("xe_mm")
        s_xe_ready = sem("xe_ready")
        s_up_mm = sem("up_mm")
        s_act_ready = sem("act_ready")
        s_high_ready = sem("high_ready")
        s_low_ready = sem("low_ready")
        s_actT_mm = sem("actT_mm")
        s_actT_high = sem("actT_high")
        s_actT_low = sem("actT_low")
        s_down_mm = sem("down_mm")
        s_y_ready = sem("y_ready")
        s_y_loaded = [sem(f"y_loaded{i}") for i in range(4)]
        s_sum_ready = sem("sum_ready")
        s_out_done = sem("out_done")

        PT, XT = T - CT, T - 2 * CT
        misc = [("tr", 0), ("tr", 1)]
        for t in range(T + 1):
            misc += [("o", t - 4)] * (0 <= t - 4 < PT) + [("x", t - 7)] * (0 <= t - 7 < XT) + [("tr", t + 2)] * (t + 2 < T)
        use = {k: n for n, k in enumerate(misc)}

        parts = {"w1a": (FI, P, W1H, W1L), "w1b": (FI, D - P, W1BH, W1BL), "w2": (MC * D, P, W2H, W2L)}
        jobs = [(k, e0) for k in parts for e0 in range(0, E, STG // parts[k][0])]
        loads = [sum(2 if k == "w1b" else 1 for k, _ in jobs[n % 2:n + 1:2]) for n in range(len(jobs))]

        def staged(n, rows=P):
            kind, e0 = jobs[n]
            width, low_rows, high, low = parts[kind]
            ne = STG // width
            return (stage[0:rows, n % 2, 0:ne * width].rearrange("p (e c) -> p e c", c=width),
                    by_expert[0:rows, e0:e0 + ne, high:high + width], by_expert[0:rows, e0:e0 + ne, low:low + width])

        def twice(t, n):
            return eb[:, t % 2, n * D:(n + 1) * D].rearrange("p (h e) -> p h e", e=DH).unsqueeze(2).broadcast_to([P, H, 2, DH])

        def half_of(t, n, low):
            heads = qk[:, t, n * H:(n + 1) * H]
            if n == 0:
                return heads[:, :, 2 * low:2 * low + 2, :]
            return heads.rearrange("p h (a b) e -> p h a b e", b=2)[:, :, :, low, :]

        yt = [v[:, 0:T * D].rearrange("p (t d) -> p t d", t=T) for v in (v32[:].rearrange("p t e -> p (t e)"), late)]

        block = ctx.enter_context(nc.Block())

        @block.sync
        def _(sp):
            for dst, src in ((cwb, A["cwb"]), (wtok, A["wtok"]), (btok, A["btok"]), (unit, A["unit"]), (pjt, A["pjt"]), (pjb, A["pjb"])):
                sp.dma_start(dst[:], src).then_inc(s_tok_loaded, 16)
            sp.dma_start(xp1, A["xp1"]).then_inc(s_img_loaded, 16)
            for b in range(B):
                sp.dma_start(h[:, CT * b + IT, :], A["txt"][b]).then_inc(s_txt_loaded, 16)
            for dst, src_ in ((wq, A["wq"]), (lnw[:], A["lnw"]), (lnb[:], A["lnb"]), (bq, A["bqkv"]),
                             (wb2[:], A["wb2"]), (wp[0:DC, :, :], A["wp"]), (mnw[:], A["mnw"]), (mnb[:], A["mnb"]),
                             (bp[DC:DC + 1, :], A["bproj"]), (temp[:], A["temp"]), (wr[:], A["wr"])):
                sp.dma_start(dst, src_).then_inc(s_attn_loaded, 16)
            sp.wait_ge(s_himg_mm, B)
            for n, (kind, e0) in enumerate(jobs):
                if n >= 2:
                    sp.wait_ge(s_w_low, n - 1)
                width = parts[kind][0]
                cols = STG // width * width
                w = A[kind][:, e0 * width:e0 * width + cols]
                if kind == "w1b":
                    for r in range(2):
                        sp.dma_start(stage[r * 64:(r + 1) * 64, n % 2, 0:cols], w).then_inc(s_w_loaded[n % 2], 16)
                else:
                    sp.dma_start(stage[:, n % 2, 0:cols], w).then_inc(s_w_loaded[n % 2], 16)
            for t in range(T):
                sp.wait_ge(s_xhi_ready, 2 * (t + 1))
                sp.wait_ge(s_xlo_ready, 2 * (t + 1))
                sp.dma_start(x2_dram[t * P:(t + 1) * P, :], xr[:, t % (2 * CT), :]).then_inc(s_x2_stored[t // CT % 2], 16)
            for k in range(4):
                sp.wait_ge(s_scattered[k], 16 * len(range(k, NS, 4)))
            for b in range(B):
                for k in range(2):
                    r0 = k * NTOK + b * CT * P
                    sp.dma_start(yt[k][:, b * CT:(b + 1) * CT, :], y_dram[r0:r0 + CT * P, :].rearrange("(c p) d -> p c d", p=P)).then_inc(s_y_loaded[b], 16)
            for b in range(B):
                sp.wait_ge(s_sum_ready, (b + 1) * CT)
                sp.dma_start(out[b].rearrange("(c p) d -> p c d", p=P), h[:, b * CT:(b + 1) * CT, :]).then_inc(s_out_done, 16)
            sp.wait_ge(s_out_done, 16 * B)

        @block.gpsimd
        def _(pool):
            step = [0]

            def link(ins):
                step[0] += 1
                ins.then_inc(s_pool_step, 1)
                pool.wait_ge(s_pool_step, step[0])

            pool.memset(ident[:], 0.0).then_inc(s_pool_step, 1)
            pool.memset(ident16[:], 0.0).then_inc(s_pool_step, 1)
            pool.memset(causal[:], FS ** -2).then_inc(s_pool_step, 1)
            pool.memset(before[:], 1.0).then_inc(s_pool_step, 1)
            pool.memset(headmask[:], FS ** -2).then_inc(s_pool_step, 1)
            pool.memset(ln_fs[:], log(FS)).then_inc(s_pool_step, 1)
            step[0] = 6
            pool.wait_ge(s_pool_step, 6)
            for m in (ident, ident16):
                pool.affine_select(out=m[:], in_=m[:], compare_op=ALU.not_equal, fill=1.0, base=0,
                                   pattern=[[-1, P]], channel_multiplier=1).then_inc(s_const_ready, 1)
            pool.affine_select(out=causal[:], in_=causal[:], compare_op=ALU.is_ge, fill=0.0, base=0,
                               pattern=[[1, P]], channel_multiplier=-1).then_inc(s_const_ready, 1)
            pool.affine_select(out=before[:], in_=before[:], compare_op=ALU.is_ge, fill=0.0, base=-1,
                               pattern=[[1, P]], channel_multiplier=-1).then_inc(s_const_ready, 1)
            link(pool.affine_select(out=headmask[:], in_=headmask[:], compare_op=ALU.is_ge, fill=0.0, base=0,
                                    pattern=[[0, G], [-SLOT, HG], [0, VE]], channel_multiplier=1))
            pool.affine_select(out=headmask[:], in_=headmask[:], compare_op=ALU.is_ge, fill=0.0, base=SLOT - 1,
                               pattern=[[0, G], [SLOT, HG], [0, VE]], channel_multiplier=-1).then_inc(s_const_ready, 1)

            for dst, pattern, base, mul in ((iota_e, [[1, E]], -E, 0), (iota_p, [[1, P]], 0, 0), (iota_p16, [[1, P]], 0, 0),
                                            (row1, [[0, 1]], 1, 1), (choice1, [[1, 2 * T]], 1, 0)):
                pool.iota(dst[:], pattern, base=base, channel_multiplier=mul, allow_small_or_imprecise_dtypes=True).then_inc(s_iota_ready, 1)
            for n in range(len(jobs)):
                w, high, low = staged(n, parts[jobs[n][0]][1])
                pool.wait_ge(s_w_high, n + 1)
                pool.tensor_tensor(low, w, high, ALU.subtract).then_inc(s_w_low, 1)

            def gather(i):
                if i >= 4:
                    pool.wait_ge(s_xe_mm, i - 3)
                pool.indirect_dma_start(xg[:, i % 4, :], None, x2_dram, bass.IndirectOffsetOnAxis(ap=tok_row[:, i:i + 1], axis=0),
                                        bounds_check=NTOK - 1, oob_is_err=False).then_inc(s_gathered[i % 4], 16)

            def scatter(i):
                pool.wait_ge(s_y_ready, i + 1)
                pool.indirect_dma_start(y_dram, bass.IndirectOffsetOnAxis(ap=dst_row[:, i:i + 1], axis=0), ye[:, i % 4, :], None,
                                        bounds_check=2 * NTOK - 1, oob_is_err=False).then_inc(s_scattered[i % 4], 16)

            pool.wait_ge(s_rank_mm, 1)
            pool.memset(xg, 0.0).then_inc(s_xg_clear, 1)
            pool.wait_ge(s_xg_clear, 1)
            for k in range(2):
                pool.wait_ge(s_x2_stored[k], 16 * T // 2)
            pool.wait_ge(s_rows_ready, 2)
            for i in range(4):
                gather(i)
            for i in range(NS + 3):
                if i + 4 < NSP:
                    gather(i + 4)
                if i >= 3:
                    scatter(i - 3)

        @block.tensor
        def _(pe):
            pe.wait_ge(s_tok_loaded, 96)
            for i in range(3):
                w = slice(i * KD, (i + 1) * KD)
                o_ = bank[0][0:KD, i * NP1:(i + 1) * NP1]
                pe.matmul(o_, wtok[:, 0, w], cwb[:, 0, :], start=True, stop=False)
                pe.matmul(o_, wtok[:, 1, w], cwb[:, 1, :], start=False, stop=False)
                mm = pe.matmul(o_, btok[:, w], unit[:], start=False, stop=True)
            mm.then_inc(s_axt_mm, 1)
            pe.wait_ge(s_axt_ready, 1)
            pe.matmul(bank[1][0:NP1, 0:NP1], axt[:, 1, :], axt[:, 0, :], start=True, stop=True).then_inc(s_setup_mm, 1)
            pe.matmul(bank[2][0:NP1, 0:D], axt[:, 2, :], pjt, start=True, stop=False)
            pe.matmul(bank[2][0:NP1, 0:D], unit[:], pjb, start=False, stop=True).then_inc(s_setup_mm, 1)
            pe.wait_ge(s_img_loaded, 16)
            pe.wait_ge(s_mt_ready, 1)
            for i in range(2):
                if i:
                    pe.wait_ge(s_g_ready, i)
                pe.matmul(bank[7][0:NP1, :], mt[:], xp1[:, i * 512:(i + 1) * 512], start=True, stop=True).then_inc(s_g_mm, 1)

            def scores(b):
                pe.wait_ge(s_g_ready, b // 2 + 1)
                if b >= 2:
                    pe.wait_ge(s_prob_ready, IT * (b - 1))
                else:
                    pe.wait_ge(s_axt_ready, 1)
                    pe.wait_ge(s_mt_ready, 1)
                for n in range(IT):
                    q0 = b * NI + n * P
                    mm = pe.matmul(bank[b % 2][:, n * NI:(n + 1) * NI], xp1[:, q0:q0 + P], gsb[:, b * NI:(b + 1) * NI], start=True, stop=True)
                mm.then_inc(s_score_mm, 1)

            def values(i):
                pe.wait_ge(s_wv_ready, 1)
                if i >= 2:
                    pe.wait_ge(s_vp_ready, i - 1)
                for n in range(IT):
                    m0 = (i * IT + n) * P
                    mm = pe.matmul(bank[5 + i % 2][:, n * D:(n + 1) * D], xp1[:, m0:m0 + P], wv, start=True, stop=True)
                mm.then_inc(s_vp_mm, 1)

            def prob_t(b):
                pe.wait_ge(s_prob_ready, IT * (b + 1))
                if b == 0:
                    pe.wait_ge(s_const_ready, 5)
                    pe.wait_ge(s_wv_ready, 1)
                if b >= 2:
                    pe.wait_ge(s_pT_ready, b - 1)
                for n in range(IT):
                    for j in range(IT):
                        mm = pe.transpose(bank[2 + b % 2][:, j * NI + n * P:j * NI + (n + 1) * P], prob[:, b % 2, n, j * P:(j + 1) * P], ident[:])
                mm.then_inc(s_pT_mm, 1)

            def himg(b):
                pe.wait_ge(s_pT_ready, b + 1)
                if b == 0:
                    pe.wait_ge(s_vp_ready, B)
                if b >= 2:
                    pe.wait_ge(s_himg_ready, IT * (b - 1))
                for n in range(IT):
                    for j in range(IT):
                        mm = pe.matmul(bank[5 + b % 2][:, n * D:(n + 1) * D], probT[:, b % 2, j, n * P:(n + 1) * P], vs[:, b * IT + j, :],
                                       start=(j == 0), stop=(j == IT - 1))
                mm.then_inc(s_himg_mm, 1)

            scores(0)
            scores(1)
            for i in range(B):
                values(i)
            pe.wait_ge(s_attn_loaded, 16 * 11)
            pe.wait_ge(s_g_ready, 2)
            for lo, hi, bk in ((0, 512, 4), (512, 3 * D, 7)):
                for c in range(2):
                    rows = P if c == 0 else D - P
                    mm = pe.matmul(bank[bk][0:1, 0:hi - lo], lnb[0:rows, c:c + 1], wq[0:rows, c, lo:hi], start=(c == 0), stop=(c == 1))
            mm.then_inc(s_lnb_mm, 1)
            for c in range(2):
                mm = pe.matmul(bank[3][DC:DC + 1, 0:D], mnb[:, 0:1], wp[0:DC, c, :], start=(c == 0), stop=(c == 1))
            mm.then_inc(s_mnb_mm, 1)
            prob_t(0)
            himg(0)
            for b in range(1, B):
                if b + 1 < B:
                    scores(b + 1)
                if b == 1:
                    pe.wait_ge(s_wp_ready, 1)
                prob_t(b)
                himg(b)

            def x_t(t):
                pe.wait_ge(s_xlow_ready, 2 * (t + 1))
                if t >= 2:
                    pe.wait_ge(s_xT_ready, t - 1)
                else:
                    pe.wait_ge(s_prob_ready, B * IT)
                ps = bank[t % 2][:, 0:3 * P // 2].bitcast(F16)
                for j in range(3):
                    mm = pe.transpose(ps[:, j * P:(j + 1) * P], xs[:, t % 2, j * P:(j + 1) * P], ident16[:])
                mm.then_inc(s_xT_mm, 1)

            def projected(out_, t, c0, c1, biased):
                x_, w = xT[:, t % 2], w_half[:, :, :, c0:c1]
                pe.matmul(out_, x_[:, 0], w[:, 0, 0], start=True, stop=False)
                pe.matmul(out_, x_[:, 1], w[:, 0, 0], start=False, stop=False)
                pe.matmul(out_, x_[:, 0], w[:, 1, 0], start=False, stop=False)
                pe.matmul(out_, x_[:, 2], w[:, 0, 1], start=False, stop=False)
                for v in range(2):
                    pe.matmul(out_[:, 0:biased], ones16[:], bias_half[:, v, c0:c0 + biased], start=False, stop=False)
                return pe.matmul(out_, x_[0:D - P, 2], w[0:D - P, 1, 1], start=False, stop=True)

            def qkv(t):
                pe.wait_ge(s_xT_ready, t + 1)
                if t == 0:
                    pe.wait_ge(s_wqlow_ready, 3)
                    pe.wait_ge(s_ones_ready, 3)
                    pe.wait_ge(s_pT_ready, B)
                    pe.wait_ge(s_himg_ready, B * IT)
                if t >= 2:
                    pe.wait_ge(s_f32_ready, t - 1)
                projected(bank[2 + t % 2][:, 0:2 * D], t, 0, 2 * D, 2 * D).then_inc(s_qk_mm, 1)
                if t >= 2:
                    pe.wait_ge(s_v_ready, t - 1)
                    pe.wait_ge(s_g1_ready, t - 1)
                projected(bank[4 + t % 2][:, 0:D + R], t, 2 * D, 3 * D + R, D).then_inc(s_vb_mm, 1)

            def hidden_t(t):
                pe.wait_ge(s_g1_ready, t + 1)
                if t >= 1:
                    pe.wait_ge(s_gT_ready, t)
                pe.transpose(bank[6][:, 0:P], g1[:, t % 2, :], ident[:]).then_inc(s_gT_mm, 1)

            def params(t):
                pe.wait_ge(s_gT_ready, t + 1)
                if t >= 1:
                    pe.wait_ge(s_pr_ready, t)
                pe.matmul(bank[7][:, 0:4 * H], g1T[:, t % 2, :], wb2[:], start=True, stop=True).then_inc(s_pr_mm, 1)

            x_t(0)
            for t in range(T + 2):
                if t + 1 < T:
                    x_t(t + 1)
                if t < T:
                    qkv(t)
                if 1 <= t <= T:
                    hidden_t(t - 1)
                if t >= 2:
                    params(t - 2)

            def take(u):
                if u == 0:
                    pe.wait_ge(s_xT_ready, T)
                else:
                    pe.wait_ge(s_t0_free, u)
                    pe.wait_ge(s_t1_free, u)

            def heads_t(t):
                u = use["tr", t]
                take(u)
                pe.wait_ge(s_feat_ready, 2 * (t + 1))
                for half, full in ((0, s_t0_full), (1, s_t1_full)):
                    for g in range(G):
                        h0 = half * H + g * HG
                        mm = pe.transpose(bank[half][:, 0:G * P // 2].bitcast(F16)[:, g * P:(g + 1) * P], qk[:, t, h0:h0 + HG].rearrange("p h s e -> p (h s e)"), ident16[:])
                    mm.then_inc(full, 1)

            def scores_of(i, n):
                return bank[2 + 2 * i + n]

            def qk_products(t):
                pe.wait_ge(s_t0_free, use["tr", t] + 1)
                pe.wait_ge(s_t1_free, use["tr", t] + 1)
                if t:
                    pe.wait_ge(s_mask_done, 4 * t)
                else:
                    pe.wait_ge(s_f32_ready, T)
                    pe.wait_ge(s_g1_ready, T)
                    pe.wait_ge(s_v_ready, T)
                for g in range(G):
                    for i in range(HG):
                        r = slice(SLOT * i, SLOT * (i + 1))
                        mm = pe.matmul(scores_of(i, g // GB)[:, g % GB * P:(g % GB + 1) * P], kT[r, t % 2, g * P:(g + 1) * P], qT[r, t % 2, g * P:(g + 1) * P],
                                       start=True, stop=True, tile_position=(SLOT * i, 0))
                mm.then_inc(s_at_mm, 1)

            def state_step(t):
                b, c = divmod(t, CT)
                pe.wait_ge(s_vg_ready, b + 1)
                if t == 0:
                    pe.wait_ge(s_pr_ready, T)
                else:
                    pe.wait_ge(s_state32, b * 2 + c)
                for g in range(G):
                    for v in range(2):
                        mm = pe.matmul(bank[7][:, g * HG * VE:(g + 1) * HG * VE],
                                       qk[:, t, H + g * HG:H + (g + 1) * HG].rearrange("p h s e -> p (h s e)"),
                                       vg[:, t * H + g * HG:t * H + (g + 1) * HG, v, :],
                                       start=(c == 0 and g == 0 and v == 0), stop=(c == 1 and g == G - 1 and v == 1), skip_group_check=True)
                mm.then_inc(s_state_mm, 1)

            def numerators(t):
                b, c = divmod(t, CT)
                if t == 0:
                    pe.wait_ge(s_gT_ready, T)
                else:
                    pe.wait_ge(s_o_ready, t)
                if c:
                    pe.wait_ge(s_state_ready, 2 * b + c)
                    for g in range(G):
                        w = slice(g * HG * VE, (g + 1) * HG * VE)
                        for v in range(2):
                            pe.matmul(bank[6][:, w], qT[:, t % 2, g * P:(g + 1) * P], st_half[:, (t - 1) % 2, v, w],
                                      start=(g == 0 and v == 0), stop=False, skip_group_check=True)
                pe.wait_ge(s_atlow_ready, 4 * (t + 1))
                for hh in range(H):
                    g, i = divmod(hh, HG)
                    for a_, v in ((0, 0), (0, 1), (1, 0)):
                        mm = pe.matmul(bank[6][:, hh * VE:(hh + 1) * VE], at_half[:, a_, i, g, :], vg[:, t * H + hh, v, :],
                                       start=(c == 0 and hh == 0 and a_ == 0 and v == 0), stop=(hh == H - 1 and a_ == 1), skip_group_check=True)
                mm.then_inc(s_num_mm, 1)

            def outputs_t(t):
                b, c = divmod(t, CT)
                u = use["o", t]
                take(u)
                pe.wait_ge(s_ohat_ready, b + 1)
                for j in range(2):
                    mm = pe.transpose(bank[0][0:DC, j * P:(j + 1) * P],
                                      o[:, b % 2, c * H:(c + 1) * H, :].rearrange("p h e -> p (h e)")[:, j * DC:(j + 1) * DC], ident[:])
                mm.then_inc(s_t0_full, 1)

            def project(t):
                u = use["o", t]
                pe.wait_ge(s_t0_free, u + 1)
                if t == 0:
                    pe.wait_ge(s_wp_ready, 3)
                for j in range(2):
                    mm = pe.matmul(bank[1][:, 0:D], oT[0:DC + j, u % 2, j, :], wp[0:DC + j, j, :], start=(j == 0), stop=(j == 1))
                mm.then_inc(s_t1_full, 1)

            def route(t):
                b, c = divmod(t, CT)
                u = use["x", t]
                take(u)
                pe.wait_ge(s_x2_ready, t + 1)
                for j in range(2):
                    mm = pe.transpose(bank[0][0:DC, j * P:(j + 1) * P], x2[:, b % 2, c, j * DC:(j + 1) * DC], ident[:])
                mm.then_inc(s_t0_full, 1)
                pe.wait_ge(s_t0_free, u + 1)
                for j in range(2):
                    mm = pe.matmul(bank[1][:, 0:E], x2T[:, t % 2, j, :], wr[:, j, :], start=(j == 0), stop=(j == 1))
                mm.then_inc(s_t1_full, 1)

            heads_t(0)
            qk_products(0)
            heads_t(1)
            state_step(0)
            for t in range(T + 1):
                if t < T:
                    numerators(t)
                if 0 <= t - 4 < PT:
                    outputs_t(t - 4)
                if t + 1 < T:
                    qk_products(t + 1)
                if 0 <= t - 4 < PT:
                    project(t - 4)
                if t + 1 < T and (t + 1) % CT < 2:
                    state_step(t + 1)
                if 0 <= t - 7 < XT:
                    route(t - 7)
                if t + 2 < T:
                    heads_t(t + 2)

            def last_route(b):
                pe.wait_ge(s_x2_ready, (b + 1) * CT)
                n = 2 * (b - B + 2)
                if n == 0:
                    pe.wait_ge(s_o_ready, T)
                    pe.wait_ge(s_state32, 2 * B)
                b0 = 6 if n == 0 else 2
                for i in range(CT):
                    for j in range(2):
                        c0 = i % 2 * 2 * P + j * P
                        mm = pe.transpose(bank[b0 + i // 2][0:DC, c0:c0 + P], x2[:, b % 2, i, j * DC:(j + 1) * DC], ident[:])
                    if i:
                        mm.then_inc(s_last_xT_mm, 1)
                pe.wait_ge(s_last_xT, n + 2)
                for i in range(CT):
                    for j in range(2):
                        mm = pe.matmul(bank[n // 2][:, i * E:(i + 1) * E], x2T[:, i, j, :], wr[:, j, :], start=(j == 0), stop=(j == 1))
                mm.then_inc(s_last_route, 1)

            pe.wait_ge(s_ohat_ready, B)
            pe.wait_ge(s_mask_done, 4 * T)
            for i in range(CT):
                for j in range(2):
                    c0 = i % 2 * 2 * P + j * P
                    mm = pe.transpose(bank[2 + i // 2][0:DC, c0:c0 + P],
                                      o[:, (B - 1) % 2, i * H:(i + 1) * H, :].rearrange("p h e -> p (h e)")[:, j * DC:(j + 1) * DC], ident[:])
                if i:
                    mm.then_inc(s_last_oT_mm, 1)
            for i in range(CT):
                pe.wait_ge(s_last_oT, 1 + i // 2)
                for j in range(2):
                    mm = pe.matmul(bank[4 + i // 2][:, i % 2 * D:(i % 2 + 1) * D], oT[0:DC + j, i, j, :], wp[0:DC + j, j, :], start=(j == 0), stop=(j == 1))
                if i:
                    mm.then_inc(s_last_proj, 1)
            pe.wait_ge(s_t0_free, len(misc))
            pe.wait_ge(s_t1_free, len(misc))
            last_route(B - 2)
            last_route(B - 1)

            pe.wait_ge(s_sel_ready, 1)
            pe.wait_ge(s_ones_ready, 1)
            mv_ = selsum.rearrange("p t e -> p (t e)")
            pe.matmul(bank[0][:, 0:T * E], before[:], mv_, start=True, stop=True)
            pe.matmul(bank[0][:, T * E:2 * T * E], ones[:], mv_, start=True, stop=True).then_inc(s_rank_mm, 1)
            pe.wait_ge(s_pb_ready, 1)
            pe.matmul(bank[5][:, 0:T * E], ones[:], pb.rearrange("p t e -> p (t e)"), start=True, stop=True).then_inc(s_imp_mm, 1)
            pe.wait_ge(s_onehot_ready, 2)
            for n in range(2 * T):
                mm = pe.matmul(bank[2][:, 0:2 * NSP], cola[:, n, :], colb[:, n, :, :].rearrange("p v j -> p (v j)"), start=(n == 0), stop=(n == 2 * T - 1))
            mm.then_inc(s_src_mm, 1)

            def rows_t(i, k, rnd, first=False):
                pe.wait_ge(s_gathered[k], 16 * (rnd + 1))
                if not first:
                    pe.wait_ge(s_xe_ready, i - 1)
                ps = bank[k % 2][:, 0:3 * P // 2].bitcast(F16)
                for j in range(3):
                    mm = pe.transpose(ps[:, j * P:(j + 1) * P], xg[:, k, j * P:(j + 1) * P], ident16[:])
                mm.then_inc(s_xe_mm, 1)

            def weights(n, count=WIN):
                word = pe.value_load(expert[0:1, bass.ds(n, 1)], min_val=0, max_val=8 ** WIN - 1)
                return [wx[:, bass.ds(pe.snap(((word >> 3 * k) & 7) * XW), XW)] for k in range(count)]

            def up(i, k, w, first=False):
                pe.wait_ge(s_xe_ready, i + 1)
                if not first:
                    pe.wait_ge(s_high_ready, i - 1)
                k %= 2
                o_ = bank[2 + k][:, :]
                pe.matmul(o_, xe[:, k, 0:P], w[:, W1H:W1H + FI], start=True, stop=False)
                pe.matmul(o_, xe[:, k, P:2 * P], w[:, W1H:W1H + FI], start=False, stop=False)
                pe.matmul(o_, xe[:, k, 0:P], w[:, W1L:W1L + FI], start=False, stop=False)
                pe.matmul(o_, xe[:, k, 2 * P:3 * P], w[:, W1BH:W1BH + FI], start=False, stop=False)
                pe.matmul(o_, xe[0:D - P, k, 2 * P:3 * P], w[0:D - P, W1BL:W1BL + FI], start=False, stop=True).then_inc(s_up_mm, 1)

            def act_t(i, k, first=False):
                pe.wait_ge(s_low_ready, i + 1)
                if not first:
                    pe.wait_ge(s_actT_high, i)
                    pe.wait_ge(s_actT_low, i)
                k %= 2
                for v, half in enumerate((acth, actl)):
                    ps = bank[6 + v][:, 0:FI // 2].bitcast(F16)
                    for m in range(MC):
                        mm = pe.transpose(ps[:, m * P:(m + 1) * P], half[:, k, m * P:(m + 1) * P], ident16[:])
                mm.then_inc(s_actT_mm, 1)

            def down(i, k, w, first=False):
                pe.wait_ge(s_actT_high, i + 1)
                pe.wait_ge(s_actT_low, i + 1)
                if not first:
                    pe.wait_ge(s_y_ready, i - 1)
                k %= 2
                o_ = bank[4 + k][:, 0:D]
                for m in range(MC):
                    c = slice(m * P, (m + 1) * P)
                    d = m * D
                    pe.matmul(o_, actT[:, k, 0, c], w[:, W2H + d:W2H + d + D], start=(m == 0), stop=False)
                    pe.matmul(o_, actT[:, k, 1, c], w[:, W2H + d:W2H + d + D], start=False, stop=False)
                    mm = pe.matmul(o_, actT[:, k, 0, c], w[:, W2L + d:W2L + d + D], start=False, stop=(m == MC - 1))
                mm.then_inc(s_down_mm, 1)

            pe.wait_ge(s_w_low, len(jobs))
            pe.wait_ge(s_expert_ready, 1)
            rows_t(0, 0, 0, first=True)
            rows_t(1, 1, 0, first=True)
            w = weights(0, LEAD)
            up(0, 0, w[0], first=True)
            rows_t(2, 2, 0)
            up(1, 1, w[1], first=True)
            act_t(0, 0, first=True)
            for i in range(LAG, LEAD):
                rows_t(i + 1, (i + 1) % 4, (i + 1) // 4)
                up(i, i % 4, w[i])
                act_t(i - 1, i - 1)
                down(i - LAG, (i - LAG) % 4, w[i - LAG], first=(i < 4))
            with pe.Fori(0, (NS - LEAD) // STEP) as j:
                w = weights(j + 1)
                for k in range(LEAD, LEAD + STEP):
                    i = STEP * j + k
                    rows_t(i + 1, (k + 1) % 4, STEP // 4 * j + (k + 1) // 4)
                    up(i, k % 4, w[k - LEAD + LAG])
                    act_t(i - 1, k - 1)
                    down(i - LAG, (k - LAG) % 4, w[k - LEAD])
            act_t(NS - 1, NS - 1)
            w = weights(len(WINDOWS) - 1)
            for i in range(NS - LAG, NS):
                down(i, i % 4, w[i - WINDOWS[-1]])

        @block.scalar
        def _(act):
            act.wait_ge(s_setup_mm, 2)
            act.activation(wv, bank[2][0:NP1, 0:D], ACT.Copy).then_inc(s_wv_ready, 1)
            for i in range(2):
                act.wait_ge(s_g_mm, i + 1)
                act.activation(gsb[:, i * 512:(i + 1) * 512], bank[7][0:NP1, :], ACT.Copy).then_inc(s_g_ready, 1)
            for i in range(B):
                act.wait_ge(s_vp_mm, i + 1)
                act.activation(vs[:, i * IT:(i + 1) * IT, :].rearrange("p a d -> p (a d)"), bank[5 + i % 2][:, 0:IT * D], ACT.Copy).then_inc(s_vp_ready, 1)

            def softmax(b):
                act.wait_ge(s_nbias_ready, b + 1)
                if b >= 2:
                    act.wait_ge(s_pT_mm, b - 1)
                for n in range(IT):
                    i = b * IT + n
                    act.activation(prob[:, b % 2, n, :], bank[b % 2][:, n * NI:(n + 1) * NI], ACT.Exp, bias=nbias[:, i:i + 1],
                                   scale=KD ** -0.5, accum_out=rsum[:, i:i + 1]).then_inc(s_prob_ready, 1)

            def himg(b):
                act.wait_ge(s_himg_mm, b + 1)
                act.wait_ge(s_rinv_ready, b + 1)
                for n in range(IT):
                    i = b * IT + n
                    act.activation(h[:, b * CT + n, :], bank[5 + b % 2][:, n * D:(n + 1) * D], ACT.Copy, scale=rinv[:, i:i + 1]).then_inc(s_himg_ready, 1)

            softmax(0)
            softmax(1)
            act.wait_ge(s_wq_ready, 4)
            act.activation(w_half[:, 0, :, :], wq, ACT.Copy).then_inc(s_wqhigh_ready, 1)
            act.activation(bias_half[:, 0, :], bq, ACT.Copy).then_inc(s_wqhigh_ready, 1)
            for b in range(B):
                himg(b)
                if b + 2 < B:
                    softmax(b + 2)

            def x_high(t):
                act.wait_ge(s_xn_ready, t + 1)
                if t >= 2:
                    act.wait_ge(s_xT_mm, t - 1)
                act.activation(xs[:, t % 2, 0:P], xn[:, t % 2, 0:P], ACT.Copy).then_inc(s_xhigh_ready, 1)
                act.activation(xs[:, t % 2, 2 * P:P + D], xn[:, t % 2, P:D], ACT.Copy).then_inc(s_xhigh_ready, 1)

            x_high(0)
            x_high(1)
            for t in range(T + 2):
                if t < T:
                    act.wait_ge(s_qk_mm, t + 1)
                    if t >= 2:
                        act.wait_ge(s_feat_ready, 2 * (t - 1))
                    act.activation(eb[:, t % 2, :], bank[2 + t % 2][:, 0:2 * D], ACT.Exp, bias=ln_fs[:, 0:1], scale=1.0 / FS).then_inc(s_exp_ready, 1)
                    if t + 2 < T:
                        x_high(t + 2)
                    act.wait_ge(s_vb_mm, t + 1)
                    if t >= 2:
                        act.wait_ge(s_g1_ready, t - 1)
                    act.activation(th[:, t % 2, :], bank[4 + t % 2][:, D:D + R], ACT.Tanh, scale=sh[:, t:t + 1]).then_inc(s_tanh_ready, 1)
                    act.activation(v32[:, t * H:(t + 1) * H, :], bank[4 + t % 2][:, 0:D].rearrange("p (h e) -> p h e", e=DH), ACT.Copy,
                                   scale=1.0 / VS).then_inc(s_v_ready, 1)
                    act.wait_ge(s_f32_ready, t + 1)
                    for n in range(2):
                        act.activation(half_of(t, n, 0), twice(t, n), ACT.Copy).then_inc(s_fhigh_ready, 1)
                if 1 <= t <= T:
                    act.wait_ge(s_gT_mm, t)
                    if t >= 3:
                        act.wait_ge(s_pr_mm, t - 2)
                    act.activation(g1T[:, (t - 1) % 2, :], bank[6][:, 0:P], ACT.Copy).then_inc(s_gT_ready, 1)
                if t >= 2:
                    act.wait_ge(s_pr_mm, t - 1)
                    act.activation(pr[:, t - 2, :], bank[7][:, 0:4 * H], ACT.Copy, scale=sh[:, t - 2:t - 1]).then_inc(s_pr_ready, 1)
            act.wait_ge(s_pr_ready, T)
            act.activation(ga[:], pr[:, :, 0:2 * H], ACT.Tanh, scale=0.5).then_inc(s_ga_ready, 1)
            act.activation(gb[:], pr[:, :, 2 * H:4 * H], ACT.Tanh).then_inc(s_ga_ready, 1)
            act.wait_ge(s_dph_ready, 1)
            act.activation(gd[:], gc[:], ACT.Sin, scale=PI / 4).then_inc(s_sin_ready, 1)
            act.wait_ge(s_cos_ready, 1)
            act.activation(gd[:], gc[:], ACT.Tanh, scale=0.25).then_inc(s_gate_tanh, 1)
            act.wait_ge(s_gate_tanh, 1)
            act.activation(gate1[:], gd[:], ACT.Tanh, scale=htemp[:, 0:1]).then_inc(s_gate_tanh, 1)

            def heads_t(t):
                u = use["tr", t]
                if t >= 2:
                    act.wait_ge(s_at_mm, t - 1)
                    act.wait_ge(s_num_mm, t - 1)
                act.wait_ge(s_t0_full, u + 1)
                act.activation(qT[:, t % 2, :], bank[0][:, 0:G * P // 2].bitcast(F16), ACT.Copy).then_inc(s_t0_free, 1)
                act.wait_ge(s_t1_full, u + 1)
                act.activation(kT[:, t % 2, :], bank[1][:, 0:G * P // 2].bitcast(F16), ACT.Copy).then_inc(s_t1_free, 1)

            def values_high(b):
                act.wait_ge(s_gated, b + 1)
                act.activation(vg[:, b * CT * H:(b + 1) * CT * H, 0, 0:DH], v32[:, b * CT * H:(b + 1) * CT * H, :], ACT.Copy).then_inc(s_vhigh_ready, 1)

            def rows_high(b):
                for c in range(CT):
                    act.wait_ge(s_x2_ready, b * CT + c + 1)
                    if b >= 2:
                        act.wait_ge(s_x2_stored[b % 2], 16 * CT)
                    xrow = xr[:, b % 2 * CT + c, :]
                    act.activation(xrow[:, 0:P], x2[:, b % 2, c, 0:P], ACT.Copy).then_inc(s_xhi_ready, 1)
                    act.activation(xrow[:, 2 * P:P + D], x2[:, b % 2, c, P:D], ACT.Copy).then_inc(s_xhi_ready, 1)

            heads_t(0)
            heads_t(1)
            values_high(0)
            for t in range(T + 1):
                if t < T:
                    for n in range(4):
                        act.wait_ge(s_mask_done, 4 * t + n + 1)
                        if t and n == 0:
                            act.wait_ge(s_num_mm, t)
                        i, g0 = n // 2, n % 2 * GB
                        act.activation(at_half[:, 0, i, g0:g0 + GB, :], atm[:, i, g0:g0 + GB, :], ACT.Copy).then_inc(s_athigh_ready, 1)
                    if t % CT < 2:
                        n = t // CT * 2 + t % CT
                        act.wait_ge(s_state32, n + 1)
                        act.activation(st_half[:, t % 2, 0, :], state[:], ACT.Copy).then_inc(s_sthigh_ready, 1)
                if 1 <= t and t + 1 < T:
                    heads_t(t + 1)
                if 0 <= t - 4 < PT:
                    u = use["o", t - 4]
                    act.wait_ge(s_t0_full, u + 1)
                    act.activation(oT[0:DC, u % 2, :, :].rearrange("p c n -> p (c n)"), bank[0][0:DC, 0:2 * P], ACT.Copy).then_inc(s_t0_free, 1)
                if t % CT == 1 and t // CT + 1 < B:
                    values_high(t // CT + 1)
                if t % CT == 1 and 0 <= (t - 7) // CT < B:
                    b = (t - 7) // CT
                    rows_high(b)
                if 0 <= t - 7 < XT:
                    u = use["x", t - 7]
                    act.wait_ge(s_t0_full, u + 1)
                    act.activation(x2T[:, (t - 7) % 2, :, :].rearrange("p c n -> p (c n)"), bank[0][0:DC, 0:2 * P], ACT.Copy).then_inc(s_t0_free, 1)
                    act.wait_ge(s_t1_full, u + 1)
                    act.activation(lg[:, t - 7, :], bank[1][:, 0:E], ACT.Copy).then_inc(s_t1_free, 1)
                if t < len(jobs):
                    w, high, _low = staged(t)
                    act.wait_ge(s_w_loaded[t % 2], 16 * loads[t])
                    act.activation(w, w, ACT.Copy, scale=WS).then_inc(s_w_scaled, 1)
                    act.wait_ge(s_w_scaled, t + 1)
                    act.activation(high, w, ACT.Copy).then_inc(s_w_high, 1)
            act.wait_ge(s_t1_full, len(misc))
            for i, w in ((0, 4 * P), (1, 2 * P)):
                act.wait_ge(s_last_oT_mm, i + 1)
                act.activation(oT[0:DC, 2 * i:2 * i + w // (2 * P), :, :].rearrange("p b c n -> p (b c n)"), bank[2 + i][0:DC, 0:w], ACT.Copy).then_inc(s_last_oT, 1)
            for b in range(B - 2, B):
                n = 2 * (b - B + 2)
                if n:
                    act.wait_ge(s_last_route, 1)
                for i, w in ((0, 4 * P), (1, 2 * P)):
                    act.wait_ge(s_last_xT_mm, n + i + 1)
                    act.activation(x2T[:, 2 * i:2 * i + w // (2 * P), :, :].rearrange("p b c n -> p (b c n)"),
                                   bank[(2 if n else 6) + i][0:DC, 0:w], ACT.Copy).then_inc(s_last_xT, 1)
                act.wait_ge(s_last_route, n // 2 + 1)
                act.activation(lg[:, b * CT:(b + 1) * CT, :].rearrange("p t e -> p (t e)"), bank[n // 2][:, 0:CT * E], ACT.Copy).then_inc(s_last_logits, 1)
                rows_high(b)
            act.wait_ge(s_ls_ready, 1)
            act.activation(ex, ls, ACT.Exp).then_inc(s_ex_ready, 1)

            def silu(i, k, first=False):
                act.wait_ge(s_up_mm, i + 1)
                if not first:
                    act.wait_ge(s_low_ready, i - 1)
                    act.wait_ge(s_actT_mm, i - 1)
                act.activation(act32[:, k, :], bank[2 + k][:, :], ACT.Silu, scale=1.0 / WS).then_inc(s_act_ready, 1)
                act.activation(acth[:, k, :], bank[2 + k][:, :], ACT.Silu, scale=1.0 / WS).then_inc(s_high_ready, 1)

            def high_t(i, k, first=False):
                act.wait_ge(s_actT_mm, i + 1)
                if not first:
                    act.wait_ge(s_down_mm, i - 1)
                act.activation(actT[:, k, 0, :], bank[6][:, 0:FI // 2].bitcast(F16), ACT.Copy).then_inc(s_actT_high, 1)

            silu(0, 0, first=True)
            for i in range(1, LEAD):
                silu(i, i % 2, first=(i < 2))
                high_t(i - 1, (i - 1) % 2, first=(i < 3))
            with act.Fori(0, (NS - LEAD) // 4) as j:
                for k in range(LEAD, LEAD + 4):
                    silu(4 * j + k, k % 2)
                    high_t(4 * j + k - 1, (k - 1) % 2)
            high_t(NS - 1, (NS - 1) % 2)

        @block.vector
        def _(dve):
            step = [0]

            def link(ins):
                step[0] += 1
                ins.then_inc(s_step, 1)
                dve.wait_ge(s_step, step[0])

            def rsqrt(y, a, w):
                sq = nwt[:, 5, 0:w]
                yi = y.bitcast(I32)
                link(dve.tensor_scalar(yi, a.bitcast(I32), 1, None, ALU.logical_shift_right))
                link(dve.tensor_scalar(yi, yi, -1.0, RSQRT_MAGIC, ALU.mult, ALU.add))
                for _ in range(3):
                    link(dve.tensor_tensor(sq, y, y, ALU.mult))
                    link(dve.scalar_tensor_tensor(out=sq, in0=sq, scalar=-0.5, in1=a, op0=ALU.mult, op1=ALU.mult))
                    link(dve.scalar_tensor_tensor(out=y, in0=sq, scalar=1.5, in1=y, op0=ALU.add, op1=ALU.mult))

            dve.memset(ones[:], 1.0).then_inc(s_ones_ready, 1)
            dve.memset(ones16[:], 1.0).then_inc(s_ones_ready, 1)
            dve.memset(oT[DC:DC + 1, :, :, :], 1.0).then_inc(s_ones_ready, 1)
            link(dve.memset(vg[:, :, 0, DH:VE], 1.0))
            link(dve.memset(vg[:, :, 1, DH:VE], 0.0))
            dve.wait_ge(s_axt_mm, 1)
            dve.tensor_copy(axt[:].rearrange("p a n -> p (a n)"), bank[0][0:KD, 0:3 * NP1]).then_inc(s_axt_ready, 1)
            dve.wait_ge(s_setup_mm, 1)
            dve.tensor_copy(mt[:], bank[1][0:NP1, 0:NP1]).then_inc(s_mt_ready, 1)

            def negmax(b):
                dve.wait_ge(s_score_mm, b + 1)
                i = b * IT
                link(dve.tensor_reduce(nmax[:, i:i + IT], bank[b % 2][:, :].rearrange("p (n m) -> p n m", n=IT), AX_X, ALU.max, negate=True))
                dve.tensor_scalar(nbias[:, i:i + IT], nmax[:, i:i + IT], KD ** -0.5, None, ALU.mult).then_inc(s_nbias_ready, 1)

            negmax(0)
            negmax(1)
            dve.wait_ge(s_attn_loaded, 16 * 11)
            dve.wait_ge(s_lnb_mm, 1)
            dve.wait_ge(s_mnb_mm, 1)
            link(dve.tensor_tensor(bq[:, 0:512], bank[4][0:1, 0:512], bq[:, 0:512], ALU.add))
            link(dve.tensor_tensor(bq[:, 512:3 * D], bank[7][0:1, 0:3 * D - 512], bq[:, 512:3 * D], ALU.add))
            for w, scale in ((slice(0, 2 * D), FS), (slice(2 * D, 3 * D), VS)):
                link(dve.tensor_scalar(bq[:, w], bq[:, w], scale, None, ALU.mult))
            dve.tensor_tensor(wp[DC:DC + 1, 1, :], bank[3][DC:DC + 1, 0:D], bp[DC:DC + 1, :], ALU.add).then_inc(s_wp_ready, 1)
            for c in range(2):
                for w, scale in ((slice(0, 2 * D), FS), (slice(2 * D, 3 * D), VS)):
                    dve.tensor_scalar(wq[:, c, w], wq[:, c, w], lnw[:, c:c + 1], scale, ALU.mult, ALU.mult).then_inc(s_wq_ready, 1)
                dve.tensor_scalar(wp[0:DC, c, :], wp[0:DC, c, :], mnw[:, 0:1], None, ALU.mult).then_inc(s_wp_ready, 1)
            link(dve.tensor_scalar(htemp[:], temp[:], 0.1, 2.0, ALU.max, ALU.min))
            link(dve.tensor_scalar(htemp[:], htemp[:], 0.5, None, ALU.mult))

            def moments(t, src):
                link(dve.bn_stats(stat[:, t, :], src))
                link(dve.bn_aggr(mv[:, t, :], stat[:, t, :]))

            dve.wait_ge(s_txt_loaded, 16 * B)
            for b in range(B):
                moments(b * CT + IT, h[:, b * CT + IT, :])
            dve.wait_ge(s_wqhigh_ready, 2)
            dve.tensor_tensor(w_half[:, 1, 0, :], wq[:, 0, :], w_half[:, 0, 0, :], ALU.subtract).then_inc(s_wqlow_ready, 1)
            dve.tensor_tensor(w_half[0:D - P, 1, 1, :], wq[0:D - P, 1, :], w_half[0:D - P, 0, 1, :], ALU.subtract).then_inc(s_wqlow_ready, 1)
            dve.tensor_tensor(bias_half[:, 1, :], bq, bias_half[:, 0, :], ALU.subtract).then_inc(s_wqlow_ready, 1)
            for b in range(B):
                dve.wait_ge(s_prob_ready, IT * (b + 1))
                dve.reciprocal(rinv[:, b * IT:(b + 1) * IT], rsum[:, b * IT:(b + 1) * IT]).then_inc(s_rinv_ready, 1)
                dve.wait_ge(s_pT_mm, b + 1)
                if b >= 2:
                    dve.wait_ge(s_himg_mm, b - 1)
                dve.tensor_copy(probT[:, b % 2, :, :].rearrange("p a n -> p (a n)"), bank[2 + b % 2][:, :]).then_inc(s_pT_ready, 1)
                if b + 2 < B:
                    negmax(b + 2)
                if b >= 1:
                    for n in range(IT):
                        dve.wait_ge(s_himg_ready, (b - 1) * IT + n + 1)
                        moments((b - 1) * CT + n, h[:, (b - 1) * CT + n, :])
            for n in range(IT):
                dve.wait_ge(s_himg_ready, (B - 1) * IT + n + 1)
                moments((B - 1) * CT + n, h[:, (B - 1) * CT + n, :])

            mean, var = mv[:, :, 0], mv[:, :, 1]
            va, r2 = nwt[:, 0, 0:T], nwt[:, 1, 0:T]
            link(dve.tensor_scalar(va, var, EPS, None, ALU.add))
            rsqrt(r1[:], va, T)
            link(dve.tensor_tensor(va, var, r1[:], ALU.mult))
            link(dve.tensor_tensor(va, va, r1[:], ALU.mult))
            link(dve.tensor_scalar(va, va, EPS, None, ALU.add))
            rsqrt(r2, va, T)
            link(dve.scalar_tensor_tensor(out=sh[:], in0=va, scalar=0.5, in1=r2, op0=ALU.mult, op1=ALU.mult))
            link(dve.tensor_tensor(r12[:], r1[:], r2, ALU.mult))
            link(dve.scalar_tensor_tensor(out=nmr[:], in0=mean, scalar=-1.0, in1=r12[:], op0=ALU.mult, op1=ALU.mult))

            def normalize(t):
                if t >= 2:
                    dve.wait_ge(s_xlow_ready, 2 * (t - 1))
                dve.tensor_scalar(xn[:, t % 2, :], h[:, t, :], r12[:, t:t + 1], nmr[:, t:t + 1], ALU.mult, ALU.add).then_inc(s_xn_ready, 1)

            def x_low(t):
                dve.wait_ge(s_xhigh_ready, 2 * (t + 1))
                dve.tensor_tensor(xs[:, t % 2, P:2 * P], xn[:, t % 2, 0:P], xs[:, t % 2, 0:P], ALU.subtract).then_inc(s_xlow_ready, 1)
                dve.tensor_tensor(xs[:, t % 2, P + D:2 * D], xn[:, t % 2, P:D], xs[:, t % 2, 2 * P:P + D], ALU.subtract).then_inc(s_xlow_ready, 1)

            def x_t(t):
                dve.wait_ge(s_xT_mm, t + 1)
                if t >= 2:
                    dve.wait_ge(s_vb_mm, t - 1)
                dve.tensor_copy(xT[:, t % 2, :, :].rearrange("p c n -> p (c n)"), bank[t % 2][:, 0:3 * P // 2].bitcast(F16)).then_inc(s_xT_ready, 1)

            normalize(0)
            normalize(1)
            x_low(0)
            x_low(1)
            x_t(0)
            def features_low(t):
                for n in range(2):
                    dve.wait_ge(s_fhigh_ready, 2 * t + n + 1)
                    dve.tensor_tensor(half_of(t, n, 1), twice(t, n), half_of(t, n, 0), ALU.subtract).then_inc(s_feat_ready, 1)

            for t in range(T):
                if t + 1 < T:
                    x_t(t + 1)
                if t + 2 < T:
                    normalize(t + 2)
                dve.wait_ge(s_exp_ready, t + 1)
                link(dve.tensor_scalar(eb[:, t % 2, :], eb[:, t % 2, :], FS, None, ALU.min))
                dve.scalar_tensor_tensor(out=eb[:, t % 2, :], in0=bank[2 + t % 2][:, 0:2 * D], scalar=0.0,
                                         in1=eb[:, t % 2, :], op0=ALU.max, op1=ALU.add).then_inc(s_f32_ready, 1)
                if t + 2 < T:
                    x_low(t + 2)
                dve.wait_ge(s_tanh_ready, t + 1)
                dve.wait_ge(s_v_ready, t + 1)
                if t >= 2:
                    dve.wait_ge(s_gT_mm, t - 1)
                dve.scalar_tensor_tensor(out=g1[:, t % 2, :], in0=th[:, t % 2, :], scalar=1.0, in1=bank[4 + t % 2][:, D:D + R],
                                         op0=ALU.add, op1=ALU.mult).then_inc(s_g1_ready, 1)
                if t:
                    features_low(t - 1)
            features_low(T - 1)
            dve.wait_ge(s_ga_ready, 2)
            dve.tensor_tensor(gc[:], gb[:, :, 0:H], gb[:, :, H:2 * H], ALU.subtract).then_inc(s_dph_ready, 1)
            link(dve.tensor_scalar(ga[:], ga[:], 1.0, None, ALU.add))
            link(dve.tensor_tensor(ga[:, :, 0:H], ga[:, :, 0:H], ga[:, :, H:2 * H], ALU.mult))
            dve.wait_ge(s_sin_ready, 1)
            link(dve.tensor_tensor(gc[:], gd[:], gd[:], ALU.mult))
            link(dve.tensor_scalar(gc[:], gc[:], -2.0, 1.0, ALU.mult, ALU.add))
            link(dve.tensor_tensor(gc[:], gc[:], gc[:], ALU.mult))
            link(dve.tensor_scalar(gc[:], gc[:], 2.0, -1.0, ALU.mult, ALU.add))
            dve.tensor_tensor(gc[:], gc[:], ga[:, :, 0:H], ALU.mult).then_inc(s_cos_ready, 1)
            dve.wait_ge(s_gate_tanh, 2)
            link(dve.tensor_scalar(gate1[:], gate1[:], 0.5, 1.5, ALU.mult, ALU.add))

            def gated_values(b):
                w = slice(b * CT * H, (b + 1) * CT * H)
                g_ = gate1[:].rearrange("p t h -> p (t h)")[:, w]
                dve.tensor_tensor(v32[:, w, :], v32[:, w, :], g_.unsqueeze(2).broadcast_to([P, CT * H, DH]), ALU.mult).then_inc(s_gated, 1)

            def values_low(b):
                w = slice(b * CT * H, (b + 1) * CT * H)
                dve.wait_ge(s_vhigh_ready, b + 1)
                dve.tensor_tensor(vg[:, w, 1, 0:DH], v32[:, w, :], vg[:, w, 0, 0:DH], ALU.subtract).then_inc(s_vg_ready, 1)

            def second_norm(b):
                t0 = b * CT
                va, r, nm = nwt[:, 2, 0:CT], nwt[:, 3, 0:CT], nwt[:, 4, 0:CT]
                link(dve.tensor_scalar(va, mv[:, t0:t0 + CT, 1], EPS, None, ALU.add))
                rsqrt(r, va, CT)
                link(dve.scalar_tensor_tensor(out=nm, in0=mv[:, t0:t0 + CT, 0], scalar=-1.0, in1=r, op0=ALU.mult, op1=ALU.mult))
                if b >= 2:
                    dve.wait_ge(s_t0_full, use["x", t0 - 2 * CT + CT - 1] + 1)
                    dve.wait_ge(s_xlo_ready, 2 * (t0 - CT))
                for cc in range(CT):
                    dve.tensor_scalar(x2[:, b % 2, cc, :], h[:, t0 + cc, :], r[:, cc:cc + 1], nm[:, cc:cc + 1],
                                      ALU.mult, ALU.add).then_inc(s_x2_ready, 1)

            def rows_low(b):
                for cc in range(CT):
                    dve.wait_ge(s_xhi_ready, 2 * (b * CT + cc + 1))
                    xrow, xf = xr[:, b % 2 * CT + cc, :], x2[:, b % 2, cc, :]
                    dve.tensor_tensor(xrow[:, P:2 * P], xf[:, 0:P], xrow[:, 0:P], ALU.subtract).then_inc(s_xlo_ready, 1)
                    dve.tensor_tensor(xrow[:, P + D:2 * D], xf[:, P:D], xrow[:, 2 * P:P + D], ALU.subtract).then_inc(s_xlo_ready, 1)

            gated_values(0)
            values_low(0)
            for t in range(T + 1):
                b, c = divmod(t, CT)
                if t < T:
                    dve.wait_ge(s_at_mm, t + 1)
                    if t:
                        dve.wait_ge(s_atlow_ready, 4 * t)
                    for n in range(4):
                        i, g0 = n // 2, n % 2 * GB
                        dve.tensor_tensor(atm[:, i, g0:g0 + GB, :], bank[2 + n][:, 0:GB * P].rearrange("p (g l) -> p g l", g=GB),
                                          causal[:].unsqueeze(1).broadcast_to([P, GB, P]), ALU.mult).then_inc(s_mask_done, 1)
                    if c < 2:
                        n = 2 * b + c
                        dve.wait_ge(s_state_mm, n + 1)
                        if n:
                            dve.wait_ge(s_state_ready, n)
                        dve.tensor_tensor(state[:], bank[7][:, 0:H * VE],
                                          headmask[:].rearrange("p g h e -> p (g h e)"), ALU.mult).then_inc(s_state32, 1)
                if 0 <= t - 5 < T:
                    tt = t - 5
                    u = use["o", tt]
                    dve.wait_ge(s_t1_full, u + 1)
                    dve.tensor_tensor(h[:, tt, :], bank[1][:, 0:D], h[:, tt, :], ALU.add).then_inc(s_t1_free, 1)
                    dve.wait_ge(s_t1_free, u + 1)
                    moments(tt, h[:, tt, :])
                if t < T:
                    if c == 1 and b + 1 < B:
                        gated_values(b + 1)
                    if c == 2 and b + 1 < B:
                        values_low(b + 1)
                    for n in range(4):
                        i, g0 = n // 2, n % 2 * GB
                        dve.wait_ge(s_athigh_ready, 4 * t + n + 1)
                        dve.tensor_tensor(at_half[:, 1, i, g0:g0 + GB, :], atm[:, i, g0:g0 + GB, :], at_half[:, 0, i, g0:g0 + GB, :],
                                          ALU.subtract).then_inc(s_atlow_ready, 1)
                    if c < 2:
                        dve.wait_ge(s_sthigh_ready, 2 * b + c + 1)
                        dve.tensor_tensor(st_half[:, t % 2, 1, :], state[:], st_half[:, t % 2, 0, :], ALU.subtract).then_inc(s_state_ready, 1)
                if 0 <= t - 5 and (t - 5) % CT == CT - 1:
                    second_norm((t - 5) // CT)
                if c == 0 and 1 <= b <= B:
                    ob = o[:, (b - 1) % 2, :, :]
                    va, r = nwt[:, 0, :], nwt[:, 1, :]
                    dve.wait_ge(s_o_ready, t)
                    link(dve.tensor_reduce(osum[:], ob, AX_X, ALU.add))
                    link(dve.tensor_scalar(osum[:], osum[:], 1.0 / DH, None, ALU.mult))
                    link(dve.tensor_tensor(ob, ob, osum[:].unsqueeze(2).broadcast_to([P, CT * H, DH]), ALU.subtract))
                    link(dve.tensor_tensor(osq, ob, ob, ALU.mult))
                    link(dve.tensor_reduce(va, osq, AX_X, ALU.add))
                    link(dve.tensor_scalar(va, va, 1.0 / DH, EPS, ALU.mult, ALU.add))
                    rsqrt(r, va, CT * H)
                    dve.tensor_tensor(ob, ob, r.unsqueeze(2).broadcast_to([P, CT * H, DH]), ALU.mult).then_inc(s_ohat_ready, 1)
                if t % CT == 2 and 0 <= t - 8:
                    rows_low((t - 8) // CT)
                if t < T:
                    dve.wait_ge(s_num_mm, t + 1)
                    num = bank[6][:, 0:H * VE].rearrange("p (h e) -> p h e", e=VE)
                    link(dve.tensor_scalar(rden[:, 0, :], num[:, :, DH], 1e-6, None, ALU.add))
                    link(dve.reciprocal(rden[:, 1, :], rden[:, 0, :]))
                    dve.tensor_tensor(o[:, b % 2, c * H:(c + 1) * H, :], num[:, :, 0:DH], rden[:, 1, :].unsqueeze(2).broadcast_to([P, H, DH]),
                                      ALU.mult).then_inc(s_o_ready, 1)


            def bt(v, n=E):
                return v.unsqueeze(2).broadcast_to([P, T, n])

            def be(v):
                return v.unsqueeze(1).broadcast_to([P, T, E])

            dve.wait_ge(s_iota_ready, 5)
            link(dve.memset(keep, 1.0))
            link(dve.memset(keep[:, :, 0:1], 0.0))
            for k in range(WIN // 2):
                ins = dve.memset(pow8[:].rearrange("p (a k) -> p a k", a=2)[:, :, k], float(8 ** k))
            link(ins)
            t0 = PT - 1
            dve.wait_ge(s_t1_full, use["o", t0] + 1)
            dve.tensor_tensor(h[:, t0, :], bank[1][:, 0:D], h[:, t0, :], ALU.add).then_inc(s_t1_free, 1)
            dve.wait_ge(s_t1_free, len(misc))
            moments(t0, h[:, t0, :])
            second_norm(B - 2)
            for i, n in ((0, 2), (1, 1)):
                ts = slice(PT + 2 * i, PT + 2 * i + n)
                hs = h[:, ts, :].rearrange("p t d -> p (t d)")
                dve.wait_ge(s_last_proj, i + 1)
                link(dve.tensor_tensor(hs, bank[4 + i][:, 0:n * D], hs, ALU.add))
            for t in range(PT, T):
                ins = dve.bn_stats(stat[:, t, :], h[:, t, :])
            link(ins)
            for t in range(PT, T):
                ins = dve.bn_aggr(mv[:, t, :], stat[:, t, :])
            link(ins)
            second_norm(B - 1)
            rows_low(B - 2)
            rows_low(B - 1)
            dve.wait_ge(s_last_logits, 2)
            mx, e1, e2, b1, b2, rs, z = (small[:, n, :] for n in range(7))
            link(dve.tensor_reduce(mx, lg[:], AX_X, ALU.max))
            dve.tensor_tensor(ls, lg[:], bt(mx), ALU.subtract).then_inc(s_ls_ready, 1)
            dve.wait_ge(s_ls_ready, 1)

            def first_of(eq, dst):
                link(dve.tensor_tensor(eq, eq, be(iota_e[:]), ALU.mult))
                link(dve.tensor_reduce(mx, eq, AX_X, ALU.min))
                link(dve.tensor_tensor(dst, be(iota_e[:]), bt(mx), ALU.is_equal))

            link(dve.tensor_scalar(tmp, ls, 0.0, None, ALU.is_equal))
            first_of(tmp, sel[:, 0, :, :])
            link(dve.scalar_tensor_tensor(out=pb, in0=sel[:, 0, :, :], scalar=-1e30, in1=ls, op0=ALU.mult, op1=ALU.add))
            link(dve.tensor_reduce(mx, pb, AX_X, ALU.max))
            link(dve.tensor_tensor(tmp, pb, bt(mx), ALU.is_equal))
            first_of(tmp, sel[:, 1, :, :])
            dve.tensor_tensor(selsum, sel[:, 0, :, :], sel[:, 1, :, :], ALU.add).then_inc(s_sel_ready, 1)
            dve.wait_ge(s_ex_ready, 1)
            link(dve.tensor_reduce(z, ex, AX_X, ALU.add))
            link(dve.reciprocal(rs, z))
            dve.tensor_tensor(pb, ex, bt(rs), ALU.mult).then_inc(s_pb_ready, 1)
            dve.wait_ge(s_rank_mm, 1)
            link(dve.tensor_copy(tot, bank[0][:, T * E:2 * T * E].rearrange("p (t e) -> p e t", e=E)))
            flat = lambda v: v.rearrange("p e t -> p (e t)")
            link(dve.tensor_tensor_scan(flat(inc), flat(keep), flat(tot), 0.0, ALU.mult, ALU.add))
            link(dve.tensor_scalar(cnti[:], inc[:, :, T - 1], float(P - 1), None, ALU.add))
            link(dve.tensor_scalar(cnti[:], cnti[:], 7, None, ALU.logical_shift_right))
            link(dve.tensor_copy(cnt[:, 0, :], cnti[:]))
            link(dve.tensor_tensor_scan(cnt[:, 1, :], ones[:, 0:E], cnt[:, 0, :], 0.0, ALU.mult, ALU.add))
            link(dve.tensor_tensor(cnt[:, 2, :], cnt[:, 1, :], cnt[:, 0, :], ALU.subtract))
            link(dve.tensor_tensor(inc, inc, tot, ALU.subtract))
            link(dve.tensor_tensor(tmp, bank[0][:, 0:T * E].rearrange("p (t e) -> p t e", e=E), inc.rearrange("p e t -> p t e"), ALU.add))
            link(dve.tensor_scalar(cnt[:, 3, :], cnt[:, 2, :], float(P), None, ALU.mult))
            link(dve.tensor_tensor(tmp, tmp, be(cnt[:, 3, :]), ALU.add))
            for k in range(2):
                link(dve.tensor_tensor(ls, sel[:, k, :, :], tmp, ALU.mult))
                link(dve.tensor_reduce(slot[:, k, :], ls, AX_X, ALU.add))
            link(dve.tensor_copy(sloti[:, 0, :], slot[:].rearrange("p k t -> p (k t)")))
            link(dve.tensor_scalar(sloti[:, 1, :], sloti[:, 0, :], 7, None, ALU.logical_shift_right))
            link(dve.tensor_scalar(sloti[:, 2, :], sloti[:, 0, :], P - 1, None, ALU.bitwise_and))
            link(dve.tensor_copy(slotf[:], sloti[:, 1:3, :]))
            for n in range(2 * T):
                ins = dve.tensor_scalar(cola[:, n, :], iota_p16[:], slotf[:, 1, n:n + 1], None, ALU.is_equal)
            ins.then_inc(s_onehot_ready, 1)
            link(dve.tensor_tensor(cole, iota_p[:, 0:NSP].unsqueeze(1).broadcast_to([P, 2 * T, NSP]),
                                   slotf[:, 0, :].unsqueeze(2).broadcast_to([P, 2 * T, NSP]), ALU.is_equal))
            link(dve.tensor_scalar(colb[:, :, 0, :], cole, row1[:, 0:1], None, ALU.mult))
            dve.tensor_tensor(colb[:, :, 1, :], cole, choice1[:].unsqueeze(2).broadcast_to([P, 2 * T, NSP]), ALU.mult).then_inc(s_onehot_ready, 1)
            link(dve.tensor_tensor(passed, cnt[0:1, 1, :].unsqueeze(1).broadcast_to([1, NSP, E]),
                                   iota_p[0:1, 0:NSP].unsqueeze(2).broadcast_to([1, NSP, E]), ALU.is_le))
            link(dve.tensor_reduce(expf[:], passed, AX_X, ALU.add))
            link(dve.tensor_scalar(expf[:], expf[:], float(E - 1), None, ALU.min))
            for n, i in enumerate(WINDOWS):
                ins = dve.tensor_tensor(packf[:, n, :], expf[:, i:i + WIN], pow8[:], ALU.mult)
            link(ins)
            link(dve.tensor_reduce(packs[:], packf[:].rearrange("p n (a k) -> p n a k", a=2), AX_X, ALU.add))
            link(dve.tensor_copy(packi[:], packs[:]))
            link(dve.tensor_scalar(packi[:, :, 1], packi[:, :, 1], 3 * WIN // 2, None, ALU.logical_shift_left))
            dve.tensor_tensor(expert[:], packi[:, :, 0], packi[:, :, 1], ALU.bitwise_or).then_inc(s_expert_ready, 1)
            dve.wait_ge(s_src_mm, 1)
            link(dve.tensor_copy(src[:, 0:2, :].rearrange("p v j -> p (v j)"), bank[2][:, 0:2 * NSP]))
            link(dve.scalar_tensor_tensor(out=src[:, 2, :], in0=src[:, 1, :], scalar=float(P), in1=src[:, 0, :], op0=ALU.mult, op1=ALU.add))
            link(dve.tensor_scalar(src[:, 3, :], src[:, 0, :], 0.0, NO_TOKEN, ALU.is_equal, ALU.mult))
            link(dve.tensor_tensor(src[:, 2, :], src[:, 2, :], src[:, 3, :], ALU.add))
            dve.tensor_scalar(dst_row[:], src[:, 2, :], -float(P + 1), None, ALU.add).then_inc(s_rows_ready, 1)
            link(dve.tensor_scalar(src[:, 3, :], src[:, 2, :], float(NTOK + P + 1), -float(NTOK), ALU.is_ge, ALU.mult))
            link(dve.tensor_tensor(src[:, 3, :], src[:, 3, :], src[:, 2, :], ALU.add))
            dve.tensor_scalar(tok_row[:], src[:, 3, :], -float(P + 1), None, ALU.add).then_inc(s_rows_ready, 1)

            def rows_t(i, k, first=False):
                dve.wait_ge(s_xe_mm, i + 1)
                if not first:
                    dve.wait_ge(s_up_mm, i - 1)
                dve.tensor_copy(xe[:, k, :], bank[k][:, 0:3 * P // 2].bitcast(F16)).then_inc(s_xe_ready, 1)

            def low(i, k, first=False):
                dve.wait_ge(s_high_ready, i + 1)
                if not first:
                    dve.wait_ge(s_actT_mm, i - 1)
                dve.tensor_tensor(actl[:, k, :], act32[:, k, :], acth[:, k, :], ALU.subtract).then_inc(s_low_ready, 1)

            def low_t(i, k, first=False):
                dve.wait_ge(s_actT_mm, i + 1)
                if not first:
                    dve.wait_ge(s_down_mm, i - 1)
                dve.tensor_copy(actT[:, k, 1, :], bank[7][:, 0:FI // 2].bitcast(F16)).then_inc(s_actT_low, 1)

            def result(i, k, rnd=None):
                dve.wait_ge(s_down_mm, i + 1)
                if rnd is not None:
                    dve.wait_ge(s_scattered[k], 16 * rnd)
                dve.tensor_scalar(ye[:, k, :], bank[4 + k % 2][:, 0:D], 1.0 / WS, None, ALU.mult).then_inc(s_y_ready, 1)

            dve.wait_ge(s_imp_mm, 1)
            link(dve.tensor_reduce(imp[:], bank[5][:, 0:T * E].rearrange("p (t e) -> p e t", e=E), AX_X, ALU.add))
            link(dve.tensor_scalar(imp[:], imp[:], 0.1, 0.91, ALU.mult, ALU.add))
            for k, ek, bk in ((0, e1, b1), (1, e2, b2)):
                link(dve.tensor_tensor(ls, sel[:, k, :, :], ex, ALU.mult))
                link(dve.tensor_reduce(ek, ls, AX_X, ALU.add))
                link(dve.tensor_tensor(ls, sel[:, k, :, :], be(imp[:]), ALU.mult))
                link(dve.tensor_reduce(bk, ls, AX_X, ALU.add))
            link(dve.tensor_tensor(e1, e1, b2, ALU.mult))
            link(dve.tensor_tensor(e2, e2, b1, ALU.mult))
            link(dve.tensor_tensor(z, e1, e2, ALU.add))
            link(dve.reciprocal(rs, z))
            link(dve.tensor_tensor(gate[:, 0, :], e1, rs, ALU.mult))
            link(dve.tensor_tensor(gate[:, 1, :], e2, rs, ALU.mult))
            rows_t(0, 0, first=True)
            rows_t(1, 1, first=True)
            low(0, 0, first=True)
            rows_t(2, 0)
            low_t(0, 0, first=True)
            low(1, 1, first=True)
            for i in range(2, LEAD):
                rows_t(i + 1, (i + 1) % 2)
                low_t(i - 1, (i - 1) % 2, first=(i < 3))
                low(i, i % 2)
                result(i - 2, (i - 2) % 4, rnd=(i - 2) // 4 or None)
            with dve.Fori(0, (NS - LEAD) // 4) as j:
                for k in range(LEAD, LEAD + 4):
                    i = 4 * j + k
                    rows_t(i + 1, (k + 1) % 2)
                    low_t(i - 1, (k - 1) % 2)
                    low(i, k % 2)
                    result(i - 2, (k - 2) % 4, rnd=j + (k - 2) // 4)
            low_t(NS - 1, (NS - 1) % 2)
            for i in range(NS - 2, NS):
                result(i, i % 4, rnd=i // 4)

            for b in range(B):
                dve.wait_ge(s_y_loaded[b], 32)
                for t in range(b * CT, (b + 1) * CT):
                    link(dve.scalar_tensor_tensor(out=h[:, t, :], in0=yt[0][:, t, :], scalar=gate[:, 0, t:t + 1], in1=h[:, t, :], op0=ALU.mult, op1=ALU.add))
                    dve.scalar_tensor_tensor(out=h[:, t, :], in0=yt[1][:, t, :], scalar=gate[:, 1, t:t + 1], in1=h[:, t, :],
                                             op0=ALU.mult, op1=ALU.add).then_inc(s_sum_ready, 1)


def kernel(**inputs):
    import numpy as np
    import concourse.bacc as _bacc
    from concourse.bass_utils import run_bass_kernel_spmd as _run

    a = {k: np.asarray(v) for k, v in inputs.items()}
    f32 = np.float32
    two = lambda w: np.ascontiguousarray(w.reshape(2, DC, -1).transpose(1, 0, 2))
    rest_twice = lambda w: np.stack([w[0:P], np.concatenate([w[P:D], w[P:D]], 0)], 1)
    unit = np.zeros((1, NP1), f32)
    unit[0, NP1 - 1] = 1.0
    x = a["x"].reshape(B, 3, 16, 4, 16, 4).transpose(1, 3, 5, 0, 2, 4).reshape(48, B * NI)
    wb2 = a["L0_attn_Wb2"].reshape(R, H, 5)
    lay = {
        "xp1": np.concatenate([x, np.ones((1, B * NI), f32)], 0),
        "cwb": two(np.concatenate([a["L0_tok_conv_w"].reshape(D, 48), a["L0_tok_conv_b"][:, None]], 1)),
        "wtok": two(np.concatenate([a["L0_tok_q_w"], a["L0_tok_k_w"], a["L0_tok_v_w"]], 0).T),
        "btok": np.concatenate([a["L0_tok_q_b"], a["L0_tok_k_b"], a["L0_tok_v_b"]])[None],
        "unit": unit,
        "pjt": a["L0_tok_proj_w"].T,
        "pjb": a["L0_tok_proj_b"][None],
        "txt": a["txt"],
        "wq": rest_twice(np.concatenate([a["L0_attn_Wqkv"], a["L0_attn_Wb1"]], 1)),
        "lnw": rest_twice(a["L0_attn_ln_w"][:, None])[:, :, 0],
        "lnb": rest_twice(a["L0_attn_ln_b"][:, None])[:, :, 0],
        "bqkv": a["L0_attn_bqkv"][None],
        "wb2": np.concatenate([wb2[:, :, i] for i in (0, 2, 1, 3)], 1),
        "wp": two(a["L0_attn_Wproj"]),
        "mnw": np.tile(a["L0_attn_mn_w"], DC // DH)[:, None],
        "mnb": np.tile(a["L0_attn_mn_b"], DC // DH)[:, None],
        "bproj": a["L0_attn_bproj"][None],
        "temp": np.broadcast_to(a["L0_attn_temperature"][None], (P, 1)),
        "wr": two(a["L0_ffn_router_w"].T),
        "w1a": a["L0_ffn_w1"].transpose(2, 0, 1).reshape(D, E * FI)[0:P],
        "w1b": a["L0_ffn_w1"].transpose(2, 0, 1).reshape(D, E * FI)[P:D],
        "w2": a["L0_ffn_w2"].transpose(2, 0, 1).reshape(MC, P, E, D).transpose(1, 2, 0, 3).reshape(P, E * MC * D),
    }
    nc = _bacc.Bacc("TRN2", target_bir_lowering=False, num_devices=1)
    arrays = {f"in_{k}": np.ascontiguousarray(v) for k, v in lay.items()}
    aps = {k: nc.dram_tensor(f"in_{k}", arrays[f"in_{k}"].shape, F32, kind="ExternalInput").ap() for k in lay}
    x2_dram = nc.dram_tensor("x2_rows", (NTOK, 2 * D), F16, kind="Internal").ap()
    y_dram = nc.dram_tensor("y_rows", (2 * NTOK, D), F32, kind="Internal").ap()
    out = nc.dram_tensor("out_0", (B, CT * P, D), F32, kind="ExternalOutput").ap()
    build(nc, aps, x2_dram, y_dram, out)
    r = _run(nc, [arrays], core_ids=[0])
    return r.results[0]["out_0"]
```

```python
from contextlib import ExitStack
from math import log, prod

import concourse.bass as bass
from concourse import mybir

ALU = mybir.AluOpType
ACT = mybir.ActivationFunctionType
F32 = mybir.dt.float32
F16 = mybir.dt.float16
I32 = mybir.dt.int32
U32 = mybir.dt.uint32
AX_X = mybir.AxisListType.X

P = 128
B = 4
NI = 256
D = 192
DC = D // 2
KD = 96
NP1 = 3 * 4 * 4 + 1
CT = 3
T = B * CT
IT = NI // P
H = 12
DH = D // H
SLOT = 4 * DH
HG = P // SLOT
G = H // HG
GB = G // 2
VS = 64.0
FS = 16.0
VE = DH + 1
R = 128
E = 8
FI = 512
MC = FI // P
NS = T * 2 + E - 1
NSP = NS + 1
LEAD = 7
STEP = 8
LAG = 2
assert (NS - LEAD) % STEP == 0
WIN = STEP + LAG
WINDOWS = [0] + list(range(LEAD - LAG, NS - LAG, STEP))
assert WIN * 3 < 32 and LEAD <= WIN
NTOK = T * P
WS = 256.0
W1H, W1L = 0, FI
W1BH, W1BL = 2 * FI, 3 * FI
W2H = 4 * FI
W2L = W2H + MC * D
XW = W2L + MC * D
STG = 2048
EPS = 1e-5
PI = 3.141592653589793
RSQRT_MAGIC = float(0x5F3759DF)
NO_TOKEN = 100000.0
SUM_SHARED = (2,)
SUM_ORDER = (0, 1, 3) + SUM_SHARED
assert sorted(SUM_ORDER) == list(range(B))


def build(nc, A, x2_dram, y_dram, out):
    with ExitStack() as ctx:
        def sb(name, shape, dt=F32):
            return ctx.enter_context(nc.sbuf_tensor(name, shape, dt))

        def sem(name):
            return ctx.enter_context(nc.semaphore(name))

        bank = [ctx.enter_context(nc.psum_tensor(f"bank{i}", [P, 512], F32)) for i in range(8)]

        def parts_of(name, *shapes):
            sizes = [prod(s[1:]) for s in shapes]
            whole = places.setdefault(name, sb(name, [P, max_words[name]]) if name not in places else None)
            views, at_ = [], 0
            for shape, n in zip(shapes, sizes):
                view = whole[0:shape[0], at_:at_ + n]
                names = "abc"[:len(shape) - 1]
                if len(names) > 1:
                    view = view.rearrange("p (" + " ".join(names) + ") -> p " + " ".join(names), **dict(zip(names, shape[1:])))
                views.append(view)
                at_ += n
            assert at_ <= max_words[name]
            return views

        places = {}
        max_words = {"first_place": 2 * CT * D, "second_place": 2 * CT * D, "fourth_place": 2 * D, "third_place": 2 * (D + 2 * D + 3 * R + D)}
        wtok, btok, pjt = parts_of("first_place", (DC, 2, 3 * KD), (1, 3 * KD), (KD, D))
        (o,) = parts_of("first_place", (P, 2, CT * H * DH))
        o = o.rearrange("p b (h e) -> p b h e", e=DH)
        (bias_half,) = parts_of("first_place", (1, 3 * D))
        bias_half = bias_half.bitcast(F16).rearrange("p (v n) -> p v n", v=2)
        bq, pr = parts_of("second_place", (1, 3 * D), (P, T, 4 * H))
        (x2,) = parts_of("second_place", (P, 2, CT * D))
        x2 = x2.rearrange("p b (c d) -> p b c d", d=D)
        xn, eb, th, g1, g1T, xs = parts_of("third_place", (P, 2, D), (P, 2, 2 * D), (P, 2, R), (P, 2, R), (P, 2, P), (P, 2 * D))
        xs = xs.bitcast(F16).rearrange("p (b n) -> p b n", b=2)
        osq, x2T, keep, ls, ex, pb, tmp, selsum, tot, inc, sel2 = parts_of(
            "third_place", (P, CT * H, DH), (DC, CT, 2 * P), (P, E, T), (P, T, E), (P, T, E), (P, T, E), (P, T, E), (P, T, E), (P, E, T), (P, E, T), (P, 2 * T * E))
        sel2 = sel2.rearrange("p (k t e) -> p k t e", k=2, e=E)
        x2T = x2T.rearrange("p b (c n) -> p b c n", n=P)
        wv, pjb = parts_of("fourth_place", (NP1, D), (1, D))
        (passed,) = parts_of("fourth_place", (1, NSP, E))
        ident = sb("ident", [P, P])
        ident16 = sb("ident16", [P, P], F16)
        causal = sb("causal", [P, P])
        before = sb("before", [P, P])
        ones = sb("ones", [P, P])
        headmask = sb("headmask", [P, G, HG, VE])
        ln_fs = sb("ln_fs", [P, 1])
        qkT = sb("qkT", [P, 2, G * P])
        qT, kT = (qkT[:, i, :].bitcast(F16).rearrange("p (b n) -> p b n", b=2) for i in range(2))
        xp1 = qkT[:].rearrange("p a n -> p (a n)")[0:NP1, 0:B * NI]
        early = sb("early", [P, 2 * STG])
        stage = early[:].rearrange("p (b n) -> p b n", b=2)
        atm = sb("atm", [P, HG, G, P])
        cwb = sb("cwb", [DC, 2, NP1])
        unit = sb("unit", [1, NP1])
        axt = sb("axt", [KD, 3, NP1])
        mt = sb("mt", [NP1, NP1])
        at_half = sb("at_half", [P, 2, HG, G, P], F16)
        wq = at_half[:].rearrange("p v i g l -> p (v i g l)").bitcast(F32)[:, 0:2 * (3 * D + R)].rearrange("p (c n) -> p c n", c=2)
        gsb = atm[:].rearrange("p i g l -> p (i g l)")[0:NP1, 0:B * NI]
        prob = early[:, 0:2 * IT * NI].rearrange("p (b n m) -> p b n m", b=2, n=IT)
        probT = early[:, 2 * IT * NI:4 * IT * NI].rearrange("p (b n m) -> p b n m", b=2, n=IT)
        vs = early[:, 4 * IT * NI:4 * IT * NI + B * IT * D].rearrange("p (t d) -> p t d", d=D)
        nmax = sb("nmax", [P, B * IT])
        nbias = sb("nbias", [P, B * IT])
        rsum = sb("rsum", [P, B * IT])
        rinv = sb("rinv", [P, B * IT])
        h = sb("h", [P, T, D])
        w_half = sb("w_half", [P, 2, 2, 3 * D + R], F16)
        lnw = sb("lnw", [P, 2])
        lnb = sb("lnb", [P, 2])
        wb2 = sb("wb2", [R, 4 * H])
        wp = sb("wp", [DC + 1, 2, D])
        mnw = sb("mnw", [DC, 1])
        mnb = sb("mnb", [DC, 1])
        bp = sb("bp", [DC + 1, D])
        temp = sb("temp", [P, 1])
        htemp = sb("htemp", [P, 1])
        stat = sb("stat", [P, T, 6])
        mv = sb("mv", [P, T, 2])
        nwt = sb("nwt", [P, 6, CT * H])
        r12 = sb("r12", [P, T])
        nmr = sb("nmr", [P, T])
        sh = sb("sh", [P, T])
        xT = atm[:].rearrange("p i g l -> p (i g l)")[:, B * NI:B * NI + 4 * P].bitcast(F16).rearrange("p (b c n) -> p b c n", b=2, c=4)
        qk = sb("qk", [P, T, 2 * H, 4, DH], F16)
        ga = sb("ga", [P, T, 2 * H])
        gb = sb("gb", [P, T, 2 * H])
        gc = sb("gc", [P, T, H])
        gd = sb("gd", [P, T, H])
        gate1 = sb("gate1", [P, T, H])
        v32 = sb("v32", [P, T * H, DH])
        vg = sb("vg", [P, T * H, 2, VE], F16)
        state = sb("state", [P, G * HG * VE])
        st_half = sb("st_half", [P, 2, 2, G * HG * VE], F16)
        rden = sb("rden", [P, 2, H])
        osum = sb("osum", [P, CT * H])
        oT = sb("oT", [DC + 1, CT, 2, P])
        xr = sb("xr", [P, 2 * CT, 2 * D], F16)
        wr = sb("wr", [DC, 2, E])
        lg = sb("lg", [P, T, E])
        wx = sb("wx", [P, E * XW], F16)
        by_expert = wx[:].rearrange("p (e c) -> p e c", c=XW)
        iota_e = sb("iota_e", [P, E])
        iota_p = sb("iota_p", [P, P])
        iota_p16 = sb("iota_p16", [P, P], F16)
        row1 = sb("row1", [P, 1])
        choice1 = sb("choice1", [P, 2 * T])
        sel = sb("sel", [P, 2, T, E])
        small = sb("small", [P, 10, T])
        cnt = sb("cnt", [P, 4, E])
        cnti = sb("cnti", [P, E], I32)
        slot = sb("slot", [P, 2, T])
        sloti = sb("sloti", [P, 3, 2 * T], I32)
        slotf = sb("slotf", [P, 2, 2 * T])
        late = qk[:].rearrange("p t h s e -> p (t h s e)").bitcast(F32)
        at = [0]

        def carve(words):
            at[0] += words
            return late[:, at[0] - words:at[0]]

        cola = carve(T * P).bitcast(F16).rearrange("p (n c) -> p n c", c=P)
        cole = carve(2 * T * NSP).rearrange("p (n c) -> p n c", c=NSP)
        colb = carve(2 * T * NSP).bitcast(F16).rearrange("p (n v c) -> p n v c", v=2, c=NSP)
        src = sb("src", [P, 4, NSP])
        dst_row = sb("dst_row", [P, NSP], U32)
        tok_row = sb("tok_row", [P, NSP], U32)
        expf = sb("expf", [1, NSP])
        pow8 = sb("pow8", [1, WIN])
        packf = sb("packf", [1, len(WINDOWS), WIN])
        packs = sb("packs", [1, len(WINDOWS), 2])
        packi = sb("packi", [1, len(WINDOWS), 2], I32)
        expert = sb("expert", [1, len(WINDOWS)], I32)
        imp = sb("imp", [P, E])
        gate = sb("gate", [P, 2, T])
        xg = carve(4 * D).bitcast(F16).rearrange("p (k c) -> p k c", k=4)
        xe = carve(3 * P).bitcast(F16).rearrange("p (k c) -> p k c", k=2)
        act32 = carve(2 * FI).rearrange("p (k c) -> p k c", k=2)
        acth = carve(FI).bitcast(F16).rearrange("p (k c) -> p k c", k=2)
        actl = carve(FI).bitcast(F16).rearrange("p (k c) -> p k c", k=2)
        actT = carve(2 * FI).bitcast(F16).rearrange("p (k v n) -> p k v n", k=2, v=2)
        ye = carve(4 * D).rearrange("p (k c) -> p k c", k=4)

        s_tok_loaded = sem("tok_loaded")
        s_img_loaded = sem("img_loaded")
        s_txt_loaded = sem("txt_loaded")
        s_attn_loaded = sem("attn_loaded")
        s_const_ready = sem("const_ready")
        s_pool_step = sem("pool_step")
        s_axt_mm = sem("axt_mm")
        s_axt_ready = sem("axt_ready")
        s_setup_mm = sem("setup_mm")
        s_mt_ready = sem("mt_ready")
        s_wv_ready = sem("wv_ready")
        s_lnb_mm = sem("lnb_mm")
        s_mnb_mm = sem("mnb_mm")
        s_wq_ready = sem("wq_ready")
        s_wp_ready = sem("wp_ready")
        s_step = sem("step")
        s_ones_ready = sem("ones_ready")
        s_g_mm = sem("g_mm")
        s_g_ready = sem("g_ready")
        s_vp_mm = sem("vp_mm")
        s_vp_ready = sem("vp_ready")
        s_score_mm = sem("score_mm")
        s_nbias_ready = sem("nbias_ready")
        s_prob_ready = sem("prob_ready")
        s_rinv_ready = sem("rinv_ready")
        s_pT_mm = sem("pT_mm")
        s_pT_ready = sem("pT_ready")
        s_himg_mm = sem("himg_mm")
        s_himg_ready = sem("himg_ready")
        s_wqhigh_ready = sem("wqhigh_ready")
        s_wqlow_ready = sem("wqlow_ready")
        s_biaslow_ready = sem("biaslow_ready")
        s_bias_placed = sem("bias_placed")
        s_xn_ready = sem("xn_ready")
        s_xhigh_ready = sem("xhigh_ready")
        s_xlow_ready = sem("xlow_ready")
        s_xT_mm = sem("xT_mm")
        s_xT_ready = sem("xT_ready")
        s_qk_mm = sem("qk_mm")
        s_vb_mm = sem("vb_mm")
        s_exp_ready = sem("exp_ready")
        s_f32_ready = sem("f32_ready")
        s_fhigh_ready = sem("fhigh_ready")
        s_qlow_ready = sem("qlow_ready")
        s_klow_ready = sem("klow_ready")
        s_tanh_ready = sem("tanh_ready")
        s_v_ready = sem("v_ready")
        s_g1_ready = sem("g1_ready")
        s_gT_mm = sem("gT_mm")
        s_gT_ready = sem("gT_ready")
        s_pr_mm = sem("pr_mm")
        s_pr_ready = sem("pr_ready")
        s_ga_ready = sem("ga_ready")
        s_dph_ready = sem("dph_ready")
        s_sin_ready = sem("sin_ready")
        s_cos_ready = sem("cos_ready")
        s_gate_tanh = sem("gate_tanh")
        s_gated = sem("gated")
        s_vhigh_ready = sem("vhigh_ready")
        s_vg_ready = sem("vg_ready")
        s_t0_full = sem("t0_full")
        s_t0_free = sem("t0_free")
        s_t1_full = sem("t1_full")
        s_t1_free = sem("t1_free")
        s_at_mm = sem("at_mm")
        s_mask_done = sem("mask_done")
        s_athigh_ready = sem("athigh_ready")
        s_atlow_ready = sem("atlow_ready")
        s_state_mm = sem("state_mm")
        s_state32 = sem("state32")
        s_sthigh_ready = sem("sthigh_ready")
        s_state_ready = sem("state_ready")
        s_num_mm = sem("num_mm")
        s_o_ready = sem("o_ready")
        s_ohat_ready = sem("ohat_ready")
        s_x2_ready = sem("x2_ready")
        s_last_oT_mm = sem("last_oT_mm")
        s_last_oT = sem("last_oT")
        s_last_proj = sem("last_proj")
        s_last_xT_mm = sem("last_xT_mm")
        s_last_xT = sem("last_xT")
        s_last_route = sem("last_route")
        s_last_logits = sem("last_logits")
        s_xhi_ready = sem("xhi_ready")
        s_xlo_ready = sem("xlo_ready")
        s_x2_stored = [sem(f"x2_stored{i}") for i in range(2)]
        s_w_loaded = [sem(f"w_loaded{i}") for i in range(2)]
        s_w_scaled = sem("w_scaled")
        s_w_high = sem("w_high")
        s_w_low = sem("w_low")
        s_iota_ready = sem("iota_ready")
        s_ls_ready = sem("ls_ready")
        s_ex_ready = sem("ex_ready")
        s_pb_ready = sem("pb_ready")
        s_sel_ready = sem("sel_ready")
        s_rank_mm = sem("rank_mm")
        s_imp_mm = sem("imp_mm")
        s_slot_ready = sem("slot_ready")
        s_onehot_ready = sem("onehot_ready")
        s_imp_ready = sem("imp_ready")
        s_src_mm = sem("src_mm")
        s_rows_ready = sem("rows_ready")
        s_expert_ready = sem("expert_ready")
        s_xg_clear = sem("xg_clear")
        s_gathered = [sem(f"gathered{i}") for i in range(4)]
        s_scattered = [sem(f"scattered{i}") for i in range(4)]
        s_xe_mm = sem("xe_mm")
        s_xe_ready = sem("xe_ready")
        s_up_mm = sem("up_mm")
        s_act_ready = sem("act_ready")
        s_high_ready = sem("high_ready")
        s_low_ready = sem("low_ready")
        s_actT_mm = sem("actT_mm")
        s_actT_high = sem("actT_high")
        s_actT_low = sem("actT_low")
        s_down_mm = sem("down_mm")
        s_y_ready = sem("y_ready")
        s_y_loaded = [[sem(f"y{k}_loaded{b}") for b in range(B)] for k in range(2)]
        s_gate_ready = sem("gate_ready")
        s_first_scaled = sem("first_scaled")
        s_first_added = sem("first_added")
        s_sum_ready = sem("sum_ready")
        s_out_done = sem("out_done")

        PT = T - CT
        route_at = {CT * b + 8: b for b in range(B - 2)}
        misc = [("tr", 0), ("tr", 1)]
        for t in range(T + 1):
            misc += [("o", t - 4)] * (0 <= t - 4 < PT) + [(k, route_at.get(t)) for k in "xr" if t in route_at] + [("tr", t + 2)] * (t + 2 < T)
        use = {k: n for n, k in enumerate(misc)}

        parts = {"w1a": (FI, P, W1H, W1L), "w1b": (FI, D - P, W1BH, W1BL), "w2": (MC * D, P, W2H, W2L)}
        jobs = [(k, e0) for k in parts for e0 in range(0, E, STG // parts[k][0])]
        loads = [sum(2 if k == "w1b" else 1 for k, _ in jobs[n % 2:n + 1:2]) for n in range(len(jobs))]

        def staged(n, rows=P):
            kind, e0 = jobs[n]
            width, low_rows, high, low = parts[kind]
            ne = STG // width
            return (stage[0:rows, n % 2, 0:ne * width].rearrange("p (e c) -> p e c", c=width),
                    by_expert[0:rows, e0:e0 + ne, high:high + width], by_expert[0:rows, e0:e0 + ne, low:low + width])

        def twice(t, n):
            return eb[:, t % 2, n * D:(n + 1) * D].rearrange("p (h e) -> p h e", e=DH).unsqueeze(2).broadcast_to([P, H, 2, DH])

        def half_of(t, n, low):
            heads = qk[:, t, n * H:(n + 1) * H]
            if n == 0:
                return heads[:, :, 2 * low:2 * low + 2, :]
            return heads.rearrange("p h (a b) e -> p h a b e", b=2)[:, :, :, low, :]

        yt = [v[:, 0:T * D].rearrange("p (t d) -> p t d", t=T) for v in (v32[:].rearrange("p t e -> p (t e)"), late)]

        block = ctx.enter_context(nc.Block())

        @block.sync
        def _(sp):
            for dst, src in ((cwb, A["cwb"]), (wtok, A["wtok"]), (btok, A["btok"]), (unit, A["unit"]), (pjt, A["pjt"]), (pjb, A["pjb"])):
                sp.dma_start(dst[:], src).then_inc(s_tok_loaded, 16)
            sp.dma_start(xp1, A["xp1"]).then_inc(s_img_loaded, 16)
            for b in range(B):
                sp.dma_start(h[:, CT * b + IT, :], A["txt"][b]).then_inc(s_txt_loaded, 16)
            for dst, src_ in ((wq, A["wq"]), (lnw[:], A["lnw"]), (lnb[:], A["lnb"]), (bq, A["bqkv"]),
                             (wb2[:], A["wb2"]), (wp[0:DC, :, :], A["wp"]), (mnw[:], A["mnw"]), (mnb[:], A["mnb"]),
                             (bp[DC:DC + 1, :], A["bproj"]), (temp[:], A["temp"]), (wr[:], A["wr"])):
                sp.dma_start(dst, src_).then_inc(s_attn_loaded, 16)
            sp.wait_ge(s_wqhigh_ready, 2)
            sp.wait_ge(s_biaslow_ready, 1)
            for v in range(2):
                sp.dma_start(w_half[D - P + v:D - P + v + 1, 1, 1, 0:3 * D], bias_half[:, v, :]).then_inc(s_bias_placed, 16)
            sp.wait_ge(s_himg_mm, B)
            for n, (kind, e0) in enumerate(jobs):
                if n >= 2:
                    sp.wait_ge(s_w_low, n - 1)
                width = parts[kind][0]
                cols = STG // width * width
                w = A[kind][:, e0 * width:e0 * width + cols]
                if kind == "w1b":
                    for r in range(2):
                        sp.dma_start(stage[r * 64:(r + 1) * 64, n % 2, 0:cols], w).then_inc(s_w_loaded[n % 2], 16)
                else:
                    sp.dma_start(stage[:, n % 2, 0:cols], w).then_inc(s_w_loaded[n % 2], 16)
            for t in range(T):
                sp.wait_ge(s_xhi_ready, 2 * (t + 1))
                sp.wait_ge(s_xlo_ready, 2 * (t + 1))
                sp.dma_start(x2_dram[t * P:(t + 1) * P, :], xr[:, t % (2 * CT), :]).then_inc(s_x2_stored[t // CT % 2], 16)
            for k in range(4):
                sp.wait_ge(s_scattered[k], 16 * len(range(k, NS, 4)))
            for b in range(B):
                for k in range(2):
                    r0 = k * NTOK + b * CT * P
                    sp.dma_start(yt[k][:, b * CT:(b + 1) * CT, :], y_dram[r0:r0 + CT * P, :].rearrange("(c p) d -> p c d", p=P)).then_inc(s_y_loaded[k][b], 16)
            for i, b in enumerate(SUM_ORDER):
                sp.wait_ge(s_sum_ready, (i + 1) * CT)
                sp.dma_start(out[b].rearrange("(c p) d -> p c d", p=P), h[:, b * CT:(b + 1) * CT, :]).then_inc(s_out_done, 16)
            sp.wait_ge(s_out_done, 16 * B)

        @block.gpsimd
        def _(pool):
            step = [0]

            def link(ins):
                step[0] += 1
                ins.then_inc(s_pool_step, 1)
                pool.wait_ge(s_pool_step, step[0])

            pool.memset(ident[:], 0.0).then_inc(s_pool_step, 1)
            pool.memset(ident16[:], 0.0).then_inc(s_pool_step, 1)
            pool.memset(causal[:], FS ** -2).then_inc(s_pool_step, 1)
            pool.memset(before[:], 1.0).then_inc(s_pool_step, 1)
            pool.memset(headmask[:], FS ** -2).then_inc(s_pool_step, 1)
            pool.memset(ln_fs[:], log(FS)).then_inc(s_pool_step, 1)
            step[0] = 6
            pool.wait_ge(s_pool_step, 6)
            for m in (ident, ident16):
                pool.affine_select(out=m[:], in_=m[:], compare_op=ALU.not_equal, fill=1.0, base=0,
                                   pattern=[[-1, P]], channel_multiplier=1).then_inc(s_const_ready, 1)
            pool.affine_select(out=causal[:], in_=causal[:], compare_op=ALU.is_ge, fill=0.0, base=0,
                               pattern=[[1, P]], channel_multiplier=-1).then_inc(s_const_ready, 1)
            pool.affine_select(out=before[:], in_=before[:], compare_op=ALU.is_ge, fill=0.0, base=-1,
                               pattern=[[1, P]], channel_multiplier=-1).then_inc(s_const_ready, 1)
            link(pool.affine_select(out=headmask[:], in_=headmask[:], compare_op=ALU.is_ge, fill=0.0, base=0,
                                    pattern=[[0, G], [-SLOT, HG], [0, VE]], channel_multiplier=1))
            pool.affine_select(out=headmask[:], in_=headmask[:], compare_op=ALU.is_ge, fill=0.0, base=SLOT - 1,
                               pattern=[[0, G], [SLOT, HG], [0, VE]], channel_multiplier=-1).then_inc(s_const_ready, 1)

            for dst, pattern, base, mul in ((iota_e, [[1, E]], -E, 0), (iota_p, [[1, P]], 0, 0), (iota_p16, [[1, P]], 0, 0),
                                            (row1, [[0, 1]], 1, 1), (choice1, [[1, 2 * T]], 1, 0)):
                pool.iota(dst[:], pattern, base=base, channel_multiplier=mul, allow_small_or_imprecise_dtypes=True).then_inc(s_iota_ready, 1)
            pool.wait_ge(s_wqhigh_ready, 2)
            pool.tensor_tensor(bias_half[:, 1, :], bq, bias_half[:, 0, :], ALU.subtract).then_inc(s_biaslow_ready, 1)
            pool.tensor_tensor(w_half[:, 1, 0, :], wq[:, 0, :], w_half[:, 0, 0, :], ALU.subtract).then_inc(s_wqlow_ready, 1)
            pool.tensor_tensor(w_half[0:D - P, 1, 1, :], wq[0:D - P, 1, :], w_half[0:D - P, 0, 1, :], ALU.subtract).then_inc(s_wqlow_ready, 1)

            def x_low(t):
                pool.wait_ge(s_xhigh_ready, 2 * (t + 1))
                pool.tensor_tensor(xs[:, t % 2, P:2 * P], xn[:, t % 2, 0:P], xs[:, t % 2, 0:P], ALU.subtract).then_inc(s_xlow_ready, 1)
                pool.tensor_tensor(xs[:, t % 2, P + D:2 * D], xn[:, t % 2, P:D], xs[:, t % 2, 2 * P:P + D], ALU.subtract).then_inc(s_xlow_ready, 1)

            x_low(0)
            x_low(1)
            for t in range(T):
                if t + 2 < T:
                    x_low(t + 2)
                pool.wait_ge(s_fhigh_ready, 2 * t + 2)
                pool.tensor_tensor(half_of(t, 1, 1), twice(t, 1), half_of(t, 1, 0), ALU.subtract).then_inc(s_klow_ready, 1)
            for n in range(len(jobs)):
                w, high, low = staged(n, parts[jobs[n][0]][1])
                pool.wait_ge(s_w_high, n + 1)
                pool.tensor_tensor(low, w, high, ALU.subtract).then_inc(s_w_low, 1)

            def gather(i):
                if i >= 4:
                    pool.wait_ge(s_xe_mm, i - 3)
                pool.indirect_dma_start(xg[:, i % 4, :], None, x2_dram, bass.IndirectOffsetOnAxis(ap=tok_row[:, i:i + 1], axis=0),
                                        bounds_check=NTOK - 1, oob_is_err=False).then_inc(s_gathered[i % 4], 16)

            def scatter(i):
                pool.wait_ge(s_y_ready, i + 1)
                pool.indirect_dma_start(y_dram, bass.IndirectOffsetOnAxis(ap=dst_row[:, i:i + 1], axis=0), ye[:, i % 4, :], None,
                                        bounds_check=2 * NTOK - 1, oob_is_err=False).then_inc(s_scattered[i % 4], 16)

            pool.wait_ge(s_rank_mm, 1)
            pool.memset(xg, 0.0).then_inc(s_xg_clear, 1)
            pool.wait_ge(s_xg_clear, 1)
            for k in range(2):
                pool.wait_ge(s_x2_stored[k], 16 * T // 2)
            pool.wait_ge(s_rows_ready, 2)
            for i in range(4):
                gather(i)
            for i in range(NS + 3):
                if i + 4 < NSP:
                    gather(i + 4)
                if i >= 3:
                    scatter(i - 3)
            for i, b in enumerate(SUM_SHARED):
                pool.wait_ge(s_first_scaled, (i + 1) * CT)
                pool.tensor_tensor(h[:, b * CT:(b + 1) * CT, :], h[:, b * CT:(b + 1) * CT, :], yt[0][:, b * CT:(b + 1) * CT, :],
                                   ALU.add).then_inc(s_first_added, 1)

        @block.tensor
        def _(pe):
            pe.wait_ge(s_tok_loaded, 96)
            for i in range(3):
                w = slice(i * KD, (i + 1) * KD)
                o_ = bank[0][0:KD, i * NP1:(i + 1) * NP1]
                pe.matmul(o_, wtok[:, 0, w], cwb[:, 0, :], start=True, stop=False)
                pe.matmul(o_, wtok[:, 1, w], cwb[:, 1, :], start=False, stop=False)
                mm = pe.matmul(o_, btok[:, w], unit[:], start=False, stop=True)
            mm.then_inc(s_axt_mm, 1)
            pe.wait_ge(s_axt_ready, 1)
            pe.matmul(bank[1][0:NP1, 0:NP1], axt[:, 1, :], axt[:, 0, :], start=True, stop=True).then_inc(s_setup_mm, 1)
            pe.matmul(bank[2][0:NP1, 0:D], axt[:, 2, :], pjt, start=True, stop=False)
            pe.matmul(bank[2][0:NP1, 0:D], unit[:], pjb, start=False, stop=True).then_inc(s_setup_mm, 1)
            pe.wait_ge(s_img_loaded, 16)
            pe.wait_ge(s_mt_ready, 1)
            for i in range(2):
                if i:
                    pe.wait_ge(s_g_ready, i)
                pe.matmul(bank[7][0:NP1, :], mt[:], xp1[:, i * 512:(i + 1) * 512], start=True, stop=True).then_inc(s_g_mm, 1)

            def scores(b):
                pe.wait_ge(s_g_ready, b // 2 + 1)
                if b >= 2:
                    pe.wait_ge(s_prob_ready, IT * (b - 1))
                else:
                    pe.wait_ge(s_axt_ready, 1)
                    pe.wait_ge(s_mt_ready, 1)
                for n in range(IT):
                    q0 = b * NI + n * P
                    mm = pe.matmul(bank[b % 2][:, n * NI:(n + 1) * NI], xp1[:, q0:q0 + P], gsb[:, b * NI:(b + 1) * NI], start=True, stop=True)
                mm.then_inc(s_score_mm, 1)

            def values(i):
                pe.wait_ge(s_wv_ready, 1)
                if i >= 2:
                    pe.wait_ge(s_vp_ready, i - 1)
                for n in range(IT):
                    m0 = (i * IT + n) * P
                    mm = pe.matmul(bank[5 + i % 2][:, n * D:(n + 1) * D], xp1[:, m0:m0 + P], wv, start=True, stop=True)
                mm.then_inc(s_vp_mm, 1)

            def prob_t(b):
                pe.wait_ge(s_prob_ready, IT * (b + 1))
                if b == 0:
                    pe.wait_ge(s_const_ready, 5)
                    pe.wait_ge(s_wv_ready, 1)
                if b >= 2:
                    pe.wait_ge(s_pT_ready, b - 1)
                for n in range(IT):
                    for j in range(IT):
                        mm = pe.transpose(bank[2 + b % 2][:, j * NI + n * P:j * NI + (n + 1) * P], prob[:, b % 2, n, j * P:(j + 1) * P], ident[:])
                mm.then_inc(s_pT_mm, 1)

            def himg(b):
                pe.wait_ge(s_pT_ready, b + 1)
                if b == 0:
                    pe.wait_ge(s_vp_ready, B)
                if b >= 2:
                    pe.wait_ge(s_himg_ready, IT * (b - 1))
                for n in range(IT):
                    for j in range(IT):
                        mm = pe.matmul(bank[5 + b % 2][:, n * D:(n + 1) * D], probT[:, b % 2, j, n * P:(n + 1) * P], vs[:, b * IT + j, :],
                                       start=(j == 0), stop=(j == IT - 1))
                mm.then_inc(s_himg_mm, 1)

            scores(0)
            scores(1)
            for i in range(B):
                values(i)
            prob_t(0)
            pe.wait_ge(s_attn_loaded, 16 * 11)
            pe.wait_ge(s_g_ready, 2)
            for lo, hi, bk in ((0, 512, 4), (512, 3 * D, 7)):
                for c in range(2):
                    rows = P if c == 0 else D - P
                    mm = pe.matmul(bank[bk][0:1, 0:hi - lo], lnb[0:rows, c:c + 1], wq[0:rows, c, lo:hi], start=(c == 0), stop=(c == 1))
            mm.then_inc(s_lnb_mm, 1)
            for c in range(2):
                mm = pe.matmul(bank[3][DC:DC + 1, 0:D], mnb[:, 0:1], wp[0:DC, c, :], start=(c == 0), stop=(c == 1))
            mm.then_inc(s_mnb_mm, 1)
            himg(0)
            for b in range(1, B):
                if b + 1 < B:
                    scores(b + 1)
                if b == 1:
                    pe.wait_ge(s_wp_ready, 1)
                prob_t(b)
                himg(b)

            def x_t(t):
                pe.wait_ge(s_xlow_ready, 2 * (t + 1))
                if t >= 2:
                    pe.wait_ge(s_xT_ready, t - 1)
                else:
                    pe.wait_ge(s_prob_ready, B * IT)
                ps = bank[t % 2][:, 0:3 * P // 2].bitcast(F16)
                for j in range(3):
                    mm = pe.transpose(ps[:, j * P:(j + 1) * P], xs[:, t % 2, j * P:(j + 1) * P], ident16[:])
                mm.then_inc(s_xT_mm, 1)

            def projected(out_, t, c0, c1):
                x_, w = xT[:, t % 2], w_half[:, :, :, c0:c1]
                pe.matmul(out_, x_[:, 0], w[:, 0, 0], start=True, stop=False)
                pe.matmul(out_, x_[:, 1], w[:, 0, 0], start=False, stop=False)
                pe.matmul(out_, x_[:, 0], w[:, 1, 0], start=False, stop=False)
                pe.matmul(out_, x_[:, 2], w[:, 0, 1], start=False, stop=False)
                return pe.matmul(out_, x_[0:D - P + 2, 3], w[0:D - P + 2, 1, 1], start=False, stop=True)

            def queries_keys(t):
                pe.wait_ge(s_xT_ready, t + 1)
                if t == 0:
                    pe.wait_ge(s_wqlow_ready, 2)
                    pe.wait_ge(s_bias_placed, 32)
                    pe.wait_ge(s_ones_ready, 4)
                    pe.wait_ge(s_pT_ready, B)
                    pe.wait_ge(s_himg_ready, B * IT)
                if t >= 2:
                    pe.wait_ge(s_f32_ready, t - 1)
                projected(bank[2 + t % 2][:, 0:2 * D], t, 0, 2 * D).then_inc(s_qk_mm, 1)

            def values_hidden(t):
                if t >= 2:
                    pe.wait_ge(s_v_ready, t - 1)
                    pe.wait_ge(s_g1_ready, t - 1)
                projected(bank[4 + t % 2][:, 0:D + R], t, 2 * D, 3 * D + R).then_inc(s_vb_mm, 1)

            def hidden_t(t):
                pe.wait_ge(s_g1_ready, t + 1)
                if t >= 1:
                    pe.wait_ge(s_gT_ready, t)
                pe.transpose(bank[6][:, 0:P], g1[:, t % 2, :], ident[:]).then_inc(s_gT_mm, 1)

            def params(t):
                pe.wait_ge(s_gT_ready, t + 1)
                if t >= 1:
                    pe.wait_ge(s_pr_ready, t)
                pe.matmul(bank[7][:, 0:4 * H], g1T[:, t % 2, :], wb2[:], start=True, stop=True).then_inc(s_pr_mm, 1)

            x_t(0)
            for t in range(T + 2):
                if t < T:
                    queries_keys(t)
                    if t + 1 < T:
                        x_t(t + 1)
                    values_hidden(t)
                if 1 <= t <= T:
                    hidden_t(t - 1)
                if t >= 2:
                    params(t - 2)

            def take(u):
                if u == 0:
                    pe.wait_ge(s_xT_ready, T)
                else:
                    pe.wait_ge(s_t0_free, u)
                    pe.wait_ge(s_t1_free, u)

            def heads_t(t):
                u = use["tr", t]
                take(u)
                pe.wait_ge(s_qlow_ready, t + 1)
                pe.wait_ge(s_klow_ready, t + 1)
                for half, full in ((0, s_t0_full), (1, s_t1_full)):
                    for g in range(G):
                        h0 = half * H + g * HG
                        mm = pe.transpose(bank[half][:, 0:G * P // 2].bitcast(F16)[:, g * P:(g + 1) * P], qk[:, t, h0:h0 + HG].rearrange("p h s e -> p (h s e)"), ident16[:])
                    mm.then_inc(full, 1)

            def scores_of(i, n):
                return bank[2 + 2 * i + n]

            def qk_products(t):
                pe.wait_ge(s_t0_free, use["tr", t] + 1)
                pe.wait_ge(s_t1_free, use["tr", t] + 1)
                if t:
                    pe.wait_ge(s_mask_done, 4 * t)
                else:
                    pe.wait_ge(s_f32_ready, T)
                    pe.wait_ge(s_g1_ready, T)
                    pe.wait_ge(s_v_ready, T)
                for g in range(G):
                    for i in range(HG):
                        r = slice(SLOT * i, SLOT * (i + 1))
                        mm = pe.matmul(scores_of(i, g // GB)[:, g % GB * P:(g % GB + 1) * P], kT[r, t % 2, g * P:(g + 1) * P], qT[r, t % 2, g * P:(g + 1) * P],
                                       start=True, stop=True, tile_position=(SLOT * i, 0))
                mm.then_inc(s_at_mm, 1)

            def state_step(t):
                b, c = divmod(t, CT)
                pe.wait_ge(s_vg_ready, b + 1)
                if t == 0:
                    pe.wait_ge(s_pr_ready, T)
                else:
                    pe.wait_ge(s_state32, b * 2 + c)
                for g in range(G):
                    for v in range(2):
                        mm = pe.matmul(bank[7][:, g * HG * VE:(g + 1) * HG * VE],
                                       qk[:, t, H + g * HG:H + (g + 1) * HG].rearrange("p h s e -> p (h s e)"),
                                       vg[:, t * H + g * HG:t * H + (g + 1) * HG, v, :],
                                       start=(c == 0 and g == 0 and v == 0), stop=(c == 1 and g == G - 1 and v == 1), skip_group_check=True)
                mm.then_inc(s_state_mm, 1)

            def numerators(t):
                b, c = divmod(t, CT)
                if t == 0:
                    pe.wait_ge(s_gT_ready, T)
                else:
                    pe.wait_ge(s_o_ready, t)
                if c:
                    pe.wait_ge(s_state_ready, 2 * b + c)
                    for g in range(G):
                        w = slice(g * HG * VE, (g + 1) * HG * VE)
                        for v in range(2):
                            pe.matmul(bank[6][:, w], qT[:, t % 2, g * P:(g + 1) * P], st_half[:, (t - 1) % 2, v, w],
                                      start=(g == 0 and v == 0), stop=False, skip_group_check=True)
                pe.wait_ge(s_atlow_ready, 4 * (t + 1))
                for hh in range(H):
                    g, i = divmod(hh, HG)
                    for a_, v in ((0, 0), (0, 1), (1, 0)):
                        mm = pe.matmul(bank[6][:, hh * VE:(hh + 1) * VE], at_half[:, a_, i, g, :], vg[:, t * H + hh, v, :],
                                       start=(c == 0 and hh == 0 and a_ == 0 and v == 0), stop=(hh == H - 1 and a_ == 1), skip_group_check=True)
                mm.then_inc(s_num_mm, 1)

            def outputs_t(t):
                b, c = divmod(t, CT)
                u = use["o", t]
                take(u)
                pe.wait_ge(s_ohat_ready, b + 1)
                for j in range(2):
                    mm = pe.transpose(bank[0][0:DC, j * P:(j + 1) * P],
                                      o[:, b % 2, c * H:(c + 1) * H, :].rearrange("p h e -> p (h e)")[:, j * DC:(j + 1) * DC], ident[:])
                mm.then_inc(s_t0_full, 1)

            def project(t):
                u = use["o", t]
                pe.wait_ge(s_t0_free, u + 1)
                if t == 0:
                    pe.wait_ge(s_wp_ready, 3)
                for j in range(2):
                    mm = pe.matmul(bank[1][:, 0:D], oT[0:DC + j, u % 2, j, :], wp[0:DC + j, j, :], start=(j == 0), stop=(j == 1))
                mm.then_inc(s_t1_full, 1)

            def route(b):
                take(use["x", b])
                pe.wait_ge(s_x2_ready, (b + 1) * CT)
                for i in range(CT):
                    for j in range(2):
                        c0 = i % 2 * 2 * P + j * P
                        mm = pe.transpose(bank[i // 2][0:DC, c0:c0 + P], x2[:, b % 2, i, j * DC:(j + 1) * DC], ident[:])
                    if i:
                        mm.then_inc((s_t0_full, s_t1_full)[i - 1], 1)
                take(use["r", b])
                for i in range(CT):
                    for j in range(2):
                        mm = pe.matmul(bank[i // 2][:, i % 2 * E:(i % 2 + 1) * E], x2T[:, i, j, :], wr[:, j, :], start=(j == 0), stop=(j == 1))
                    if i:
                        mm.then_inc((s_t0_full, s_t1_full)[i - 1], 1)

            heads_t(0)
            qk_products(0)
            heads_t(1)
            state_step(0)
            for t in range(T + 1):
                if t < T:
                    numerators(t)
                if 0 <= t - 4 < PT:
                    outputs_t(t - 4)
                if t + 1 < T:
                    qk_products(t + 1)
                if 0 <= t - 4 < PT:
                    project(t - 4)
                if t + 1 < T and (t + 1) % CT < 2:
                    state_step(t + 1)
                if t in route_at:
                    route(route_at[t])
                if t + 2 < T:
                    heads_t(t + 2)

            def last_route(b):
                pe.wait_ge(s_x2_ready, (b + 1) * CT)
                n = 2 * (b - B + 2)
                if n == 0:
                    pe.wait_ge(s_o_ready, T)
                    pe.wait_ge(s_state32, 2 * B)
                b0 = 6 if n == 0 else 2
                for i in range(CT):
                    for j in range(2):
                        c0 = i % 2 * 2 * P + j * P
                        mm = pe.transpose(bank[b0 + i // 2][0:DC, c0:c0 + P], x2[:, b % 2, i, j * DC:(j + 1) * DC], ident[:])
                    if i:
                        mm.then_inc(s_last_xT_mm, 1)
                pe.wait_ge(s_last_xT, n + 2)
                for i in range(CT):
                    for j in range(2):
                        mm = pe.matmul(bank[n // 2][:, i * E:(i + 1) * E], x2T[:, i, j, :], wr[:, j, :], start=(j == 0), stop=(j == 1))
                mm.then_inc(s_last_route, 1)

            pe.wait_ge(s_ohat_ready, B)
            pe.wait_ge(s_mask_done, 4 * T)
            for i in range(CT):
                for j in range(2):
                    c0 = i % 2 * 2 * P + j * P
                    mm = pe.transpose(bank[2 + i // 2][0:DC, c0:c0 + P],
                                      o[:, (B - 1) % 2, i * H:(i + 1) * H, :].rearrange("p h e -> p (h e)")[:, j * DC:(j + 1) * DC], ident[:])
                if i:
                    mm.then_inc(s_last_oT_mm, 1)
            for i in range(CT):
                pe.wait_ge(s_last_oT, 1 + i // 2)
                for j in range(2):
                    mm = pe.matmul(bank[4 + i // 2][:, i % 2 * D:(i % 2 + 1) * D], oT[0:DC + j, i, j, :], wp[0:DC + j, j, :], start=(j == 0), stop=(j == 1))
                if i:
                    mm.then_inc(s_last_proj, 1)
            pe.wait_ge(s_t0_free, len(misc))
            pe.wait_ge(s_t1_free, len(misc))
            last_route(B - 2)
            last_route(B - 1)

            pe.wait_ge(s_sel_ready, 1)
            pe.wait_ge(s_ones_ready, 1)
            mv_ = selsum.rearrange("p t e -> p (t e)")
            pe.matmul(bank[0][:, 0:T * E], before[:], mv_, start=True, stop=True)
            pe.matmul(bank[0][:, T * E:2 * T * E], ones[:], mv_, start=True, stop=True).then_inc(s_rank_mm, 1)
            pe.wait_ge(s_onehot_ready, 2)
            for n in range(2 * T):
                mm = pe.matmul(bank[2][:, 0:2 * NSP], cola[:, n, :], colb[:, n, :, :].rearrange("p v j -> p (v j)"), start=(n == 0), stop=(n == 2 * T - 1))
            mm.then_inc(s_src_mm, 1)
            pe.wait_ge(s_pb_ready, 1)
            pe.matmul(bank[5][:, 0:T * E], ones[:], pb.rearrange("p t e -> p (t e)"), start=True, stop=True).then_inc(s_imp_mm, 1)

            def rows_t(i, k, rnd, first=False):
                pe.wait_ge(s_gathered[k], 16 * (rnd + 1))
                if not first:
                    pe.wait_ge(s_xe_ready, i - 1)
                ps = bank[k % 2][:, 0:3 * P // 2].bitcast(F16)
                for j in range(3):
                    mm = pe.transpose(ps[:, j * P:(j + 1) * P], xg[:, k, j * P:(j + 1) * P], ident16[:])
                mm.then_inc(s_xe_mm, 1)

            def weights(n, count=WIN):
                word = pe.value_load(expert[0:1, bass.ds(n, 1)], min_val=0, max_val=8 ** WIN - 1)
                return [wx[:, bass.ds(pe.snap(((word >> 3 * k) & 7) * XW), XW)] for k in range(count)]

            def up(i, k, w, first=False):
                pe.wait_ge(s_xe_ready, i + 1)
                if not first:
                    pe.wait_ge(s_high_ready, i - 1)
                k %= 2
                o_ = bank[2 + k][:, :]
                pe.matmul(o_, xe[:, k, 0:P], w[:, W1H:W1H + FI], start=True, stop=False)
                pe.matmul(o_, xe[:, k, P:2 * P], w[:, W1H:W1H + FI], start=False, stop=False)
                pe.matmul(o_, xe[:, k, 0:P], w[:, W1L:W1L + FI], start=False, stop=False)
                pe.matmul(o_, xe[:, k, 2 * P:3 * P], w[:, W1BH:W1BH + FI], start=False, stop=False)
                pe.matmul(o_, xe[0:D - P, k, 2 * P:3 * P], w[0:D - P, W1BL:W1BL + FI], start=False, stop=True).then_inc(s_up_mm, 1)

            def act_t(i, k, first=False):
                pe.wait_ge(s_low_ready, i + 1)
                if not first:
                    pe.wait_ge(s_actT_high, i)
                    pe.wait_ge(s_actT_low, i)
                k %= 2
                for v, half in enumerate((acth, actl)):
                    ps = bank[6 + v][:, 0:FI // 2].bitcast(F16)
                    for m in range(MC):
                        mm = pe.transpose(ps[:, m * P:(m + 1) * P], half[:, k, m * P:(m + 1) * P], ident16[:])
                mm.then_inc(s_actT_mm, 1)

            def down(i, k, w, first=False):
                pe.wait_ge(s_actT_high, i + 1)
                pe.wait_ge(s_actT_low, i + 1)
                if not first:
                    pe.wait_ge(s_y_ready, i - 1)
                k %= 2
                o_ = bank[4 + k][:, 0:D]
                for m in range(MC):
                    c = slice(m * P, (m + 1) * P)
                    d = m * D
                    pe.matmul(o_, actT[:, k, 0, c], w[:, W2H + d:W2H + d + D], start=(m == 0), stop=False)
                    pe.matmul(o_, actT[:, k, 1, c], w[:, W2H + d:W2H + d + D], start=False, stop=False)
                    mm = pe.matmul(o_, actT[:, k, 0, c], w[:, W2L + d:W2L + d + D], start=False, stop=(m == MC - 1))
                mm.then_inc(s_down_mm, 1)

            pe.wait_ge(s_w_low, len(jobs))
            pe.wait_ge(s_expert_ready, 1)
            rows_t(0, 0, 0, first=True)
            rows_t(1, 1, 0, first=True)
            w = weights(0, LEAD)
            up(0, 0, w[0], first=True)
            rows_t(2, 2, 0)
            up(1, 1, w[1], first=True)
            act_t(0, 0, first=True)
            for i in range(LAG, LEAD):
                rows_t(i + 1, (i + 1) % 4, (i + 1) // 4)
                up(i, i % 4, w[i])
                act_t(i - 1, i - 1)
                down(i - LAG, (i - LAG) % 4, w[i - LAG], first=(i < 4))
            with pe.Fori(0, (NS - LEAD) // STEP) as j:
                w = weights(j + 1)
                for k in range(LEAD, LEAD + STEP):
                    i = STEP * j + k
                    rows_t(i + 1, (k + 1) % 4, STEP // 4 * j + (k + 1) // 4)
                    up(i, k % 4, w[k - LEAD + LAG])
                    act_t(i - 1, k - 1)
                    down(i - LAG, (k - LAG) % 4, w[k - LEAD])
            act_t(NS - 1, NS - 1)
            w = weights(len(WINDOWS) - 1)
            for i in range(NS - LAG, NS):
                down(i, i % 4, w[i - WINDOWS[-1]])

        @block.scalar
        def _(act):
            act.wait_ge(s_setup_mm, 2)
            act.activation(wv, bank[2][0:NP1, 0:D], ACT.Copy).then_inc(s_wv_ready, 1)
            for i in range(2):
                act.wait_ge(s_g_mm, i + 1)
                act.activation(gsb[:, i * 512:(i + 1) * 512], bank[7][0:NP1, :], ACT.Copy).then_inc(s_g_ready, 1)
            for i in range(B):
                act.wait_ge(s_vp_mm, i + 1)
                act.activation(vs[:, i * IT:(i + 1) * IT, :].rearrange("p a d -> p (a d)"), bank[5 + i % 2][:, 0:IT * D], ACT.Copy).then_inc(s_vp_ready, 1)

            def softmax(b):
                act.wait_ge(s_nbias_ready, b + 1)
                if b >= 2:
                    act.wait_ge(s_pT_mm, b - 1)
                for n in range(IT):
                    i = b * IT + n
                    act.activation(prob[:, b % 2, n, :], bank[b % 2][:, n * NI:(n + 1) * NI], ACT.Exp, bias=nbias[:, i:i + 1],
                                   scale=KD ** -0.5, accum_out=rsum[:, i:i + 1]).then_inc(s_prob_ready, 1)

            def himg(b):
                act.wait_ge(s_himg_mm, b + 1)
                act.wait_ge(s_rinv_ready, b + 1)
                for n in range(IT):
                    i = b * IT + n
                    act.activation(h[:, b * CT + n, :], bank[5 + b % 2][:, n * D:(n + 1) * D], ACT.Copy, scale=rinv[:, i:i + 1]).then_inc(s_himg_ready, 1)

            softmax(0)
            softmax(1)
            for b in range(B):
                himg(b)
                if b + 2 < B:
                    softmax(b + 2)
                if b == 1:
                    act.wait_ge(s_wq_ready, 4)
                    act.activation(w_half[:, 0, :, :], wq, ACT.Copy).then_inc(s_wqhigh_ready, 1)
                    act.activation(bias_half[:, 0, :], bq, ACT.Copy).then_inc(s_wqhigh_ready, 1)

            def x_high(t):
                act.wait_ge(s_xn_ready, t + 1)
                if t >= 2:
                    act.wait_ge(s_xT_mm, t - 1)
                act.activation(xs[:, t % 2, 0:P], xn[:, t % 2, 0:P], ACT.Copy).then_inc(s_xhigh_ready, 1)
                act.activation(xs[:, t % 2, 2 * P:P + D], xn[:, t % 2, P:D], ACT.Copy).then_inc(s_xhigh_ready, 1)

            x_high(0)
            x_high(1)
            for t in range(T + 2):
                if t < T:
                    act.wait_ge(s_qk_mm, t + 1)
                    if t >= 2:
                        act.wait_ge(s_qlow_ready, t - 1)
                        act.wait_ge(s_klow_ready, t - 1)
                    act.activation(eb[:, t % 2, :], bank[2 + t % 2][:, 0:2 * D], ACT.Exp, bias=ln_fs[:, 0:1], scale=1.0 / FS).then_inc(s_exp_ready, 1)
                    if t + 2 < T:
                        x_high(t + 2)
                    act.wait_ge(s_vb_mm, t + 1)
                    if t >= 2:
                        act.wait_ge(s_g1_ready, t - 1)
                    act.activation(th[:, t % 2, :], bank[4 + t % 2][:, D:D + R], ACT.Tanh, scale=sh[:, t:t + 1]).then_inc(s_tanh_ready, 1)
                    act.activation(v32[:, t * H:(t + 1) * H, :], bank[4 + t % 2][:, 0:D].rearrange("p (h e) -> p h e", e=DH), ACT.Copy,
                                   scale=1.0 / VS).then_inc(s_v_ready, 1)
                    act.wait_ge(s_f32_ready, t + 1)
                    for n in range(2):
                        act.activation(half_of(t, n, 0), twice(t, n), ACT.Copy).then_inc(s_fhigh_ready, 1)
                if 1 <= t <= T:
                    act.wait_ge(s_gT_mm, t)
                    if t >= 3:
                        act.wait_ge(s_pr_mm, t - 2)
                    act.activation(g1T[:, (t - 1) % 2, :], bank[6][:, 0:P], ACT.Copy).then_inc(s_gT_ready, 1)
                if t >= 2:
                    act.wait_ge(s_pr_mm, t - 1)
                    act.activation(pr[:, t - 2, :], bank[7][:, 0:4 * H], ACT.Copy, scale=sh[:, t - 2:t - 1]).then_inc(s_pr_ready, 1)

            def heads_t(t):
                u = use["tr", t]
                if t >= 2:
                    act.wait_ge(s_at_mm, t - 1)
                    act.wait_ge(s_num_mm, t - 1)
                act.wait_ge(s_t0_full, u + 1)
                act.activation(qT[:, t % 2, :], bank[0][:, 0:G * P // 2].bitcast(F16), ACT.Copy).then_inc(s_t0_free, 1)
                act.wait_ge(s_t1_full, u + 1)
                act.activation(kT[:, t % 2, :], bank[1][:, 0:G * P // 2].bitcast(F16), ACT.Copy).then_inc(s_t1_free, 1)

            act.wait_ge(s_pr_ready, T)
            act.activation(ga[:], pr[:, :, 0:2 * H], ACT.Tanh, scale=0.5).then_inc(s_ga_ready, 1)
            act.activation(gb[:], pr[:, :, 2 * H:4 * H], ACT.Tanh).then_inc(s_ga_ready, 1)
            heads_t(0)
            act.wait_ge(s_dph_ready, 1)
            act.activation(gd[:], gc[:], ACT.Sin, scale=PI / 4).then_inc(s_sin_ready, 1)
            act.wait_ge(s_cos_ready, 1)
            act.activation(gd[:], gc[:], ACT.Tanh, scale=0.25).then_inc(s_gate_tanh, 1)
            act.wait_ge(s_gate_tanh, 1)
            act.activation(gate1[:], gd[:], ACT.Tanh, scale=htemp[:, 0:1]).then_inc(s_gate_tanh, 1)

            def values_high(b):
                act.wait_ge(s_gated, b + 1)
                act.activation(vg[:, b * CT * H:(b + 1) * CT * H, 0, 0:DH], v32[:, b * CT * H:(b + 1) * CT * H, :], ACT.Copy).then_inc(s_vhigh_ready, 1)

            def rows_high(b):
                for c in range(CT):
                    act.wait_ge(s_x2_ready, b * CT + c + 1)
                    if b >= 2:
                        act.wait_ge(s_x2_stored[b % 2], 16 * CT)
                    xrow = xr[:, b % 2 * CT + c, :]
                    act.activation(xrow[:, 0:P], x2[:, b % 2, c, 0:P], ACT.Copy).then_inc(s_xhi_ready, 1)
                    act.activation(xrow[:, 2 * P:P + D], x2[:, b % 2, c, P:D], ACT.Copy).then_inc(s_xhi_ready, 1)

            values_high(0)
            heads_t(1)
            for t in range(T + 1):
                if t < T:
                    for n in range(4):
                        act.wait_ge(s_mask_done, 4 * t + n + 1)
                        if t and n == 0:
                            act.wait_ge(s_num_mm, t)
                        i, g0 = n // 2, n % 2 * GB
                        act.activation(at_half[:, 0, i, g0:g0 + GB, :], atm[:, i, g0:g0 + GB, :], ACT.Copy).then_inc(s_athigh_ready, 1)
                    if t % CT < 2:
                        n = t // CT * 2 + t % CT
                        act.wait_ge(s_state32, n + 1)
                        act.activation(st_half[:, t % 2, 0, :], state[:], ACT.Copy).then_inc(s_sthigh_ready, 1)
                if 1 <= t and t + 1 < T:
                    heads_t(t + 1)
                if t < len(jobs):
                    w, high, _low = staged(t)
                    act.wait_ge(s_w_loaded[t % 2], 16 * loads[t])
                    act.activation(w, w, ACT.Copy, scale=WS).then_inc(s_w_scaled, 1)
                if 0 <= t - 4 < PT:
                    u = use["o", t - 4]
                    act.wait_ge(s_t0_full, u + 1)
                    act.activation(oT[0:DC, u % 2, :, :].rearrange("p c n -> p (c n)"), bank[0][0:DC, 0:2 * P], ACT.Copy).then_inc(s_t0_free, 1)
                if t < len(jobs):
                    act.wait_ge(s_w_scaled, t + 1)
                    act.activation(high, w, ACT.Copy).then_inc(s_w_high, 1)
                if t % CT == 1 and t // CT + 1 < B:
                    values_high(t // CT + 1)
                if t % CT == 1 and 0 <= (t - 7) // CT < B:
                    b = (t - 7) // CT
                    rows_high(b)
                if t in route_at:
                    rb = route_at[t]
                    u = use["x", rb]
                    for i, n, full, free in ((0, 2, s_t0_full, s_t0_free), (1, 1, s_t1_full, s_t1_free)):
                        act.wait_ge(full, u + 1)
                        act.activation(x2T[:, 2 * i:2 * i + n, :, :].rearrange("p b c n -> p (b c n)"), bank[i][0:DC, 0:n * 2 * P], ACT.Copy).then_inc(free, 1)
                    for i, n, full, free in ((0, 2, s_t0_full, s_t0_free), (1, 1, s_t1_full, s_t1_free)):
                        t0 = rb * CT + 2 * i
                        act.wait_ge(full, u + 2)
                        act.activation(lg[:, t0:t0 + n, :].rearrange("p t e -> p (t e)"), bank[i][:, 0:n * E], ACT.Copy).then_inc(free, 1)
            act.wait_ge(s_t1_full, len(misc))
            for i, w in ((0, 4 * P), (1, 2 * P)):
                act.wait_ge(s_last_oT_mm, i + 1)
                act.activation(oT[0:DC, 2 * i:2 * i + w // (2 * P), :, :].rearrange("p b c n -> p (b c n)"), bank[2 + i][0:DC, 0:w], ACT.Copy).then_inc(s_last_oT, 1)
            for b in range(B - 2, B):
                n = 2 * (b - B + 2)
                if n:
                    act.wait_ge(s_last_route, 1)
                for i, w in ((0, 4 * P), (1, 2 * P)):
                    act.wait_ge(s_last_xT_mm, n + i + 1)
                    act.activation(x2T[:, 2 * i:2 * i + w // (2 * P), :, :].rearrange("p b c n -> p (b c n)"),
                                   bank[(2 if n else 6) + i][0:DC, 0:w], ACT.Copy).then_inc(s_last_xT, 1)
                act.wait_ge(s_last_route, n // 2 + 1)
                act.activation(lg[:, b * CT:(b + 1) * CT, :].rearrange("p t e -> p (t e)"), bank[n // 2][:, 0:CT * E], ACT.Copy).then_inc(s_last_logits, 1)
                rows_high(b)
            act.wait_ge(s_ls_ready, 1)
            act.activation(ex, ls, ACT.Exp).then_inc(s_ex_ready, 1)

            def silu(i, k, first=False):
                act.wait_ge(s_up_mm, i + 1)
                if not first:
                    act.wait_ge(s_low_ready, i - 1)
                    act.wait_ge(s_actT_mm, i - 1)
                act.activation(act32[:, k, :], bank[2 + k][:, :], ACT.Silu, scale=1.0 / WS).then_inc(s_act_ready, 1)
                act.activation(acth[:, k, :], bank[2 + k][:, :], ACT.Silu, scale=1.0 / WS).then_inc(s_high_ready, 1)

            def high_t(i, k, first=False):
                act.wait_ge(s_actT_mm, i + 1)
                if not first:
                    act.wait_ge(s_down_mm, i - 1)
                act.activation(actT[:, k, 0, :], bank[6][:, 0:FI // 2].bitcast(F16), ACT.Copy).then_inc(s_actT_high, 1)

            silu(0, 0, first=True)
            for i in range(1, LEAD):
                silu(i, i % 2, first=(i < 2))
                high_t(i - 1, (i - 1) % 2, first=(i < 3))
            with act.Fori(0, (NS - LEAD) // 4) as j:
                for k in range(LEAD, LEAD + 4):
                    silu(4 * j + k, k % 2)
                    high_t(4 * j + k - 1, (k - 1) % 2)
            high_t(NS - 1, (NS - 1) % 2)

            act.wait_ge(s_gate_ready, 2)
            for b in SUM_SHARED:
                act.wait_ge(s_y_loaded[0][b], 16)
                for t in range(b * CT, (b + 1) * CT):
                    act.activation(yt[0][:, t, :], yt[0][:, t, :], ACT.Copy, scale=gate[:, 0, t:t + 1]).then_inc(s_first_scaled, 1)

        @block.vector
        def _(dve):
            step = [0]

            def link(ins):
                step[0] += 1
                ins.then_inc(s_step, 1)
                dve.wait_ge(s_step, step[0])

            def after(ins):
                step[0] += 1
                ins.then_inc(s_step, 1)
                return step[0]

            def rsqrt_steps(y, a, w):
                sq = nwt[:, 5, 0:w]
                yi = y.bitcast(I32)
                n = after(dve.tensor_scalar(yi, a.bitcast(I32), 1, None, ALU.logical_shift_right))
                yield
                dve.wait_ge(s_step, n)
                n = after(dve.tensor_scalar(yi, yi, -1.0, RSQRT_MAGIC, ALU.mult, ALU.add))
                for _ in range(3):
                    yield
                    dve.wait_ge(s_step, n)
                    n = after(dve.tensor_tensor(sq, y, y, ALU.mult))
                    yield
                    dve.wait_ge(s_step, n)
                    n = after(dve.scalar_tensor_tensor(out=sq, in0=sq, scalar=-0.5, in1=a, op0=ALU.mult, op1=ALU.mult))
                    yield
                    dve.wait_ge(s_step, n)
                    n = after(dve.scalar_tensor_tensor(out=y, in0=sq, scalar=1.5, in1=y, op0=ALU.add, op1=ALU.mult))
                yield
                dve.wait_ge(s_step, n)

            dve.memset(ones[:], 1.0).then_inc(s_ones_ready, 1)
            dve.memset(w_half[D - P:D - P + 2, 1, 1, 3 * D:3 * D + R], 0.0).then_inc(s_ones_ready, 1)
            dve.memset(xT[D - P:D - P + 2, :, 3, :], 1.0).then_inc(s_ones_ready, 1)
            dve.memset(oT[DC:DC + 1, :, :, :], 1.0).then_inc(s_ones_ready, 1)
            link(dve.memset(vg[:, :, 0, DH:VE], 1.0))
            link(dve.memset(vg[:, :, 1, DH:VE], 0.0))
            dve.wait_ge(s_axt_mm, 1)
            dve.tensor_copy(axt[:].rearrange("p a n -> p (a n)"), bank[0][0:KD, 0:3 * NP1]).then_inc(s_axt_ready, 1)
            dve.wait_ge(s_setup_mm, 1)
            dve.tensor_copy(mt[:], bank[1][0:NP1, 0:NP1]).then_inc(s_mt_ready, 1)

            def negmax(b):
                dve.wait_ge(s_score_mm, b + 1)
                i = b * IT
                link(dve.tensor_reduce(nmax[:, i:i + IT], bank[b % 2][:, :].rearrange("p (n m) -> p n m", n=IT), AX_X, ALU.max, negate=True))
                dve.tensor_scalar(nbias[:, i:i + IT], nmax[:, i:i + IT], KD ** -0.5, None, ALU.mult).then_inc(s_nbias_ready, 1)

            negmax(0)
            negmax(1)

            def biases():
                dve.wait_ge(s_attn_loaded, 16 * 11)
                dve.wait_ge(s_lnb_mm, 1)
                dve.wait_ge(s_mnb_mm, 1)
                dve.tensor_tensor(wp[DC:DC + 1, 1, :], bank[3][DC:DC + 1, 0:D], bp[DC:DC + 1, :], ALU.add).then_inc(s_wp_ready, 1)
                n = after(dve.tensor_tensor(bq[:, 0:512], bank[4][0:1, 0:512], bq[:, 0:512], ALU.add))
                n = after(dve.tensor_tensor(bq[:, 512:3 * D], bank[7][0:1, 0:3 * D - 512], bq[:, 512:3 * D], ALU.add))
                dve.wait_ge(s_step, n)
                for w, scale in ((slice(0, 2 * D), FS), (slice(2 * D, 3 * D), VS)):
                    n = after(dve.tensor_scalar(bq[:, w], bq[:, w], scale, None, ALU.mult))
                n = after(dve.tensor_scalar(htemp[:], temp[:], 0.1, 2.0, ALU.max, ALU.min))
                dve.wait_ge(s_step, n)
                n = after(dve.tensor_scalar(htemp[:], htemp[:], 0.5, None, ALU.mult))

            def weight_scales():
                for c in range(2):
                    for w, scale in ((slice(0, 2 * D), FS), (slice(2 * D, 3 * D), VS)):
                        dve.tensor_scalar(wq[:, c, w], wq[:, c, w], lnw[:, c:c + 1], scale, ALU.mult, ALU.mult).then_inc(s_wq_ready, 1)
                    dve.tensor_scalar(wp[0:DC, c, :], wp[0:DC, c, :], mnw[:, 0:1], None, ALU.mult).then_inc(s_wp_ready, 1)

            def moments(t, src):
                link(dve.bn_stats(stat[:, t, :], src))
                link(dve.bn_aggr(mv[:, t, :], stat[:, t, :]))

            def two_norms(t0, t1):
                n = t1 - t0
                a, r = nwt[:, 0, 0:2 * n], nwt[:, 1, 0:2 * n]
                link(dve.tensor_scalar(a[:, 0:n], mv[:, t0:t1, 1], EPS, None, ALU.add))
                link(dve.scalar_tensor_tensor(out=a[:, n:2 * n], in0=a[:, 0:n], scalar=EPS, in1=mv[:, t0:t1, 1], op0=ALU.mult, op1=ALU.add))
                for _ in rsqrt_steps(r, a, 2 * n):
                    pass
                dve.tensor_copy(r12[:, t0:t1], r[:, n:2 * n])
                dve.scalar_tensor_tensor(out=nmr[:, t0:t1], in0=mv[:, t0:t1, 0], scalar=-1.0, in1=r[:, n:2 * n], op0=ALU.mult, op1=ALU.mult)
                link(dve.tensor_tensor(a[:, 0:n], r[:, 0:n], a[:, n:2 * n], ALU.mult))
                link(dve.scalar_tensor_tensor(out=sh[:, t0:t1], in0=a[:, 0:n], scalar=0.5, in1=r[:, n:2 * n], op0=ALU.mult, op1=ALU.mult))

            for b in range(B):
                dve.wait_ge(s_prob_ready, IT * (b + 1))
                dve.reciprocal(rinv[:, b * IT:(b + 1) * IT], rsum[:, b * IT:(b + 1) * IT]).then_inc(s_rinv_ready, 1)
                dve.wait_ge(s_pT_mm, b + 1)
                if b >= 2:
                    dve.wait_ge(s_himg_mm, b - 1)
                dve.tensor_copy(probT[:, b % 2, :, :].rearrange("p a n -> p (a n)"), bank[2 + b % 2][:, :]).then_inc(s_pT_ready, 1)
                if b == 0:
                    biases()
                if b + 2 < B:
                    negmax(b + 2)
                if b == 0:
                    dve.wait_ge(s_txt_loaded, 16 * B)
                    for bb in range(B):
                        moments(bb * CT + IT, h[:, bb * CT + IT, :])
                if b == 1:
                    weight_scales()
                if b >= 1:
                    for n in range(IT):
                        dve.wait_ge(s_himg_ready, (b - 1) * IT + n + 1)
                        moments((b - 1) * CT + n, h[:, (b - 1) * CT + n, :])
            two_norms(0, T - CT)

            def normalize(t):
                if t >= 2:
                    dve.wait_ge(s_xlow_ready, 2 * (t - 1))
                dve.tensor_scalar(xn[:, t % 2, :], h[:, t, :], r12[:, t:t + 1], nmr[:, t:t + 1], ALU.mult, ALU.add).then_inc(s_xn_ready, 1)

            def x_t(t):
                dve.wait_ge(s_xT_mm, t + 1)
                if t >= 2:
                    dve.wait_ge(s_vb_mm, t - 1)
                ps = bank[t % 2][:, 0:3 * P // 2].bitcast(F16)
                dve.tensor_copy(xT[0:D - P, t % 2, 3, :], ps[0:D - P, 2 * P:3 * P])
                dve.tensor_copy(xT[:, t % 2, 0:3, :].rearrange("p c n -> p (c n)"), ps).then_inc(s_xT_ready, 1)

            normalize(0)
            normalize(1)
            x_t(0)
            for n in range(IT):
                dve.wait_ge(s_himg_ready, (B - 1) * IT + n + 1)
                moments((B - 1) * CT + n, h[:, (B - 1) * CT + n, :])
            two_norms(T - CT, T)

            def queries_low(t):
                dve.wait_ge(s_fhigh_ready, 2 * t + 1)
                dve.tensor_tensor(half_of(t, 0, 1), twice(t, 0), half_of(t, 0, 0), ALU.subtract).then_inc(s_qlow_ready, 1)

            for t in range(T):
                if t + 1 < T:
                    x_t(t + 1)
                if t + 2 < T:
                    normalize(t + 2)
                dve.wait_ge(s_exp_ready, t + 1)
                link(dve.tensor_scalar(eb[:, t % 2, :], eb[:, t % 2, :], FS, None, ALU.min))
                dve.scalar_tensor_tensor(out=eb[:, t % 2, :], in0=bank[2 + t % 2][:, 0:2 * D], scalar=0.0,
                                         in1=eb[:, t % 2, :], op0=ALU.max, op1=ALU.add).then_inc(s_f32_ready, 1)
                dve.wait_ge(s_tanh_ready, t + 1)
                dve.wait_ge(s_v_ready, t + 1)
                if t >= 2:
                    dve.wait_ge(s_gT_mm, t - 1)
                dve.scalar_tensor_tensor(out=g1[:, t % 2, :], in0=th[:, t % 2, :], scalar=1.0, in1=bank[4 + t % 2][:, D:D + R],
                                         op0=ALU.add, op1=ALU.mult).then_inc(s_g1_ready, 1)
                if t:
                    queries_low(t - 1)
            queries_low(T - 1)
            dve.wait_ge(s_ga_ready, 2)
            dve.tensor_tensor(gc[:], gb[:, :, 0:H], gb[:, :, H:2 * H], ALU.subtract).then_inc(s_dph_ready, 1)
            link(dve.tensor_scalar(ga[:], ga[:], 1.0, None, ALU.add))
            link(dve.tensor_tensor(ga[:, :, 0:H], ga[:, :, 0:H], ga[:, :, H:2 * H], ALU.mult))
            dve.wait_ge(s_sin_ready, 1)
            link(dve.tensor_tensor(gc[:], gd[:], gd[:], ALU.mult))
            link(dve.tensor_scalar(gc[:], gc[:], -2.0, 1.0, ALU.mult, ALU.add))
            link(dve.tensor_tensor(gc[:], gc[:], gc[:], ALU.mult))
            link(dve.tensor_scalar(gc[:], gc[:], 2.0, -1.0, ALU.mult, ALU.add))
            dve.tensor_tensor(gc[:], gc[:], ga[:, :, 0:H], ALU.mult).then_inc(s_cos_ready, 1)
            dve.wait_ge(s_gate_tanh, 2)
            link(dve.tensor_scalar(gate1[:], gate1[:], 0.5, 1.5, ALU.mult, ALU.add))

            def gated_values(b):
                w = slice(b * CT * H, (b + 1) * CT * H)
                g_ = gate1[:].rearrange("p t h -> p (t h)")[:, w]
                dve.tensor_tensor(v32[:, w, :], v32[:, w, :], g_.unsqueeze(2).broadcast_to([P, CT * H, DH]), ALU.mult).then_inc(s_gated, 1)

            def values_low(b):
                w = slice(b * CT * H, (b + 1) * CT * H)
                dve.wait_ge(s_vhigh_ready, b + 1)
                dve.tensor_tensor(vg[:, w, 1, 0:DH], v32[:, w, :], vg[:, w, 0, 0:DH], ALU.subtract).then_inc(s_vg_ready, 1)

            def second_norm(b):
                t0 = b * CT
                va, r, nm = nwt[:, 2, 0:CT], nwt[:, 3, 0:CT], nwt[:, 4, 0:CT]
                n = after(dve.tensor_scalar(va, mv[:, t0:t0 + CT, 1], EPS, None, ALU.add))
                yield
                dve.wait_ge(s_step, n)
                yield from rsqrt_steps(r, va, CT)
                link(dve.scalar_tensor_tensor(out=nm, in0=mv[:, t0:t0 + CT, 0], scalar=-1.0, in1=r, op0=ALU.mult, op1=ALU.mult))
                if b >= 2:
                    dve.wait_ge(s_t1_full, use["x", b - 2] + 1)
                    dve.wait_ge(s_xlo_ready, 2 * (t0 - CT))
                for cc in range(CT):
                    dve.tensor_scalar(x2[:, b % 2, cc, :], h[:, t0 + cc, :], r[:, cc:cc + 1], nm[:, cc:cc + 1],
                                      ALU.mult, ALU.add).then_inc(s_x2_ready, 1)

            def rows_low(b):
                for cc in range(CT):
                    dve.wait_ge(s_xhi_ready, 2 * (b * CT + cc + 1))
                    xrow, xf = xr[:, b % 2 * CT + cc, :], x2[:, b % 2, cc, :]
                    dve.tensor_tensor(xrow[:, P:2 * P], xf[:, 0:P], xrow[:, 0:P], ALU.subtract).then_inc(s_xlo_ready, 1)
                    dve.tensor_tensor(xrow[:, P + D:2 * D], xf[:, P:D], xrow[:, 2 * P:P + D], ALU.subtract).then_inc(s_xlo_ready, 1)

            def head_norm(b):
                ob = o[:, b % 2, :, :]
                va, r = nwt[:, 0, :], nwt[:, 1, :]
                dve.wait_ge(s_o_ready, (b + 1) * CT)
                n = after(dve.tensor_reduce(osum[:], ob, AX_X, ALU.add))
                yield
                dve.wait_ge(s_step, n)
                n = after(dve.tensor_scalar(osum[:], osum[:], 1.0 / DH, None, ALU.mult))
                yield
                dve.wait_ge(s_step, n)
                n = after(dve.tensor_tensor(ob, ob, osum[:].unsqueeze(2).broadcast_to([P, CT * H, DH]), ALU.subtract))
                yield
                dve.wait_ge(s_step, n)
                n = after(dve.tensor_tensor(osq, ob, ob, ALU.mult))
                yield
                dve.wait_ge(s_step, n)
                n = after(dve.tensor_reduce(va, osq, AX_X, ALU.add))
                yield
                dve.wait_ge(s_step, n)
                n = after(dve.tensor_scalar(va, va, 1.0 / DH, EPS, ALU.mult, ALU.add))
                yield
                dve.wait_ge(s_step, n)
                yield from rsqrt_steps(r, va, CT * H)
                dve.tensor_tensor(ob, ob, r.unsqueeze(2).broadcast_to([P, CT * H, DH]), ALU.mult).then_inc(s_ohat_ready, 1)

            def go_on(chain):
                next(chain, None)

            def finish(chain):
                for _ in chain:
                    pass

            gated_values(0)
            for t in range(T + 1):
                chain = iter(())
                b, c = divmod(t, CT)
                if c == 0 and b:
                    chain = head_norm(b - 1)
                    go_on(chain)
                if t < T:
                    dve.wait_ge(s_at_mm, t + 1)
                    if t:
                        dve.wait_ge(s_atlow_ready, 4 * t)
                    for n in range(4):
                        i, g0 = n // 2, n % 2 * GB
                        dve.tensor_tensor(atm[:, i, g0:g0 + GB, :], bank[2 + n][:, 0:GB * P].rearrange("p (g l) -> p g l", g=GB),
                                          causal[:].unsqueeze(1).broadcast_to([P, GB, P]), ALU.mult).then_inc(s_mask_done, 1)
                        go_on(chain)
                    if t == 0:
                        values_low(0)
                    if c < 2:
                        n = 2 * b + c
                        dve.wait_ge(s_state_mm, n + 1)
                        if n:
                            dve.wait_ge(s_state_ready, n)
                        dve.tensor_tensor(state[:], bank[7][:, 0:H * VE],
                                          headmask[:].rearrange("p g h e -> p (g h e)"), ALU.mult).then_inc(s_state32, 1)
                        go_on(chain)
                if 0 <= t - 5 < T:
                    tt = t - 5
                    u = use["o", tt]
                    dve.wait_ge(s_t1_full, u + 1)
                    dve.tensor_tensor(h[:, tt, :], bank[1][:, 0:D], h[:, tt, :], ALU.add).then_inc(s_t1_free, 1)
                    go_on(chain)
                    dve.wait_ge(s_t1_free, u + 1)
                    n = after(dve.bn_stats(stat[:, tt, :], h[:, tt, :]))
                    go_on(chain)
                    dve.wait_ge(s_step, n)
                    n = after(dve.bn_aggr(mv[:, tt, :], stat[:, tt, :]))
                    go_on(chain)
                    dve.wait_ge(s_step, n)
                    if tt % CT == CT - 1:
                        chain = second_norm(tt // CT)
                        go_on(chain)
                if t < T:
                    if c == 1 and b + 1 < B:
                        gated_values(b + 1)
                    if c == 2 and b + 1 < B:
                        values_low(b + 1)
                    for n in range(4):
                        i, g0 = n // 2, n % 2 * GB
                        dve.wait_ge(s_athigh_ready, 4 * t + n + 1)
                        dve.tensor_tensor(at_half[:, 1, i, g0:g0 + GB, :], atm[:, i, g0:g0 + GB, :], at_half[:, 0, i, g0:g0 + GB, :],
                                          ALU.subtract).then_inc(s_atlow_ready, 1)
                        go_on(chain)
                    if c < 2:
                        dve.wait_ge(s_sthigh_ready, 2 * b + c + 1)
                        dve.tensor_tensor(st_half[:, t % 2, 1, :], state[:], st_half[:, t % 2, 0, :], ALU.subtract).then_inc(s_state_ready, 1)
                finish(chain)
                if t % CT == 2 and 0 <= t - 8:
                    rows_low((t - 8) // CT)
                if t < T:
                    dve.wait_ge(s_num_mm, t + 1)
                    num = bank[6][:, 0:H * VE].rearrange("p (h e) -> p h e", e=VE)
                    link(dve.tensor_scalar(rden[:, 0, :], num[:, :, DH], 1e-6, None, ALU.add))
                    link(dve.reciprocal(rden[:, 1, :], rden[:, 0, :]))
                    dve.tensor_tensor(o[:, b % 2, c * H:(c + 1) * H, :], num[:, :, 0:DH], rden[:, 1, :].unsqueeze(2).broadcast_to([P, H, DH]),
                                      ALU.mult).then_inc(s_o_ready, 1)


            def bt(v, n=E):
                return v.unsqueeze(2).broadcast_to([P, T, n])

            def be(v):
                return v.unsqueeze(1).broadcast_to([P, T, E])

            dve.wait_ge(s_iota_ready, 5)
            link(dve.memset(keep, 1.0))
            link(dve.memset(keep[:, :, 0:1], 0.0))
            for k in range(WIN // 2):
                ins = dve.memset(pow8[:].rearrange("p (a k) -> p a k", a=2)[:, :, k], float(8 ** k))
            link(ins)
            t0 = PT - 1
            dve.wait_ge(s_t1_full, use["o", t0] + 1)
            dve.tensor_tensor(h[:, t0, :], bank[1][:, 0:D], h[:, t0, :], ALU.add).then_inc(s_t1_free, 1)
            dve.wait_ge(s_t1_free, len(misc))
            moments(t0, h[:, t0, :])
            finish(second_norm(B - 2))
            for i, n in ((0, 2), (1, 1)):
                ts = slice(PT + 2 * i, PT + 2 * i + n)
                hs = h[:, ts, :].rearrange("p t d -> p (t d)")
                dve.wait_ge(s_last_proj, i + 1)
                link(dve.tensor_tensor(hs, bank[4 + i][:, 0:n * D], hs, ALU.add))
            for t in range(PT, T):
                ins = dve.bn_stats(stat[:, t, :], h[:, t, :])
            link(ins)
            for t in range(PT, T):
                ins = dve.bn_aggr(mv[:, t, :], stat[:, t, :])
            link(ins)
            finish(second_norm(B - 1))
            rows_low(B - 2)
            dve.wait_ge(s_last_logits, 2)
            mx, e1, e2, b1, b2, rs, z = (small[:, n, :] for n in range(7))
            link(dve.tensor_reduce(mx, lg[:], AX_X, ALU.max))
            dve.tensor_tensor(ls, lg[:], bt(mx), ALU.subtract).then_inc(s_ls_ready, 1)
            dve.wait_ge(s_ls_ready, 1)

            def first_of(eq, dst):
                link(dve.tensor_tensor(eq, eq, be(iota_e[:]), ALU.mult))
                link(dve.tensor_reduce(mx, eq, AX_X, ALU.min))
                link(dve.tensor_tensor(dst, be(iota_e[:]), bt(mx), ALU.is_equal))

            link(dve.tensor_scalar(tmp, ls, 0.0, None, ALU.is_equal))
            first_of(tmp, sel[:, 0, :, :])
            link(dve.scalar_tensor_tensor(out=pb, in0=sel[:, 0, :, :], scalar=-1e30, in1=ls, op0=ALU.mult, op1=ALU.add))
            link(dve.tensor_reduce(mx, pb, AX_X, ALU.max))
            link(dve.tensor_tensor(tmp, pb, bt(mx), ALU.is_equal))
            first_of(tmp, sel[:, 1, :, :])
            dve.tensor_tensor(selsum, sel[:, 0, :, :], sel[:, 1, :, :], ALU.add).then_inc(s_sel_ready, 1)
            rows_low(B - 1)
            dve.wait_ge(s_rank_mm, 1)
            link(dve.tensor_copy(tot, bank[0][:, T * E:2 * T * E].rearrange("p (t e) -> p e t", e=E)))
            flat = lambda v: v.rearrange("p e t -> p (e t)")
            link(dve.tensor_tensor_scan(flat(inc), flat(keep), flat(tot), 0.0, ALU.mult, ALU.add))
            n_tiles = after(dve.tensor_scalar(cnti[:], inc[:, :, T - 1], float(P - 1), None, ALU.add))
            n_before = after(dve.tensor_tensor(tot, inc, tot, ALU.subtract))
            dve.wait_ge(s_step, n_tiles)
            n_tiles = after(dve.tensor_scalar(cnti[:], cnti[:], 7, None, ALU.logical_shift_right))
            dve.wait_ge(s_step, n_before)
            n_before = after(dve.tensor_tensor(tmp, bank[0][:, 0:T * E].rearrange("p (t e) -> p t e", e=E), tot.rearrange("p e t -> p t e"), ALU.add))
            dve.wait_ge(s_step, n_tiles)
            link(dve.tensor_copy(cnt[:, 0, :], cnti[:]))
            link(dve.tensor_tensor_scan(cnt[:, 1, :], ones[:, 0:E], cnt[:, 0, :], 0.0, ALU.mult, ALU.add))
            link(dve.tensor_tensor(cnt[:, 2, :], cnt[:, 1, :], cnt[:, 0, :], ALU.subtract))
            link(dve.scalar_tensor_tensor(out=tmp, in0=be(cnt[:, 2, :]), scalar=float(P), in1=tmp, op0=ALU.mult, op1=ALU.add))
            both = [P, 2, T, E]
            link(dve.tensor_tensor(sel2, sel[:], tmp.unsqueeze(1).broadcast_to(both), ALU.mult))
            link(dve.tensor_reduce(slot[:], sel2, AX_X, ALU.add))
            link(dve.tensor_copy(sloti[:, 0, :], slot[:].rearrange("p k t -> p (k t)")))
            dve.tensor_scalar(sloti[:, 1, :], sloti[:, 0, :], 7, None, ALU.logical_shift_right)
            link(dve.tensor_scalar(sloti[:, 2, :], sloti[:, 0, :], P - 1, None, ALU.bitwise_and))
            dve.tensor_copy(slotf[:], sloti[:, 1:3, :]).then_inc(s_slot_ready, 1)
            dve.wait_ge(s_slot_ready, 1)
            dve.tensor_tensor(cola, iota_p16[:].unsqueeze(1).broadcast_to([P, 2 * T, P]),
                              slotf[:, 1, :].unsqueeze(2).broadcast_to([P, 2 * T, P]), ALU.is_equal).then_inc(s_onehot_ready, 1)
            link(dve.tensor_tensor(cole, iota_p[:, 0:NSP].unsqueeze(1).broadcast_to([P, 2 * T, NSP]),
                                   slotf[:, 0, :].unsqueeze(2).broadcast_to([P, 2 * T, NSP]), ALU.is_equal))
            dve.tensor_scalar(colb[:, :, 0, :], cole, row1[:, 0:1], None, ALU.mult)
            dve.tensor_tensor(colb[:, :, 1, :], cole, choice1[:].unsqueeze(2).broadcast_to([P, 2 * T, NSP]), ALU.mult).then_inc(s_onehot_ready, 1)
            link(dve.tensor_tensor(passed, cnt[0:1, 1, :].unsqueeze(1).broadcast_to([1, NSP, E]),
                                   iota_p[0:1, 0:NSP].unsqueeze(2).broadcast_to([1, NSP, E]), ALU.is_le))
            link(dve.tensor_reduce(expf[:], passed, AX_X, ALU.add))
            dve.wait_ge(s_src_mm, 1)
            link(dve.tensor_copy(src[:, 0:2, :].rearrange("p v j -> p (v j)"), bank[2][:, 0:2 * NSP]))
            link(dve.scalar_tensor_tensor(out=src[:, 2, :], in0=src[:, 1, :], scalar=float(P), in1=src[:, 0, :], op0=ALU.mult, op1=ALU.add))
            link(dve.tensor_scalar(src[:, 3, :], src[:, 0, :], 0.0, NO_TOKEN, ALU.is_equal, ALU.mult))
            link(dve.tensor_tensor(src[:, 2, :], src[:, 2, :], src[:, 3, :], ALU.add))
            dve.tensor_scalar(dst_row[:], src[:, 2, :], -float(P + 1), None, ALU.add).then_inc(s_rows_ready, 1)
            link(dve.tensor_scalar(src[:, 3, :], src[:, 2, :], float(NTOK + P + 1), -float(NTOK), ALU.is_ge, ALU.mult))
            link(dve.tensor_tensor(src[:, 3, :], src[:, 3, :], src[:, 2, :], ALU.add))
            dve.tensor_scalar(tok_row[:], src[:, 3, :], -float(P + 1), None, ALU.add).then_inc(s_rows_ready, 1)
            link(dve.tensor_scalar(expf[:], expf[:], float(E - 1), None, ALU.min))
            for n, i in enumerate(WINDOWS):
                ins = dve.tensor_tensor(packf[:, n, :], expf[:, i:i + WIN], pow8[:], ALU.mult)
            link(ins)
            link(dve.tensor_reduce(packs[:], packf[:].rearrange("p n (a k) -> p n a k", a=2), AX_X, ALU.add))
            link(dve.tensor_copy(packi[:], packs[:]))
            link(dve.tensor_scalar(packi[:, :, 1], packi[:, :, 1], 3 * WIN // 2, None, ALU.logical_shift_left))
            dve.tensor_tensor(expert[:], packi[:, :, 0], packi[:, :, 1], ALU.bitwise_or).then_inc(s_expert_ready, 1)
            dve.wait_ge(s_ex_ready, 1)
            link(dve.tensor_reduce(z, ex, AX_X, ALU.add))
            link(dve.reciprocal(rs, z))
            dve.tensor_tensor(pb, ex, bt(rs), ALU.mult).then_inc(s_pb_ready, 1)

            def rows_t(i, k, first=False):
                dve.wait_ge(s_xe_mm, i + 1)
                if not first:
                    dve.wait_ge(s_up_mm, i - 1)
                dve.tensor_copy(xe[:, k, :], bank[k][:, 0:3 * P // 2].bitcast(F16)).then_inc(s_xe_ready, 1)

            def low(i, k, first=False):
                dve.wait_ge(s_high_ready, i + 1)
                if not first:
                    dve.wait_ge(s_actT_mm, i - 1)
                dve.tensor_tensor(actl[:, k, :], act32[:, k, :], acth[:, k, :], ALU.subtract).then_inc(s_low_ready, 1)

            def low_t(i, k, first=False):
                dve.wait_ge(s_actT_mm, i + 1)
                if not first:
                    dve.wait_ge(s_down_mm, i - 1)
                dve.tensor_copy(actT[:, k, 1, :], bank[7][:, 0:FI // 2].bitcast(F16)).then_inc(s_actT_low, 1)

            def result(i, k, rnd=None):
                dve.wait_ge(s_down_mm, i + 1)
                if rnd is not None:
                    dve.wait_ge(s_scattered[k], 16 * rnd)
                dve.tensor_scalar(ye[:, k, :], bank[4 + k % 2][:, 0:D], 1.0 / WS, None, ALU.mult).then_inc(s_y_ready, 1)

            rows_t(0, 0, first=True)
            rows_t(1, 1, first=True)
            dve.wait_ge(s_imp_mm, 1)
            dve.tensor_reduce(imp[:], bank[5][:, 0:T * E].rearrange("p (t e) -> p e t", e=E), AX_X, ALU.add).then_inc(s_imp_ready, 1)
            low(0, 0, first=True)
            rows_t(2, 0)
            low_t(0, 0, first=True)
            low(1, 1, first=True)
            for i in range(2, LEAD):
                rows_t(i + 1, (i + 1) % 2)
                low_t(i - 1, (i - 1) % 2, first=(i < 3))
                low(i, i % 2)
                result(i - 2, (i - 2) % 4, rnd=(i - 2) // 4 or None)
            with dve.Fori(0, (NS - LEAD) // 4) as j:
                for k in range(LEAD, LEAD + 4):
                    i = 4 * j + k
                    rows_t(i + 1, (k + 1) % 2)
                    low_t(i - 1, (k - 1) % 2)
                    low(i, k % 2)
                    result(i - 2, (k - 2) % 4, rnd=j + (k - 2) // 4)
            low_t(NS - 1, (NS - 1) % 2)
            for i in range(NS - 2, NS):
                result(i, i % 4, rnd=i // 4)

            dve.wait_ge(s_imp_ready, 1)
            link(dve.tensor_scalar(imp[:], imp[:], 0.1, 0.91, ALU.mult, ALU.add))
            for k, ek, bk in ((0, e1, b1), (1, e2, b2)):
                link(dve.tensor_tensor(ls, sel[:, k, :, :], ex, ALU.mult))
                link(dve.tensor_reduce(ek, ls, AX_X, ALU.add))
                link(dve.tensor_tensor(ls, sel[:, k, :, :], be(imp[:]), ALU.mult))
                link(dve.tensor_reduce(bk, ls, AX_X, ALU.add))
            link(dve.tensor_tensor(e1, e1, b2, ALU.mult))
            link(dve.tensor_tensor(e2, e2, b1, ALU.mult))
            link(dve.tensor_tensor(z, e1, e2, ALU.add))
            link(dve.reciprocal(rs, z))
            dve.tensor_tensor(gate[:, 0, :], e1, rs, ALU.mult).then_inc(s_gate_ready, 1)
            dve.tensor_tensor(gate[:, 1, :], e2, rs, ALU.mult).then_inc(s_gate_ready, 1)
            dve.wait_ge(s_gate_ready, 2)
            for b in SUM_ORDER:
                ts = range(b * CT, (b + 1) * CT)
                if b in SUM_SHARED:
                    dve.wait_ge(s_first_added, SUM_SHARED.index(b) + 1)
                else:
                    dve.wait_ge(s_y_loaded[0][b], 16)
                    for t in ts:
                        n = after(dve.scalar_tensor_tensor(out=h[:, t, :], in0=yt[0][:, t, :], scalar=gate[:, 0, t:t + 1], in1=h[:, t, :],
                                                           op0=ALU.mult, op1=ALU.add))
                    dve.wait_ge(s_step, n)
                dve.wait_ge(s_y_loaded[1][b], 16)
                for t in ts:
                    dve.scalar_tensor_tensor(out=h[:, t, :], in0=yt[1][:, t, :], scalar=gate[:, 1, t:t + 1], in1=h[:, t, :],
                                             op0=ALU.mult, op1=ALU.add).then_inc(s_sum_ready, 1)


def kernel(**inputs):
    import numpy as np
    import concourse.bacc as _bacc
    from concourse.bass_utils import run_bass_kernel_spmd as _run

    a = {k: np.asarray(v) for k, v in inputs.items()}
    f32 = np.float32
    two = lambda w: np.ascontiguousarray(w.reshape(2, DC, -1).transpose(1, 0, 2))
    rest_twice = lambda w: np.stack([w[0:P], np.concatenate([w[P:D], w[P:D]], 0)], 1)
    unit = np.zeros((1, NP1), f32)
    unit[0, NP1 - 1] = 1.0
    x = a["x"].reshape(B, 3, 16, 4, 16, 4).transpose(1, 3, 5, 0, 2, 4).reshape(48, B * NI)
    wb2 = a["L0_attn_Wb2"].reshape(R, H, 5)
    lay = {
        "xp1": np.concatenate([x, np.ones((1, B * NI), f32)], 0),
        "cwb": two(np.concatenate([a["L0_tok_conv_w"].reshape(D, 48), a["L0_tok_conv_b"][:, None]], 1)),
        "wtok": two(np.concatenate([a["L0_tok_q_w"], a["L0_tok_k_w"], a["L0_tok_v_w"]], 0).T),
        "btok": np.concatenate([a["L0_tok_q_b"], a["L0_tok_k_b"], a["L0_tok_v_b"]])[None],
        "unit": unit,
        "pjt": a["L0_tok_proj_w"].T,
        "pjb": a["L0_tok_proj_b"][None],
        "txt": a["txt"],
        "wq": rest_twice(np.concatenate([a["L0_attn_Wqkv"], a["L0_attn_Wb1"]], 1)),
        "lnw": rest_twice(a["L0_attn_ln_w"][:, None])[:, :, 0],
        "lnb": rest_twice(a["L0_attn_ln_b"][:, None])[:, :, 0],
        "bqkv": a["L0_attn_bqkv"][None],
        "wb2": np.concatenate([wb2[:, :, i] for i in (0, 2, 1, 3)], 1),
        "wp": two(a["L0_attn_Wproj"]),
        "mnw": np.tile(a["L0_attn_mn_w"], DC // DH)[:, None],
        "mnb": np.tile(a["L0_attn_mn_b"], DC // DH)[:, None],
        "bproj": a["L0_attn_bproj"][None],
        "temp": np.broadcast_to(a["L0_attn_temperature"][None], (P, 1)),
        "wr": two(a["L0_ffn_router_w"].T),
        "w1a": a["L0_ffn_w1"].transpose(2, 0, 1).reshape(D, E * FI)[0:P],
        "w1b": a["L0_ffn_w1"].transpose(2, 0, 1).reshape(D, E * FI)[P:D],
        "w2": a["L0_ffn_w2"].transpose(2, 0, 1).reshape(MC, P, E, D).transpose(1, 2, 0, 3).reshape(P, E * MC * D),
    }
    nc = _bacc.Bacc("TRN2", target_bir_lowering=False, num_devices=1)
    arrays = {f"in_{k}": np.ascontiguousarray(v) for k, v in lay.items()}
    aps = {k: nc.dram_tensor(f"in_{k}", arrays[f"in_{k}"].shape, F32, kind="ExternalInput").ap() for k in lay}
    x2_dram = nc.dram_tensor("x2_rows", (NTOK, 2 * D), F16, kind="Internal").ap()
    y_dram = nc.dram_tensor("y_rows", (2 * NTOK, D), F32, kind="Internal").ap()
    out = nc.dram_tensor("out_0", (B, CT * P, D), F32, kind="ExternalOutput").ap()
    build(nc, aps, x2_dram, y_dram, out)
    r = _run(nc, [arrays], core_ids=[0])
    return r.results[0]["out_0"]
```
